# Optimizing a Trainium2 kernel written in Bass

```python
import numpy as np
import jax
import jax.numpy as jnp

def _softmax(x, axis=-1):
    return jax.nn.softmax(x, axis=axis)

def _gelu(x):
    return jax.nn.gelu(x, approximate=True)

def _silu(x):
    return jax.nn.silu(x)

def _sigmoid(x):
    return jax.nn.sigmoid(x)

def _layernorm(x, axis=-1, eps=1e-05):
    m = jnp.mean(x, axis=axis, keepdims=True)
    v = jnp.var(x, axis=axis, keepdims=True)
    return (x - m) / jnp.sqrt(v + eps)

def _scatter_add(tgt, idx, src, axis=0):
    return tgt.at[idx].add(src)

def _segment_sum(src, seg, n):
    return jax.ops.segment_sum(src, seg, n)
kernel_name = 'mk_decoder_preln_d1_seqx_r4_f3b047'

def setup_inputs(seed: int=0):
    np.random.seed(seed)
    _w = jnp.asarray

    def _rec_inputs():
        import jax
        import jax.numpy as jnp
        _rk = jax.random.key(seed)
        x = -4.161e-06 + 1 * jax.random.normal(jax.random.fold_in(_rk, 1), (2, 512, 512), jnp.float32)
        _lenS = 512 - jax.random.randint(jax.random.fold_in(_rk, 7), (2,), 0, max(1, 512 // 4) + 1, jnp.int32)
        _lenS2 = 1024 - jax.random.randint(jax.random.fold_in(_rk, 8), (2,), 0, max(1, 1024 // 4) + 1, jnp.int32)
        _ctx_2048P = jax.random.normal(jax.random.fold_in(_rk, 11), (2, 16, 512), jnp.float32)
        _ctx_2048c = jax.random.dirichlet(jax.random.fold_in(_rk, 511), 0.3 * jnp.ones((16,), jnp.float32), (2, 1024))
        _ctx_2048t = jnp.einsum('bsk,bkd->bsd', _ctx_2048c, _ctx_2048P)
        _ctx_2048t = _ctx_2048t * jax.lax.rsqrt(jnp.mean(jnp.square(_ctx_2048t)) + 1e-12) * 0.953939
        ctx_2048 = -0.000192764 + 0.999654 * (_ctx_2048t + 0.3 * jax.random.normal(jax.random.fold_in(_rk, 611), (2, 1024, 512), jnp.float32))
        return (x, ctx_2048)
    x, ctx_2048 = _rec_inputs()

    def _L0_attn_setup():
        import jax, jax.numpy as jnp
        import numpy as np
        import math
        D_MODEL = 512
        NUM_HEADS = 16
        HEAD_DIM = D_MODEL // NUM_HEADS
        key = jax.random.key(seed)
        k_x, k_wqkv, k_bqkv, k_wo, k_bo = jax.random.split(key, 5)
        B, S = (2, 512)
        scale = 1.0 / math.sqrt(D_MODEL)
        return {'x': jax.random.normal(k_x, (B, S, D_MODEL), dtype=jnp.float32), 'w_qkv': jax.random.normal(k_wqkv, (3 * D_MODEL, D_MODEL), dtype=jnp.float32) * scale, 'b_qkv': jax.random.normal(k_bqkv, (3 * D_MODEL,), dtype=jnp.float32) * 0.01, 'w_out': jax.random.normal(k_wo, (D_MODEL, D_MODEL), dtype=jnp.float32) * scale, 'b_out': jax.random.normal(k_bo, (D_MODEL,), dtype=jnp.float32) * 0.01}
    _L0_attn_all = _L0_attn_setup()
    _L0_attn_in = {k: v for k, v in _L0_attn_all.items() if k in ('w_qkv', 'b_qkv', 'w_out', 'b_out')}
    del _L0_attn_all

    def _L0_xattn_setup():
        import jax, jax.numpy as jnp
        import numpy as np
        FP8_MAX = 448.0
        EPS = 1e-05

        def _fp8_roundtrip(x):
            return x.astype(jnp.float8_e4m3fn).astype(jnp.float32)

        def _div_clamp_fp8(x, scale):
            y = jnp.clip(x.astype(jnp.float32) / scale, -FP8_MAX, FP8_MAX)
            y = y.astype(jnp.bfloat16).astype(jnp.float32)
            return _fp8_roundtrip(y)

        def _ln(x, w, b):
            mu = jnp.mean(x, axis=-1, keepdims=True)
            var = jnp.mean(jnp.square(x - mu), axis=-1, keepdims=True)
            return (x - mu) * jax.lax.rsqrt(var + EPS) * w + b

        def _fp8_linear_pertensor(x, wq, w_scale, in_scale):
            xq = _div_clamp_fp8(x, in_scale)
            return jnp.einsum('bsi,oi->bso', xq * in_scale, wq) * w_scale

        def _gqa(q, k, v):
            scale = 1.0 / np.sqrt(q.shape[-1])
            scores = jnp.einsum('bsghd,btgd->bghst', q, k) * scale
            p = jax.nn.softmax(scores, axis=-1)
            return jnp.einsum('bghst,btgd->bsghd', p, v)
        key = jax.random.key(seed)
        ks = jax.random.split(key, 8)
        B, S, SC, H, NH, G, D = (2, 512, 128, 512, 16, 8, 128)

        def qw(k, out_f, in_f):
            w = jax.random.normal(k, (out_f, in_f), jnp.float32) * 0.02
            sc = jnp.max(jnp.abs(w)) / FP8_MAX
            return (_fp8_roundtrip(w / sc), sc.astype(jnp.float32))
        wq, wq_s = qw(ks[0], NH * D, H)
        wqx, wqx_s = qw(ks[1], NH * D, H)
        wk, wk_s = qw(ks[2], G * D, H)
        wv, wv_s = qw(ks[3], G * D, H)
        wproj, wp_s = qw(ks[4], H, 2 * NH * D)
        return {'hidden_states': jax.random.normal(ks[5], (B, S, H), jnp.float32), 'cond': jax.random.normal(ks[6], (B, SC, H), jnp.float32), 'ln_w': jnp.ones((H,), jnp.float32), 'ln_b': jnp.zeros((H,), jnp.float32), 'wq': wq, 'wq_scale': wq_s, 'q_in_scale': jnp.full((H,), 0.05, jnp.float32), 'wqx': wqx, 'wqx_scale': wqx_s, 'qx_in_scale': jnp.full((H,), 0.05, jnp.float32), 'wk': wk, 'wk_scale': wk_s, 'k_in_scale': jnp.full((H,), 0.05, jnp.float32), 'wv': wv, 'wv_scale': wv_s, 'v_in_scale': jnp.full((H,), 0.05, jnp.float32), 'w_kv_x': jax.random.normal(ks[7], (2 * G * D, H), jnp.float32) * 0.02, 'qln_w': jnp.ones((D,), jnp.float32), 'qln_b': jnp.zeros((D,), jnp.float32), 'kln_w': jnp.ones((D,), jnp.float32), 'kln_b': jnp.zeros((D,), jnp.float32), 'qxln_w': jnp.ones((D,), jnp.float32), 'qxln_b': jnp.zeros((D,), jnp.float32), 'kxln_w': jnp.ones((D,), jnp.float32), 'kxln_b': jnp.zeros((D,), jnp.float32), 'wproj': wproj, 'proj_w_scale': wp_s, 'proj_in_scale': jnp.asarray(0.05, jnp.float32), 'proj_smooth': jnp.full((2 * NH * D,), 0.05, jnp.float32)}
    _L0_xattn_all = _L0_xattn_setup()
    _L0_xattn_in = {k: v for k, v in _L0_xattn_all.items() if k in ('ln_w', 'ln_b', 'wq', 'wq_scale', 'q_in_scale', 'wqx', 'wqx_scale', 'qx_in_scale', 'wk', 'wk_scale', 'k_in_scale', 'wv', 'wv_scale', 'v_in_scale', 'w_kv_x', 'qln_w', 'qln_b', 'kln_w', 'kln_b', 'qxln_w', 'qxln_b', 'kxln_w', 'kxln_b', 'wproj', 'proj_w_scale', 'proj_in_scale', 'proj_smooth')}
    del _L0_xattn_all

    def _L0_ffn_setup():
        import jax, jax.numpy as jnp
        import numpy as np
        TOP_P = 0.9
        S, B, H, I, E = (512, 4, 512, 1024, 8)

        def _top_p_weights(probs, top_p):
            order = jnp.argsort(-probs, axis=-1)
            sp = jnp.take_along_axis(probs, order, axis=-1)
            cum = jnp.cumsum(sp, axis=-1)
            exceed = cum > top_p
            first_idx = jnp.argmax(exceed, axis=-1)
            first = jnp.arange(probs.shape[-1])[None, :] == first_idx[:, None]
            keep = ~exceed | first
            kept = jnp.where(keep, sp, 0.0)
            t_idx = jnp.arange(probs.shape[0])[:, None]
            return jnp.zeros_like(probs).at[t_idx, order].set(kept)
        key = jax.random.key(seed)
        ks = jax.random.split(key, 5)
        scale = 0.02
        return {'hidden_states': jax.random.normal(ks[0], (S, B, H), dtype=jnp.float32), 'router_w': jax.random.normal(ks[1], (E, H), dtype=jnp.float32) * scale, 'gate_w': jax.random.normal(ks[2], (E, I, H), dtype=jnp.float32) * scale, 'up_w': jax.random.normal(ks[3], (E, I, H), dtype=jnp.float32) * scale, 'down_w': jax.random.normal(ks[4], (E, H, I), dtype=jnp.float32) * scale}
    _L0_ffn_all = _L0_ffn_setup()
    _L0_ffn_in = {k: v for k, v in _L0_ffn_all.items() if k in ('router_w', 'gate_w', 'up_w', 'down_w')}
    del _L0_ffn_all
    return {'x': x, 'ctx_2048': ctx_2048, 'L0_attn_w_qkv': _L0_attn_in['w_qkv'], 'L0_attn_b_qkv': _L0_attn_in['b_qkv'], 'L0_attn_w_out': _L0_attn_in['w_out'], 'L0_attn_b_out': _L0_attn_in['b_out'], 'L0_xattn_ln_w': _L0_xattn_in['ln_w'], 'L0_xattn_ln_b': _L0_xattn_in['ln_b'], 'L0_xattn_wq': _L0_xattn_in['wq'], 'L0_xattn_wq_scale': _L0_xattn_in['wq_scale'], 'L0_xattn_q_in_scale': _L0_xattn_in['q_in_scale'], 'L0_xattn_wqx': _L0_xattn_in['wqx'], 'L0_xattn_wqx_scale': _L0_xattn_in['wqx_scale'], 'L0_xattn_qx_in_scale': _L0_xattn_in['qx_in_scale'], 'L0_xattn_wk': _L0_xattn_in['wk'], 'L0_xattn_wk_scale': _L0_xattn_in['wk_scale'], 'L0_xattn_k_in_scale': _L0_xattn_in['k_in_scale'], 'L0_xattn_wv': _L0_xattn_in['wv'], 'L0_xattn_wv_scale': _L0_xattn_in['wv_scale'], 'L0_xattn_v_in_scale': _L0_xattn_in['v_in_scale'], 'L0_xattn_w_kv_x': _L0_xattn_in['w_kv_x'], 'L0_xattn_qln_w': _L0_xattn_in['qln_w'], 'L0_xattn_qln_b': _L0_xattn_in['qln_b'], 'L0_xattn_kln_w': _L0_xattn_in['kln_w'], 'L0_xattn_kln_b': _L0_xattn_in['kln_b'], 'L0_xattn_qxln_w': _L0_xattn_in['qxln_w'], 'L0_xattn_qxln_b': _L0_xattn_in['qxln_b'], 'L0_xattn_kxln_w': _L0_xattn_in['kxln_w'], 'L0_xattn_kxln_b': _L0_xattn_in['kxln_b'], 'L0_xattn_wproj': _L0_xattn_in['wproj'], 'L0_xattn_proj_w_scale': _L0_xattn_in['proj_w_scale'], 'L0_xattn_proj_in_scale': _L0_xattn_in['proj_in_scale'], 'L0_xattn_proj_smooth': _L0_xattn_in['proj_smooth'], 'L0_ffn_router_w': _L0_ffn_in['router_w'], 'L0_ffn_gate_w': _L0_ffn_in['gate_w'], 'L0_ffn_up_w': _L0_ffn_in['up_w'], 'L0_ffn_down_w': _L0_ffn_in['down_w']}

def reference(x, ctx_2048, L0_attn_w_qkv, L0_attn_b_qkv, L0_attn_w_out, L0_attn_b_out, L0_xattn_ln_w, L0_xattn_ln_b, L0_xattn_wq, L0_xattn_wq_scale, L0_xattn_q_in_scale, L0_xattn_wqx, L0_xattn_wqx_scale, L0_xattn_qx_in_scale, L0_xattn_wk, L0_xattn_wk_scale, L0_xattn_k_in_scale, L0_xattn_wv, L0_xattn_wv_scale, L0_xattn_v_in_scale, L0_xattn_w_kv_x, L0_xattn_qln_w, L0_xattn_qln_b, L0_xattn_kln_w, L0_xattn_kln_b, L0_xattn_qxln_w, L0_xattn_qxln_b, L0_xattn_kxln_w, L0_xattn_kxln_b, L0_xattn_wproj, L0_xattn_proj_w_scale, L0_xattn_proj_in_scale, L0_xattn_proj_smooth, L0_ffn_router_w, L0_ffn_gate_w, L0_ffn_up_w, L0_ffn_down_w):
    import jax
    import jax.numpy as jnp

    def _L0_attn_ref(x, w_qkv, b_qkv, w_out, b_out):
        import jax, jax.numpy as jnp
        import numpy as np
        import math
        D_MODEL = 512
        NUM_HEADS = 16
        HEAD_DIM = D_MODEL // NUM_HEADS
        B, S, D = x.shape
        H, Hd = (NUM_HEADS, HEAD_DIM)
        qkv = jnp.einsum('bsd,ed->bse', x, w_qkv) + b_qkv
        qkv = qkv.reshape(B, S, 3, H, Hd)
        q = jnp.transpose(qkv[:, :, 0], (0, 2, 1, 3))
        k = jnp.transpose(qkv[:, :, 1], (0, 2, 1, 3))
        v = jnp.transpose(qkv[:, :, 2], (0, 2, 1, 3))
        scores = jnp.einsum('bhqd,bhkd->bhqk', q, k) / math.sqrt(Hd)
        causal = jnp.triu(jnp.full((S, S), -jnp.inf, dtype=scores.dtype), k=1)
        scores = scores + causal[None, None]
        attn = jax.nn.softmax(scores, axis=-1)
        out = jnp.einsum('bhqk,bhkd->bhqd', attn, v)
        out = jnp.transpose(out, (0, 2, 1, 3)).reshape(B, S, D)
        return jnp.einsum('bsd,ed->bse', out, w_out) + b_out

    def _L0_xattn_ref(hidden_states, cond, ln_w, ln_b, wq, wq_scale, q_in_scale, wqx, wqx_scale, qx_in_scale, wk, wk_scale, k_in_scale, wv, wv_scale, v_in_scale, w_kv_x, qln_w, qln_b, kln_w, kln_b, qxln_w, qxln_b, kxln_w, kxln_b, wproj, proj_w_scale, proj_in_scale, proj_smooth):
        import jax, jax.numpy as jnp
        import numpy as np
        FP8_MAX = 448.0
        EPS = 1e-05

        def _fp8_roundtrip(x):
            return x.astype(jnp.float8_e4m3fn).astype(jnp.float32)

        def _div_clamp_fp8(x, scale):
            y = jnp.clip(x.astype(jnp.float32) / scale, -FP8_MAX, FP8_MAX)
            y = y.astype(jnp.bfloat16).astype(jnp.float32)
            return _fp8_roundtrip(y)

        def _ln(x, w, b):
            mu = jnp.mean(x, axis=-1, keepdims=True)
            var = jnp.mean(jnp.square(x - mu), axis=-1, keepdims=True)
            return (x - mu) * jax.lax.rsqrt(var + EPS) * w + b

        def _fp8_linear_pertensor(x, wq, w_scale, in_scale):
            xq = _div_clamp_fp8(x, in_scale)
            return jnp.einsum('bsi,oi->bso', xq * in_scale, wq) * w_scale

        def _gqa(q, k, v):
            scale = 1.0 / np.sqrt(q.shape[-1])
            scores = jnp.einsum('bsghd,btgd->bghst', q, k) * scale
            p = jax.nn.softmax(scores, axis=-1)
            return jnp.einsum('bghst,btgd->bsghd', p, v)
        b, s, _ = hidden_states.shape
        sc = cond.shape[1]
        d = qln_w.shape[0]
        nh = wq.shape[0] // d
        g = wk.shape[0] // d
        hpg = nh // g
        ln_out = _ln(hidden_states, ln_w, ln_b)
        q = _fp8_linear_pertensor(ln_out, wq, wq_scale, q_in_scale).reshape(b, s, g, hpg, d)
        q = _ln(q, qln_w, qln_b)
        k = _fp8_linear_pertensor(ln_out, wk, wk_scale, k_in_scale).reshape(b, s, g, d)
        k = _ln(k, kln_w, kln_b)
        v = _fp8_linear_pertensor(ln_out, wv, wv_scale, v_in_scale).reshape(b, s, g, d)
        core = _gqa(q, k, v).reshape(b, s, nh * d)
        qx = _fp8_linear_pertensor(ln_out, wqx, wqx_scale, qx_in_scale).reshape(b, s, g, hpg, d)
        qx = _ln(qx, qxln_w, qxln_b)
        kvx = jnp.einsum('bsi,oi->bso', cond, w_kv_x)
        kx, vx = jnp.split(kvx, 2, axis=-1)
        kx = _ln(kx.reshape(b, sc, g, d), kxln_w, kxln_b)
        vx = vx.reshape(b, sc, g, d)
        xout = _gqa(qx, kx, vx).reshape(b, s, nh * d)
        cat = jnp.concatenate([core, xout], axis=-1)
        catq = _div_clamp_fp8(cat, proj_smooth)
        return jnp.einsum('bsi,oi->bso', catq, wproj) * (proj_in_scale * proj_w_scale)

    def _L0_ffn_ref(hidden_states, router_w, gate_w, up_w, down_w):
        import jax, jax.numpy as jnp
        import numpy as np
        TOP_P = 0.9
        S, B, H, I, E = (512, 4, 512, 1024, 8)

        def _top_p_weights(probs, top_p):
            order = jnp.argsort(-probs, axis=-1)
            sp = jnp.take_along_axis(probs, order, axis=-1)
            cum = jnp.cumsum(sp, axis=-1)
            exceed = cum > top_p
            first_idx = jnp.argmax(exceed, axis=-1)
            first = jnp.arange(probs.shape[-1])[None, :] == first_idx[:, None]
            keep = ~exceed | first
            kept = jnp.where(keep, sp, 0.0)
            t_idx = jnp.arange(probs.shape[0])[:, None]
            return jnp.zeros_like(probs).at[t_idx, order].set(kept)
        s, b, h = hidden_states.shape
        x = hidden_states.reshape(-1, h)
        probs = jax.nn.softmax(x @ router_w.T, axis=-1)
        w = _top_p_weights(probs, TOP_P)
        out = jnp.zeros_like(x)
        n_exp = router_w.shape[0]
        for e in range(n_exp):
            g = jax.nn.silu(x @ gate_w[e].T)
            u = x @ up_w[e].T
            y = g * u @ down_w[e].T
            out = out + y * w[:, e:e + 1]
        return out.reshape(s, b, h)
    x = x + _L0_attn_ref(_layernorm(x, axis=-1), L0_attn_w_qkv, L0_attn_b_qkv, L0_attn_w_out, L0_attn_b_out)
    x = x + _L0_xattn_ref(_layernorm(x, axis=-1), ctx_2048, L0_xattn_ln_w, L0_xattn_ln_b, L0_xattn_wq, L0_xattn_wq_scale, L0_xattn_q_in_scale, L0_xattn_wqx, L0_xattn_wqx_scale, L0_xattn_qx_in_scale, L0_xattn_wk, L0_xattn_wk_scale, L0_xattn_k_in_scale, L0_xattn_wv, L0_xattn_wv_scale, L0_xattn_v_in_scale, L0_xattn_w_kv_x, L0_xattn_qln_w, L0_xattn_qln_b, L0_xattn_kln_w, L0_xattn_kln_b, L0_xattn_qxln_w, L0_xattn_qxln_b, L0_xattn_kxln_w, L0_xattn_kxln_b, L0_xattn_wproj, L0_xattn_proj_w_scale, L0_xattn_proj_in_scale, L0_xattn_proj_smooth)
    x = x + _L0_ffn_ref(_layernorm(x, axis=-1), L0_ffn_router_w, L0_ffn_gate_w, L0_ffn_up_w, L0_ffn_down_w)
    return x

_drawn_inputs = setup_inputs


def setup_inputs(seed=0):
    import zlib

    import numpy as np

    out = dict(_drawn_inputs(seed))
    spreads = {'L0_xattn_ln_w': (1.0, 0.6),
     'L0_xattn_ln_b': (0.0, 0.1),
     'L0_xattn_q_in_scale': (0.05000000074505806, 0.6),
     'L0_xattn_qx_in_scale': (0.05000000074505806, 0.6),
     'L0_xattn_k_in_scale': (0.05000000074505806, 0.6),
     'L0_xattn_v_in_scale': (0.05000000074505806, 0.6),
     'L0_xattn_qln_w': (1.0, 0.6),
     'L0_xattn_qln_b': (0.0, 0.8),
     'L0_xattn_kln_w': (1.0, 0.6),
     'L0_xattn_kln_b': (0.0, 0.8),
     'L0_xattn_qxln_w': (1.0, 0.6),
     'L0_xattn_qxln_b': (0.0, 0.732),
     'L0_xattn_kxln_w': (1.0, 0.6),
     'L0_xattn_kxln_b': (0.0, 0.8),
     'L0_xattn_proj_smooth': (0.05000000074505806, 0.2)}
    factors = {'L0_attn_b_qkv': 4.77, 'L0_attn_b_out': 5.356, 'L0_ffn_router_w': 4.582}
    for name, (base, spread) in spreads.items():
        noise = np.random.default_rng([zlib.crc32(name.encode()), seed]).standard_normal(out[name].shape)
        drawn = base * np.exp(spread * noise) if base else spread * noise
        out[name] = jnp.asarray(drawn.astype(out[name].dtype))
    for name, factor in factors.items():
        out[name] = (out[name] * factor).astype(out[name].dtype)
    return out
```

```python
from contextlib import ExitStack

import numpy as np
import concourse.bass as bass
from concourse import mybir

ALU = mybir.AluOpType
ACT = mybir.ActivationFunctionType
AX = mybir.AxisListType
F32 = mybir.dt.float32
F16 = mybir.dt.float16
BF16 = mybir.dt.bfloat16
I32 = mybir.dt.int32
U16 = mybir.dt.uint16

P = 128
B, S, D = 2, 512, 512
T = B * S
NT = T // P
BT = S // P
KT = D // P
WS = 64.0
EPS = 1e-5
RSQRT_SEED = float(0x5F3759DF)
NEWTON = 3
RSQRT_STEPS = 3 + 3 * NEWTON

HD = 32
QUADS = 4
HQ = 4
SCALE_A = 1.0 / float(np.sqrt(HD))
UA = HQ * BT


def rsqrt(dve, sem, base, var, half, out, tmp):
    k = 0

    def step(ins):
        nonlocal k
        ins.then_inc(sem, 1)
        k += 1
        dve.wait_ge(sem, base + k)

    step(dve.tensor_scalar(half, var, EPS, None, ALU.add))
    step(dve.tensor_scalar(tmp.bitcast(I32), half.bitcast(I32), 1, None, ALU.arith_shift_right))
    step(dve.tensor_scalar(out.bitcast(I32), tmp.bitcast(I32), -1.0, RSQRT_SEED, ALU.mult, ALU.add))
    for _ in range(NEWTON):
        step(dve.tensor_tensor(tmp, out, out, ALU.mult))
        step(dve.scalar_tensor_tensor(out=tmp, in0=tmp, scalar=-0.5, in1=half, op0=ALU.mult, op1=ALU.mult))
        step(dve.scalar_tensor_tensor(out=out, in0=tmp, scalar=1.5, in1=out, op0=ALU.add, op1=ALU.mult))
    assert k == RSQRT_STEPS


def after(eng, sem, count):
    if not isinstance(count, int) or count > 0:
        eng.wait_ge(sem, count)


def alone(eng, passed):
    def wait(sem, count):
        after(eng, sem, count)
        if not isinstance(count, int):
            eng.sem_inc(passed)
    return wait


def build(nc, ins, out):
    x_d = ins["x"].rearrange("(t p) d -> t p d", p=P)
    out_d = out.rearrange("b (t p) d -> (b t) p d", p=P)
    top = ExitStack()

    def sem(name):
        return top.enter_context(nc.semaphore(name))

    def sbuf(ctx, name, shape, dt):
        return ctx.enter_context(nc.sbuf_tensor(name, shape, dt))

    with top:
        bank = top.enter_context(nc.psum_tensor("bank", [P, 8, 512], F32))
        X = sbuf(top, "X", [P, NT, D], F32)
        ident = sbuf(top, "ident", [P, P], F32)
        cols = sbuf(top, "cols", [P, ins["cols"].shape[1]], F32)

        with ExitStack() as ctx:
            XTh = sbuf(ctx, "XTh", [P, KT, T], F16)
            XTl = sbuf(ctx, "XTl", [P, KT, T], F16)
            with ExitStack() as c2:
                first_norm(nc, ins, sem, lambda n, s, d: sbuf(c2, n, s, d), bank, X, ident, cols, XTh, XTl, x_d)
            with ExitStack() as c2:
                causal_attention(nc, ins, sem, lambda n, s, d: sbuf(c2, n, s, d), bank, X, ident, XTh, XTl)
        with ExitStack() as ctx:
            rcols = sbuf(ctx, "rcols", [P, COLS], F32)
            xq = sbuf(ctx, "xq", [P, 4, KT, T], F16)
            cxh = sbuf(ctx, "cxh", [P, KT, B * SX], F16)
            cxl = sbuf(ctx, "cxl", [P, KT, B * SX], F16)
            with ExitStack() as c2:
                second_norm(nc, ins, sem, lambda n, s, d: sbuf(c2, n, s, d), bank, X, ident, cols, xq, cxh, cxl, rcols)
            with ExitStack() as c2:
                group_attention(nc, ins, sem, lambda n, s, d: sbuf(c2, n, s, d), bank, X, ident, cols, rcols, xq, cxh,
                                cxl)
        with ExitStack() as ctx:
            experts(nc, ins, sem, lambda n, s, d: sbuf(ctx, n, s, d), bank, X, ident, out_d)


def first_norm(nc, ins, sem, sb, bank, X, ident, cols, XTh, XTl, x_d):
    x_in = [sem(f"x_in{t}") for t in range(NT)]
    cols_in = sem("cols_in")
    id_set = sem("id_set")
    tiles = norm_tiles(sem, sb, "n1")
    with nc.Block() as block:
        @block.sync
        def _(sp):
            for t in range(NT):
                sp.dma_start(X[:, t, :], x_d[t]).then_inc(x_in[t], 16)
            sp.dma_start(cols[:], ins["cols"]).then_inc(cols_in, 16)
            sp.wait_ge(cols_in, 16)

        @block.gpsimd
        def _(pool):
            pool.memset(ident[:], 0.0).then_inc(id_set, 1)
            pool.wait_ge(id_set, 1)
            pool.affine_select(out=ident[:], in_=ident[:], compare_op=ALU.not_equal, fill=1.0, base=0,
                               pattern=[[-1, P]], channel_multiplier=1).then_inc(id_set, 1)

        @block.vector
        def _(dve):
            norm_vector(dve, tiles, X, XTh, XTl, bank, lambda t: dve.wait_ge(x_in[t], 16))

        @block.scalar
        def _(act):
            norm_scalar(act, tiles, X, XTh, bank)

        @block.tensor
        def _(pe):
            pe.wait_ge(id_set, 2)
            norm_tensor(pe, tiles, bank, ident)


class norm_tiles:

    def __init__(self, sem, sb, tag):
        self.stats = sb(f"stats_{tag}", [P, NT, 6], F32)
        self.mv = sb(f"mv_{tag}", [P, NT, 2], F32)
        self.half = sb(f"half_{tag}", [P, NT], F32)
        self.tmp = sb(f"tmp_{tag}", [P, NT], F32)
        self.rstd = sb(f"rstd_{tag}", [P, NT], F32)
        self.shift = sb(f"shift_{tag}", [P, NT], F32)
        self.xn = sb(f"xn_{tag}", [P, NT, D], F32)
        self.s_stats = sem(f"{tag}_stats")
        self.s_mv = sem(f"{tag}_mv")
        self.s_rsqrt = sem(f"{tag}_rsqrt")
        self.s_shift = sem(f"{tag}_shift")
        self.s_xn = sem(f"{tag}_xn")
        self.s_turned = sem(f"{tag}_turned")
        self.s_hi = sem(f"{tag}_hi")
        self.s_lo = sem(f"{tag}_lo")


def norm_stats(dve, n, src, arrived, base=0):
    for t in range(NT):
        arrived(t)
        dve.bn_stats(n.stats[:, t, :], src[:, t, :]).then_inc(n.s_stats, 1)
    for t in range(NT):
        dve.wait_ge(n.s_stats, NT * base + t + 1)
        dve.bn_aggr(n.mv[:, t, :], n.stats[:, t, :]).then_inc(n.s_mv, 1)
    dve.wait_ge(n.s_mv, NT * (base + 1))
    rsqrt(dve, n.s_rsqrt, RSQRT_STEPS * base, n.mv[:, :, 1], n.half[:], n.rstd[:], n.tmp[:])
    dve.scalar_tensor_tensor(out=n.shift[:], in0=n.mv[:, :, 0], scalar=-1.0, in1=n.rstd[:],
                             op0=ALU.mult, op1=ALU.mult).then_inc(n.s_shift, 1)


def norm_vector(dve, n, X, XTh, XTl, bank, arrived):
    norm_stats(dve, n, X, arrived)
    for t in range(NT):
        dve.wait_ge(n.s_hi, t + 1)
        dve.tensor_tensor(XTl[:, :, t * P:(t + 1) * P], bank[:, t % 2, :].rearrange("p (k c) -> p k c", k=KT),
                          XTh[:, :, t * P:(t + 1) * P], ALU.subtract).then_inc(n.s_lo, 1)


def norm_scalar(act, n, X, XTh, bank):
    act.wait_ge(n.s_shift, 1)
    for t in range(NT):
        act.activation(n.xn[:, t, :], X[:, t, :], ACT.Identity, scale=n.rstd[:, t:t + 1],
                       bias=n.shift[:, t:t + 1]).then_inc(n.s_xn, 1)
    for t in range(NT):
        act.wait_ge(n.s_turned, t + 1)
        act.activation(XTh[:, :, t * P:(t + 1) * P], bank[:, t % 2, :].rearrange("p (k c) -> p k c", k=KT),
                       ACT.Copy).then_inc(n.s_hi, 1)


def norm_tensor(pe, n, bank, ident):
    for t in range(NT):
        pe.wait_ge(n.s_xn, t + 1)
        if t >= 2:
            pe.wait_ge(n.s_lo, t - 1)
        for k in range(KT):
            ins = pe.transpose(bank[:, t % 2, k * P:(k + 1) * P], n.xn[:, t, k * P:(k + 1) * P], ident[:])
        ins.then_inc(n.s_turned, 1)


def three(pe, ps, ah, al, bh, bl, start, stop):
    pe.matmul(ps, ah, bh, start=start, stop=False)
    pe.matmul(ps, al, bh, start=False, stop=False)
    return pe.matmul(ps, ah, bl, start=False, stop=stop)


def causal_attention(nc, ins, sem, sb, bank, X, ident, XTh, XTl):
    STEPS = QUADS * B
    NQ = 3 * P
    wraw = sb("wraw", [P, KT, NQ], F32)
    woraw = sb("woraw", [P, D], F32)
    wh, wl = sb("wh", [P, KT, NQ], F16), sb("wl", [P, KT, NQ], F16)
    woh, wol = sb("woh", [P, D], F16), sb("wol", [P, D], F16)
    qkb = sb("qkb", [P, 2], F32)
    vb = sb("vb", [P, P], F32)
    bout = sb("bout", [P, D], F32)
    identb, mask = sb("identb", [P, P], BF16), sb("mask", [P, P], BF16)
    qf, kf, vf, af = (sb(x, [P, S], F32) for x in ("qf", "kf", "vf", "af"))
    qh, ql, kh, kl = (sb(x, [P, S], F16) for x in ("qh", "ql", "kh", "kl"))
    qs = [sb(f"qs{b}", [P, HQ, S], F16) for b in range(B)]
    ks = [sb(f"ks{b}", [P, HQ, S], F16) for b in range(B)]
    vh = [sb(f"vh{b}", [P, BT, P], F16) for b in range(B)]
    vl = [sb(f"vl{b}", [P, BT, P], F16) for b in range(B)]
    ao = [sb(f"ao{b}", [P, BT, P], F32) for b in range(B)]
    aoh, aol = sb("aoh", [P, S], F16), sb("aol", [P, S], F16)
    prob = [sb(f"prob{i}", [P, S], F32) for i in range(2)]
    pth = [sb(f"pth{i}", [P, S], F16) for i in range(2)]
    ptl = [sb(f"ptl{i}", [P, S], F16) for i in range(2)]
    mx, nm, rs, ri = (sb(x, [P, 4], F32) for x in ("mx", "nm", "rs", "ri"))
    SC, PT, O, J = ([bank[:, i, :], bank[:, i + 1, :]] for i in (0, 2, 4, 6))

    passed_sp, passed_pool = sem("a_passed_sp"), sem("a_passed_pool")
    w_in, wo_in, b_in, c_in = sem("a_w_in"), sem("a_wo_in"), sem("a_b_in"), sem("a_c_in")
    set_up = sem("a_set_up")
    w_hi, w_lo, wo_hi, wo_lo = sem("a_w_hi"), sem("a_w_lo"), sem("a_wo_hi"), sem("a_wo_lo")
    q_ps, k_ps, v_ps, t_ps, y_ps = (sem(f"a_{x}_ps") for x in ("q", "k", "v", "t", "y"))
    q_f, k_f, v_f, t_f, y_f = (sem(f"a_{x}_f") for x in ("q", "k", "v", "t", "y"))
    q_h, k_h, v_h, t_h = (sem(f"a_{x}_h") for x in ("q", "k", "v", "t"))
    q_l, k_l, v_l, t_l = (sem(f"a_{x}_l") for x in ("q", "k", "v", "t"))
    q_st, k_st = [sem(f"a_q_st{b}") for b in range(B)], [sem(f"a_k_st{b}") for b in range(B)]
    bias_x = sem("a_bias_x")
    scored, maxed, shifted, exped, turned, hi, lo, pved, recip, o_f = (
        sem(f"a_{x}") for x in ("scored", "maxed", "shifted", "exped", "turned", "hi", "lo", "pved", "recip", "o_f"))

    def loop(eng, body):
        body(0, first=True, last=False)
        with eng.Fori(1, QUADS - 1) as i:
            body(i, first=False, last=False)
        body(QUADS - 1, first=False, last=True)

    with nc.Block() as block:
        @block.sync
        def _(sp):
            wait = alone(sp, passed_sp)
            sp.dma_start(bout[:], ins["bout"]).then_inc(c_in, 16)

            def load_w(i, used):
                if used:
                    wait(w_lo, i)
                    wait(v_f, 2 * i)
                    wait(k_f, 2 * i)
                    wait(q_f, 2 * i)
                sp.dma_start(wraw[:], ins["w_qkv"][bass.ds(i, 1)].rearrange("a p k n -> p (a k) n")).then_inc(w_in, 16)
                sp.dma_start(qkb[:], ins["b_qk"][bass.ds(i, 1)].rearrange("a p n -> p (a n)")).then_inc(b_in, 16)
                sp.dma_start(vb[:], ins["b_v"][bass.ds(i, 1)].rearrange("a p n -> p (a n)")).then_inc(b_in, 16)

            def load_wo(i, used):
                if used:
                    wait(wo_lo, i)
                sp.dma_start(woraw[:], ins["w_out"][bass.ds(i, 1)].rearrange("a p n -> p (a n)")).then_inc(wo_in, 16)

            def stack(n, b, used):
                for h_done, l_done, ch, cl, dst, done, order, free in (
                        (q_h, q_l, qh, ql, qs[b], q_st[b], (0, 1, 0, 1), True),
                        (k_h, k_l, kh, kl, ks[b], k_st[b], (0, 0, 1, 1), False)):
                    wait(h_done, n + 1)
                    wait(l_done, n + 1)
                    if used and free:
                        wait(scored, UA * (n - 1))
                    for place, part in enumerate(order):
                        for h in range(HQ):
                            sp.dma_start(dst[HD * place:HD * (place + 1), h, :],
                                         (ch, cl)[part][HD * h:HD * (h + 1), :]).then_inc(done, 16)

            load_w(0, False)
            load_wo(0, False)
            stack(0, 0, False)

            def body(i, first, last):
                stack(2 * i + 1, 1, not first)
                if not last:
                    load_w(i + 1, True)
                    load_wo(i + 1, True)
                    stack(2 * i + 2, 0, True)

            loop(sp, body)

        @block.gpsimd
        def _(pool):
            wait = alone(pool, passed_pool)
            pool.memset(identb[:], 0.0).then_inc(set_up, 1)
            pool.memset(mask[:], 0.0).then_inc(set_up, 1)
            pool.wait_ge(set_up, 2)
            pool.affine_select(out=identb[:], in_=identb[:], compare_op=ALU.not_equal, fill=1.0, base=0,
                               pattern=[[-1, P]], channel_multiplier=1).then_inc(set_up, 1)
            pool.affine_select(out=mask[:], in_=mask[:], compare_op=ALU.is_ge, fill=-1e30, base=0,
                               pattern=[[-1, P]], channel_multiplier=1).then_inc(set_up, 1)

            def cast(dst, src, scale, done):
                pool.tensor_scalar(dst, src, scale, 1.0, ALU.mult, ALU.mult).then_inc(done, 1)

            def weights(i, used):
                wait(w_in, 16 * (i + 1))
                if used:
                    wait(v_ps, 2 * i)
                cast(wh[:], wraw[:], WS, w_hi)

            def out_weights(i, used):
                wait(wo_in, 16 * (i + 1))
                if used:
                    wait(y_ps, 4 * 2 * i)
                cast(woh[:], woraw[:], WS, wo_hi)

            def split(n, used, ready, src, h, l, h_done, l_done, free, free_at):
                wait(ready, n + 1)
                if used:
                    wait(free, free_at)
                cast(h, src[:], 1.0, h_done)
                wait(h_done, n + 1)
                pool.tensor_tensor(l, src[:], h, ALU.subtract).then_inc(l_done, 1)

            def project(n):
                split(n, False, q_f, qf, qh[:], ql[:], q_h, q_l, None, 0)
                split(n, False, k_f, kf, kh[:], kl[:], k_h, k_l, None, 0)

            def values(n, b, used):
                vhf, vlf = (x[b][:].rearrange("p k c -> p (k c)") for x in (vh, vl))
                split(n, used, v_f, vf, vhf, vlf, v_h, v_l, pved, UA * (n - 1))

            def outputs(n, used):
                split(n, used, t_f, af, aoh[:], aol[:], t_h, t_l, y_ps, 4 * n)

            weights(0, False)
            out_weights(0, False)
            project(0)
            values(0, 0, False)

            def stacks_made(i, b):
                wait(q_st[b], 16 * HQ * 4 * (i + 1))
                wait(k_st[b], 16 * HQ * 4 * (i + 1))

            def body(i, first, last):
                stacks_made(i, 0)
                project(2 * i + 1)
                if not first:
                    outputs(2 * i - 1, True)
                values(2 * i + 1, 1, not first)
                if not last:
                    weights(i + 1, True)
                if not first:
                    out_weights(i, True)
                if not last:
                    stacks_made(i, 1)
                    project(2 * i + 2)
                outputs(2 * i, not first)
                if not last:
                    values(2 * i + 2, 0, True)

            loop(pool, body)
            outputs(STEPS - 1, True)

        @block.scalar
        def _(act):
            def projected(n, used, ready, j, dst, bias, done, h_done):
                act.wait_ge(ready, n + 1)
                if used:
                    act.wait_ge(h_done, n)
                act.activation(dst[:], J[j], ACT.Identity, scale=1.0 / WS, bias=bias).then_inc(done, 1)

            def exp(U, u, used):
                qt = u % BT
                act.wait_ge(shifted, U + 1)
                if used:
                    act.wait_ge(turned, U - 1)
                act.activation(prob[u % 2][:, 0:P * (qt + 1)], SC[u % 2][:, 0:P * (qt + 1)], ACT.Exp, scale=SCALE_A,
                               bias=nm[:, u % 4:u % 4 + 1], accum_out=rs[:, u % 4:u % 4 + 1]).then_inc(exped, 1)

            def part_hi(U, u, used):
                L = P * (u % BT + 1)
                act.wait_ge(turned, U + 1)
                if used:
                    act.wait_ge(pved, U - 1)
                act.activation(pth[u % 2][:, 0:L], PT[u % 2][:, 0:L], ACT.Copy).then_inc(hi, 1)

            act.wait_ge(b_in, 32)
            projected(0, False, q_ps, 1, qf, qkb[:, 0:1], q_f, None)
            projected(0, False, k_ps, 1, kf, qkb[:, 1:2], k_f, None)

            def n_over_one(n):
                return not isinstance(n, int) or n > 1

            def body(i, first, last):
                quad_of_next = [i, i + 1]
                for b in range(B):
                    n = 2 * i + b
                    one(n, b, quad_of_next[b], first and b == 0, last and b == 1)

            def one(n, b, nq, first, last):
                for u in range(UA):
                    U = UA * n + u
                    exp(U, u, not (first and u < 2))
                    if not (first and u == 0):
                        part_hi(U - 1, u - 1, not (first and u <= 2))
                    if u == 1 and not last:
                        act.wait_ge(b_in, 32 * (nq + 1))
                        projected(n + 1, True, q_ps, 1, qf, qkb[:, 0:1], q_f, q_l)
                    if u == 3 and not first:
                        act.wait_ge(t_ps, n)
                        if n_over_one(n):
                            act.wait_ge(t_l, n - 1)
                        act.activation(af[:], J[0], ACT.Copy).then_inc(t_f, 1)
                    if u == 4 and not last:
                        projected(n + 1, True, k_ps, 1, kf, qkb[:, 1:2], k_f, k_l)

            loop(act, body)
            part_hi(UA * STEPS - 1, UA - 1, True)
            act.wait_ge(t_ps, STEPS)
            act.wait_ge(t_l, STEPS - 1)
            act.activation(af[:], J[0], ACT.Copy).then_inc(t_f, 1)

        @block.vector
        def _(dve):
            dve.wait_ge(c_in, 16)
            for t in range(NT):
                dve.tensor_tensor(X[:, t, :], X[:, t, :], bout[:], ALU.add).then_inc(bias_x, 1)

            def low(dst, raw, h, h_done, l_done, i):
                dve.wait_ge(h_done, i + 1)
                dve.scalar_tensor_tensor(out=dst[:], in0=raw[:], scalar=WS, in1=h[:], op0=ALU.mult,
                                         op1=ALU.subtract).then_inc(l_done, 1)

            def values(n, used, nq):
                dve.wait_ge(v_ps, n + 1)
                dve.wait_ge(b_in, 32 * (nq + 1))
                if used:
                    dve.wait_ge(v_l, n)
                dve.scalar_tensor_tensor(out=vf[:].rearrange("p (k c) -> p k c", k=BT),
                                         in0=J[0].rearrange("p (k c) -> p k c", k=BT), scalar=1.0 / WS,
                                         in1=vb[:].unsqueeze(1).broadcast_to([P, BT, P]),
                                         op0=ALU.mult, op1=ALU.add).then_inc(v_f, 1)

            def maxima(U, u):
                s = u % 4
                dve.wait_ge(scored, U + 1)
                dve.tensor_reduce(mx[:, s:s + 1], SC[u % 2][:, 0:P * (u % BT + 1)], AX.X, ALU.max).then_inc(maxed, 1)
                dve.wait_ge(maxed, U + 1)
                dve.tensor_scalar(nm[:, s:s + 1], mx[:, s:s + 1], -SCALE_A, None, ALU.mult).then_inc(shifted, 1)

            def part_lo(U, u):
                L = P * (u % BT + 1)
                dve.wait_ge(hi, U + 1)
                dve.tensor_tensor(ptl[u % 2][:, 0:L], PT[u % 2][:, 0:L], pth[u % 2][:, 0:L],
                                  ALU.subtract).then_inc(lo, 1)

            def normalise(U, u, b, n, used):
                u = u % UA
                h, qt, s = u // BT, u % BT, u % 4
                dve.wait_ge(exped, U + 1)
                dve.reciprocal(ri[:, s:s + 1], rs[:, s:s + 1]).then_inc(recip, 1)
                dve.wait_ge(recip, U + 1)
                dve.wait_ge(pved, U + 1)
                if used and u == 0:
                    dve.wait_ge(t_ps, n - 1)
                dve.tensor_scalar(ao[b][:, qt, h * HD:(h + 1) * HD], O[u % 2][:, 0:HD], ri[:, s:s + 1], None,
                                  ALU.mult).then_inc(o_f, 1)

            def project_out(n, t, b):
                dve.wait_ge(y_ps, 4 * n + t + 1)
                if isinstance(n, int) and n < 2 and t == 0:
                    dve.wait_ge(bias_x, NT)
                dve.scalar_tensor_tensor(out=X[:, BT * b + t, :], in0=J[(0, 1, 1, 0)[t]], scalar=1.0 / WS,
                                         in1=X[:, BT * b + t, :], op0=ALU.mult, op1=ALU.add).then_inc(y_f, 1)

            low(wl, wraw, wh, w_hi, w_lo, 0)
            low(wol, woraw, woh, wo_hi, wo_lo, 0)
            values(0, False, 0)

            def step(i, n, b, first, last):
                for u in range(UA):
                    U = UA * n + u
                    maxima(U, u)
                    if not (first and u == 0):
                        part_lo(U - 1, u - 1)
                    if not (first and u <= 1):
                        before = 1 if u < 2 else 0
                        normalise(U - 2, u - 2, (b + before) % 2, n - before,
                                  not (first or (isinstance(n, int) and n - before < 2)))
                    if u in (6, 7, 9, 10) and not first:
                        project_out(n - 1, (6, 7, 9, 10).index(u), 1 - b)
                    if u == 8 and not last:
                        values(n + 1, True, i if b == 0 else i + 1)
                    if u == 12 and b == 0 and not last_quad:
                        low(wl, wraw, wh, w_hi, w_lo, i + 1)
                    if u == 12 and b == 0 and not first:
                        low(wol, woraw, woh, wo_hi, wo_lo, i)

            last_quad = False

            def body(i, first, last):
                nonlocal last_quad
                last_quad = last
                step(i, 2 * i, 0, first, False)
                step(i, 2 * i + 1, 1, False, last)

            loop(dve, body)
            end = UA * STEPS
            part_lo(end - 1, UA - 1)
            normalise(end - 2, UA - 2, 1, STEPS - 1, True)
            normalise(end - 1, UA - 1, 1, STEPS - 1, True)
            for t in range(BT):
                project_out(STEPS - 1, t, 1)

        @block.tensor
        def _(pe):
            def projection(n, b, j, first_col, done):
                for k in range(KT):
                    w = slice(first_col, first_col + P)
                    ins_ = three(pe, J[j], wh[:, k, w], wl[:, k, w], XTh[:, k, S * b:S * (b + 1)],
                                 XTl[:, k, S * b:S * (b + 1)], k == 0, k == KT - 1)
                ins_.then_inc(done, 1)

            def values(n, b):
                for t in range(BT):
                    tok = slice(S * b + P * t, S * b + P * (t + 1))
                    for k in range(KT):
                        ins_ = three(pe, J[0][:, P * t:P * (t + 1)], XTh[:, k, tok], XTl[:, k, tok],
                                     wh[:, k, 2 * P:3 * P], wl[:, k, 2 * P:3 * P], k == 0, k == KT - 1)
                ins_.then_inc(v_ps, 1)

            def scores(n, U, u, b, i, used):
                h, qt = u // BT, u % BT
                L = P * (qt + 1)
                if u == 0:
                    pe.wait_ge(q_st[b], 16 * HQ * 4 * (i + 1))
                    pe.wait_ge(k_st[b], 16 * HQ * 4 * (i + 1))
                if used:
                    pe.wait_ge(exped, U - 1)
                q = qs[b][:, h, P * qt:P * (qt + 1)]
                if qt:
                    pe.matmul(SC[u % 2][:, 0:L - P], q, ks[b][:, h, 0:L - P], start=True, stop=True)
                pe.matmul(SC[u % 2][:, L - P:L], identb[:], mask[:], start=True, stop=False)
                pe.matmul(SC[u % 2][:, L - P:L], q, ks[b][:, h, L - P:L], start=False, stop=True).then_inc(scored, 1)

            def turn(U, u, used):
                pe.wait_ge(exped, U + 1)
                if used:
                    pe.wait_ge(lo, U - 1)
                for k in range(u % BT + 1):
                    ins_ = pe.transpose(PT[u % 2][:, P * k:P * (k + 1)], prob[u % 2][:, P * k:P * (k + 1)], ident[:])
                ins_.then_inc(turned, 1)

            def pv(n, U, u, b, used):
                u = u % UA
                h, qt = u // BT, u % BT
                if u == 0:
                    pe.wait_ge(v_l, n + 1)
                pe.wait_ge(lo, U + 1)
                if used:
                    pe.wait_ge(o_f, U - 1)
                for k in range(qt + 1):
                    ins_ = three(pe, O[u % 2][:, 0:HD], pth[u % 2][:, P * k:P * (k + 1)],
                                 ptl[u % 2][:, P * k:P * (k + 1)], vh[b][:, k, HD * h:HD * (h + 1)],
                                 vl[b][:, k, HD * h:HD * (h + 1)], k == 0, k == qt)
                ins_.then_inc(pved, 1)

            def turn_out(n, b):
                pe.wait_ge(o_f, UA * (n + 1))
                for t in range(BT):
                    ins_ = pe.transpose(J[0][:, P * t:P * (t + 1)], ao[b][:, t, :], ident[:])
                ins_.then_inc(t_ps, 1)

            def project_out(n, t):
                if t == 0:
                    pe.wait_ge(t_l, n + 1)
                tok = slice(P * t, P * (t + 1))
                three(pe, J[(0, 1, 1, 0)[t]], aoh[:, tok], aol[:, tok], woh[:], wol[:], True, True).then_inc(y_ps, 1)

            pe.wait_ge(set_up, 4)
            pe.wait_ge(w_lo, 1)
            projection(0, 0, 1, 0, q_ps)
            pe.wait_ge(q_f, 1)
            projection(0, 0, 1, P, k_ps)
            values(0, 0)

            def step(i, n, b, first, last):
                for u in range(UA):
                    U = UA * n + u
                    scores(n, U, u, b, i, not (first and u < 2))
                    if u == 1 and not last:
                        if b == 1:
                            pe.wait_ge(w_lo, i + 2)
                        if not first:
                            pe.wait_ge(k_f, n + 1)
                        if not (first or (isinstance(n, int) and n == 1)):
                            pe.wait_ge(y_f, 4 * (n - 2) + 3)
                        if first:
                            pe.wait_ge(k_f, 1)
                        projection(n + 1, 1 - b, 1, 0, q_ps)
                    if u == 3 and not first:
                        pe.wait_ge(v_f, n + 1)
                        if not (isinstance(n, int) and n == 1):
                            pe.wait_ge(y_f, 4 * (n - 1))
                        turn_out(n - 1, 1 - b)
                    if u == 4 and not last:
                        pe.wait_ge(q_f, n + 2)
                        projection(n + 1, 1 - b, 1, P, k_ps)
                    if u == 6 and not first:
                        if b == 1:
                            pe.wait_ge(wo_lo, i + 1)
                        project_out(n - 1, 0)
                    if u == 7 and not first:
                        if not last:
                            pe.wait_ge(k_f, n + 2)
                        project_out(n - 1, 1)
                    if u == 8 and not last:
                        if first:
                            pe.wait_ge(v_f, 1)
                        else:
                            pe.wait_ge(y_f, 4 * (n - 1) + 1)
                        values(n + 1, 1 - b)
                    if u == 9 and not first:
                        pe.wait_ge(y_f, 4 * (n - 1) + 2)
                        project_out(n - 1, 2)
                    if u == 10 and not first:
                        if not last:
                            pe.wait_ge(v_f, n + 2)
                        else:
                            pe.wait_ge(y_f, 4 * (n - 1) + 1)
                        project_out(n - 1, 3)
                    if not (first and u == 0):
                        turn(U - 1, u - 1, not (first and u <= 2))
                    if not (first and u <= 1):
                        before = 1 if u < 2 else 0
                        pv(n - before, U - 2, u - 2, (b + before) % 2, not (first and u <= 3))

            def body(i, first, last):
                step(i, 2 * i, 0, first, False)
                step(i, 2 * i + 1, 1, False, last)

            loop(pe, body)
            end = UA * STEPS
            turn(end - 1, UA - 1, True)
            pv(STEPS - 1, end - 2, UA - 2, 1, True)
            pv(STEPS - 1, end - 1, UA - 1, 1, True)
            pe.wait_ge(y_f, 4 * (STEPS - 1))
            turn_out(STEPS - 1, 1)
            for t in range(BT):
                if t:
                    pe.wait_ge(y_f, 4 * (STEPS - 1) + t)
                project_out(STEPS - 1, t)


GROUPS = 8
HPG = 2
DH = 128
SX = 1024
XT = SX // P
SCALE_X = 1.0 / float(np.sqrt(DH))
KINDS = 2 * HPG
UX = KINDS * BT
SELF_U = HPG * BT
PIECES = SELF_U + 2 * (UX - SELF_U)
PAIRS = UX // 2
BLOCKS = KINDS * BT + BT + XT
FP8_MAX = 448.0

C_LNW, C_LNB, C_IN, C_HEAD, C_SMOOTH, C_SCALAR = 0, 4, 8, 24, 32, 64
COLS = 70
SC_Q, SC_QX, SC_K, SC_V, SC_PIN, SC_PW = range(6)


def round_fp8(dve, sem, base, y, unit, total):
    dve.tensor_scalar(y, y, FP8_MAX, -FP8_MAX, ALU.min, ALU.max).then_inc(sem, 1)
    dve.wait_ge(sem, base + 1)
    dve.tensor_scalar(unit.bitcast(U16), y.bitcast(U16), 0x7F80, 0x40, ALU.bitwise_and, ALU.bitwise_or).then_inc(sem, 1)
    dve.wait_ge(sem, base + 2)
    dve.tensor_scalar(unit, unit, 1.5 * 2.0 ** -6, 2.0 ** 20, ALU.max, ALU.mult).then_inc(sem, 1)
    dve.wait_ge(sem, base + 3)
    dve.tensor_tensor(total, y, unit, ALU.add).then_inc(sem, 1)


ROUND_STEPS = 4


def second_norm(nc, ins, sem, sb, bank, X, ident, cols, xq, cxh, cxl, rcols):
    n = norm_tiles(sem, sb, "n2")
    L = [sb(f"L{i}", [P, S], F32) for i in range(2)]
    y = [sb(f"y{i}", [P, 4, S], BF16) for i in range(2)]
    unit = [sb(f"unit{i}", [P, 4, S], BF16) for i in range(2)]
    total = [sb(f"total{i}", [P, 4, S], F32) for i in range(2)]
    craw = [sb(f"craw{i}", [P, B * SX], F32) for i in range(2)]
    c_in = [sem(f"b_c_in{i}") for i in range(2)]
    c_hi, c_lo, s_rcols = sem("b_c_hi"), sem("b_c_lo"), sem("b_rcols")
    L_f, y_f, r_dve, r_pool = sem("b_L_f"), sem("b_y_f"), sem("b_r_dve"), sem("b_r_pool")
    with nc.Block() as block:
        @block.sync
        def _(sp):
            for k in range(KT):
                if k >= 2:
                    sp.wait_ge(c_lo, k - 1)
                sp.dma_start(craw[k % 2][:], ins["ctx"][k]).then_inc(c_in[k % 2], 16)

        @block.scalar
        def _(act):
            for k in range(2):
                act.wait_ge(c_in[k], 16)
                act.activation(cxh[:, k, :], craw[k][:], ACT.Copy).then_inc(c_hi, 1)
            for again in range(2):
                act.wait_ge(n.s_shift, again + 1)
                for t in range(NT):
                    act.activation(n.xn[:, t, :], (X, n.xn)[again][:, t, :], ACT.Identity, scale=n.rstd[:, t:t + 1],
                                   bias=n.shift[:, t:t + 1]).then_inc(n.s_xn, 1)
            act.wait_ge(s_rcols, 2)
            for j in range(B * KT):
                k = j % KT
                act.wait_ge(n.s_turned, j + 1)
                act.activation(L[j % 2][:], bank[:, j % 2, :], ACT.Identity, scale=cols[:, C_LNW + k:C_LNW + k + 1],
                               bias=cols[:, C_LNB + k:C_LNB + k + 1]).then_inc(L_f, 1)
                act.wait_ge(L_f, j + 1)
                if j >= 2:
                    act.wait_ge(r_pool, j - 1)
                for s in range(4):
                    c = C_IN + 4 * s + k
                    act.activation(y[j % 2][:, s, :], L[j % 2][:], ACT.Copy, scale=rcols[:, c:c + 1]).then_inc(y_f, 1)
                if j in (1, 3):
                    kk = 2 + j // 2
                    act.wait_ge(c_in[kk % 2], 32)
                    act.activation(cxh[:, kk, :], craw[kk % 2][:], ACT.Copy).then_inc(c_hi, 1)

        @block.vector
        def _(dve):
            for c in (slice(C_IN, C_IN + 4 * KT), slice(C_SMOOTH, C_SMOOTH + GROUPS * KINDS)):
                dve.reciprocal(rcols[:, c], cols[:, c]).then_inc(s_rcols, 1)
            norm_stats(dve, n, X, lambda t: None)
            norm_stats(dve, n, n.xn, lambda t: dve.wait_ge(n.s_xn, t + 1), base=1)

            def ctx_lo(k):
                dve.wait_ge(c_hi, k + 1)
                dve.tensor_tensor(cxl[:, k, :], craw[k % 2][:], cxh[:, k, :], ALU.subtract).then_inc(c_lo, 1)

            ctx_lo(0)
            ctx_lo(1)
            for j in range(B * KT):
                dve.wait_ge(y_f, 4 * (j + 1))
                round_fp8(dve, r_dve, ROUND_STEPS * j, y[j % 2][:], unit[j % 2][:], total[j % 2][:])
                if j in (2, 4):
                    ctx_lo(1 + j // 2)

        @block.gpsimd
        def _(pool):
            for j in range(B * KT):
                b, k = j // KT, j % KT
                pool.wait_ge(r_dve, ROUND_STEPS * (j + 1))
                pool.tensor_tensor(xq[:, :, k, S * b:S * (b + 1)], total[j % 2][:], unit[j % 2][:],
                                   ALU.subtract).then_inc(r_pool, 1)

        @block.tensor
        def _(pe):
            pe.wait_ge(n.s_xn, 2 * NT)
            for j in range(B * KT):
                b, k = j // KT, j % KT
                if j >= 2:
                    pe.wait_ge(L_f, j - 1)
                for t in range(BT):
                    ins_ = pe.transpose(bank[:, j % 2, P * t:P * (t + 1)],
                                        n.xn[:, BT * b + t, P * k:P * (k + 1)], ident[:])
                ins_.then_inc(n.s_turned, 1)


JOBS = ("A0 A1 A2 A3 B0 R3 C0 C1 B1 C2 C3 Y0 Y1 R0 Y2 Y3 T0 T1 T2 T3 T4 R1 T5 T6 R2").split()
SLOT_A = {0: "A0", 1: "A2", 2: "B0", 3: "C0", 4: "B1", 5: "C3", 6: "Y1", 7: "Y2", 8: "T0", 9: "T2", 10: "T4", 11: "T5"}
SLOT_B = {0: "A1", 1: "A3", 2: "R3", 3: "C1", 4: "C2", 5: "Y0", 6: "R0", 7: "Y3", 8: "T1", 9: "T3", 10: "R1",
          11: "T6", 14: "R2"}
V_ORDER = ("B0", "C0", "C1", "B1", "C2", "C3")
NEXT = [j for j in JOBS if j[0] in "ABCT"]
LATE = [j for j in JOBS if j[0] == "Y"] + ["R3"]


def jobs_of(first, last):
    return [j for j in JOBS if not (first and j in LATE) and not (last and j in NEXT)]


def job_number(name, n, first=False, last=False, prologue=False):
    if prologue:
        return NEXT.index(name)
    if first:
        return len(NEXT) + jobs_of(True, False).index(name)
    return len(NEXT) - len(LATE) + len(JOBS) * n + jobs_of(False, last).index(name)


def piece_end(u):
    if u < 0:
        return piece_end(u + UX) - PIECES
    return u + 1 if u < SELF_U else SELF_U + 2 * (u + 1 - SELF_U)


def group_attention(nc, ins, sem, sb, bank, X, ident, cols, rcols, xq, cxh, cxl):
    STEPS = GROUPS * B
    wraw = sb("xwraw", [P, KT, S], F32)
    w1h, w1l, w2h, w2l, w3h, w3l = (sb(f"x{x}", [P, KT, S], F16) for x in ("w1h", "w1l", "w2h", "w2l", "w3h", "w3l"))
    qr = sb("qr", [P, BT, 5 * DH], F32)
    kr = sb("kr", [P, XT, DH], F32)
    stats, mv = sb("xstats", [P, BLOCKS, 6], F32), sb("xmv", [P, BLOCKS, 2], F32)
    half, tmp, rstd, shift = (sb(f"x{x}", [P, BLOCKS], F32) for x in ("half", "tmp", "rstd", "shift"))
    ft = [sb(f"ft{i}", [P, S], F32) for i in range(2)]
    vt = [ft[i][:, 0:2 * DH].rearrange("p (t c) -> p t c", t=2) for i in range(2)]
    qh, ql = ([sb(f"x{x}{b}", [P, KINDS, S], F16) for b in range(B)] for x in ("qh", "ql"))
    kh, kl = ([sb(f"x{x}{b}", [P, S], F16) for b in range(B)] for x in ("kh", "kl"))
    kxh, kxl = ([sb(f"{x}{b}", [P, SX], F16) for b in range(B)] for x in ("kxh", "kxl"))
    vh, vl = ([sb(f"x{x}{b}", [P, BT, DH], F16) for b in range(B)] for x in ("vh", "vl"))
    vxh, vxl = ([sb(f"{x}{b}", [P, XT, DH], F16) for b in range(B)] for x in ("vxh", "vxl"))
    prob = [sb(f"xprob{i}", [P, SX], F32) for i in range(2)]
    pth, ptl = ([sb(f"x{x}{i}", [P, XT, 2 * P], F16) for i in range(2)] for x in ("pth", "ptl"))
    mx, nm = sb("xmx", [P, 4], F32), sb("xnm", [P, 4], F32)
    rs, ri = sb("xrs", [P, 2, BT], F32), sb("xri", [P, 2, BT], F32)
    R = sb("R", [P, S], F32)
    y, unit, total = sb("xy", [P, S], BF16), sb("xunit", [P, S], BF16), sb("xtotal", [P, S], F32)
    cat = sb("cat", [P, KINDS, S], F16)
    rsm = sb("rsm", [P, KINDS], F32)
    psc = sb("psc", [P, 1], F32)
    SC = [bank[:, 2 * i:2 * i + 2, :].rearrange("p a c -> p (a c)") for i in range(2)]
    PT, O, J = [bank[:, 4, :], bank[:, 5, :]], bank[:, 6, :], bank[:, 7, :]

    passed_sp, passed_pool, passed_dve = sem("x_passed_sp"), sem("x_passed_pool"), sem("x_passed_dve")
    w_in = sem("x_w_in")
    w_hi, w_lo = sem("x_w_hi"), sem("x_w_lo")
    job_done, job_read = sem("x_job_done"), sem("x_job_read")
    s_stats, s_mv, s_rsqrt, s_shift, applied = (sem(f"x_{x}") for x in ("stats", "mv", "rsqrt", "shift", "applied"))
    t_hi, t_lo, v_hi, v_lo = (sem(f"x_{x}") for x in ("t_hi", "t_lo", "v_hi", "v_lo"))
    scored, maxed, shifted, exped, turned, hi, lo, pved, recip = (
        sem(f"x_{x}") for x in ("scored", "maxed", "shifted", "exped", "turned", "hi", "lo", "pved", "recip"))
    o_read, rounding, rounded, s_rsm, s_psc = (sem(f"x_{x}") for x in ("o_read", "rounding", "rounded", "rsm", "psc"))
    W1N, W2N, W3N = 2 * KT, 3 * KT, KT
    WN = W1N + W2N + W3N

    def w_base(g):
        return W1N + W2N + WN * g

    def loop(body):
        def run(eng):
            body(0, True, False)
            with eng.Fori(1, GROUPS - 1) as g:
                body(g, False, False)
            body(GROUPS - 1, False, True)
        return run

    def split_ops(chunk):
        if chunk == 1:
            return [(k, k, slice(256 * s, 256 * (s + 1)), cols[:, C_IN + 4 * s + k:C_IN + 4 * s + k + 1])
                    for k in range(KT) for s in range(2)]
        if chunk == 2:
            return [x for k in range(KT) for x in
                    [(k, k, slice(DH * s, DH * (s + 1)), cols[:, C_IN + 8 + 4 * s + k:C_IN + 9 + 4 * s + k])
                     for s in range(2)] + [(k, k, slice(2 * DH, 4 * DH), WS)]]
        return [(k, k, slice(0, S), 1.0) for k in range(KT)]

    with nc.Block() as block:
        @block.sync
        def _(sp):
            wait = alone(sp, passed_sp)
            def load(chunk, g, before):
                wait(w_lo, before)
                sp.dma_start(wraw[:], ins["w_group"][bass.ds(g, 1), chunk - 1].rearrange("a p k n -> p (a k) n"))\
                    .then_inc(w_in, 16)

            load(1, 0, 0)
            load(2, 0, W1N)

            def body(g, first, last):
                if not last:
                    load(1, g + 1, w_base(g))
                    load(2, g + 1, w_base(g) + W1N)
                    load(3, g, w_base(g) + W1N + W2N)
                else:
                    load(3, g, w_base(g))

            loop(body)(sp)

        @block.gpsimd
        def _(pool):
            wait = alone(pool, passed_pool)
            def split_hi(chunk, loaded, free, count):
                wait(w_in, 16 * loaded)
                wait(free, count)
                wh = (w1h, w2h, w3h)[chunk - 1]
                for _, k, c, scale in split_ops(chunk):
                    pool.tensor_scalar(wh[:, k, c], wraw[:, k, c], scale, 1.0, ALU.mult, ALU.mult).then_inc(w_hi, 1)

            def values(name, m, b, job):
                v = V_ORDER.index(name)
                j = int(name[1])
                h, l = (vh, vl) if name[0] == "B" else (vxh, vxl)
                wait(job_read, job + 1)
                wait(pved, PAIRS * (m - 1))
                pool.tensor_scalar(h[b][:, 2 * j:2 * j + 2, :], vt[v % 2], 1.0, 1.0, ALU.mult, ALU.mult)\
                    .then_inc(v_hi, 1)
                wait(v_hi, len(V_ORDER) * m + v + 1)
                pool.tensor_tensor(l[b][:, 2 * j:2 * j + 2, :], vt[v % 2], h[b][:, 2 * j:2 * j + 2, :],
                                   ALU.subtract).then_inc(v_lo, 1)

            def apply(m):
                wait(s_shift, m + 1)
                for i in range(BLOCKS):
                    if i < 5 * BT:
                        c, t = i // BT, i % BT
                        a = qr[:, t, DH * c:DH * (c + 1)]
                    else:
                        a = kr[:, i - 5 * BT, :]
                    pool.tensor_scalar(a, a, rstd[:, i:i + 1], shift[:, i:i + 1], ALU.mult, ALU.add)\
                        .then_inc(applied, 1)

            def turned_parts(i, m, b, job):
                if i < 4:
                    h, l = qh[b][:, i, :], ql[b][:, i, :]
                elif i == 4:
                    h, l = kh[b][:], kl[b][:]
                else:
                    half_ = slice(S * (i - 5), S * (i - 4))
                    h, l = kxh[b][:, half_], kxl[b][:, half_]
                wait(job_read, job + 1)
                if i == 0:
                    wait(scored, UX * (m - 1))
                pool.tensor_scalar(h, ft[i % 2][:], 1.0, 1.0, ALU.mult, ALU.mult).then_inc(t_hi, 1)
                wait(t_hi, 7 * m + i + 1)
                pool.tensor_tensor(l, ft[i % 2][:], h, ALU.subtract).then_inc(t_lo, 1)

            def quantised(n, kind, cat_read=0):
                count = KINDS * n + kind + 1
                wait(rounding, ROUND_STEPS * count)
                wait(job_done, cat_read)
                pool.tensor_tensor(cat[:, kind, :], total[:], unit[:], ALU.subtract).then_inc(rounded, 1)

            split_hi(1, 1, None, 0)
            split_hi(2, 2, None, 0)
            for name in V_ORDER:
                values(name, 0, 0, job_number(name, 0, prologue=True))
            apply(0)
            for i in range(7):
                turned_parts(i, 0, 0, job_number(f"T{i}", 0, prologue=True))

            def step(g, n, b, first, last, last_group):
                job = lambda name: job_number(name, n, first, last)
                for u in range(UX):
                    if not last:
                        for name in [x for x in (SLOT_A.get(u), SLOT_B.get(u)) if x in V_ORDER]:
                            values(name, n + 1, 1 - b, job(name))
                    if u == 3 and not first:
                        quantised(n - 1, 3)
                    if b == 0 and not last_group:
                        if u == 2:
                            split_hi(1, 3 * g + 3, job_done, job("A3") + 1)
                    if u == 7:
                        if not last:
                            apply(n + 1)
                        if b == 0 and not last_group:
                            split_hi(2, 3 * g + 4, job_done, job("C3") + 1)
                        quantised(n, 0, 0 if first else job("Y3") + 1)
                    if b == 0 and u == 13:
                        split_hi(3, 3 * g + 5 if not last_group else 3 * g + 3, job_done,
                                 job("Y3") + 1 if not first else 0)
                    for name in (SLOT_A.get(u), SLOT_B.get(u)):
                        if not last and name and name[0] == "T":
                            turned_parts(int(name[1]), n + 1, 1 - b, job(name))
                    if u in (11, 15):
                        quantised(n, (u - 7) // 4)

            def body(g, first, last):
                step(g, 2 * g, 0, first, False, last)
                step(g, 2 * g + 1, 1, False, last, last)

            loop(body)(pool)
            quantised(STEPS - 1, 3)

        @block.scalar
        def _(act):
            def read_job(name, m, b, job, n=0):
                k, j = name[0], int(name[1])
                act.wait_ge(job_done, job + 1)
                if k == "A":
                    for s, c in enumerate((SC_Q, SC_QX)):
                        r = slice(256 * s, 256 * (s + 1))
                        last = act.activation(qr[:, j, r], J[:, r], ACT.Copy, scale=cols[:, C_SCALAR + c:C_SCALAR + c + 1])
                elif k in "BC":
                    v = V_ORDER.index(name)
                    after(act, v_lo, len(V_ORDER) * m + v - 1)
                    if v == 0:
                        after(act, t_lo, 7 * m)
                    Jv = J.rearrange("p (t s c) -> p t s c", t=2, s=2)
                    if k == "B":
                        act.activation(qr[:, 2 * j:2 * j + 2, 4 * DH:5 * DH], Jv[:, :, 0, :], ACT.Copy,
                                       scale=cols[:, C_SCALAR + SC_K:C_SCALAR + SC_K + 1])
                        last = act.activation(vt[v % 2], Jv[:, :, 1, :], ACT.Copy,
                                              scale=cols[:, C_SCALAR + SC_V:C_SCALAR + SC_V + 1])
                    else:
                        act.activation(kr[:, 2 * j:2 * j + 2, :], Jv[:, :, 0, :], ACT.Copy, scale=1.0 / WS)
                        last = act.activation(vt[v % 2], Jv[:, :, 1, :], ACT.Copy, scale=1.0 / WS)
                elif k == "T":
                    c = C_HEAD + (0, 0, 4, 4, 2, 6, 6)[j]
                    after(act, t_lo, 7 * m + j - 1 if j >= 2 else 7 * m)
                    if j == 0:
                        act.wait_ge(v_lo, len(V_ORDER) * (m + 1))
                    last = act.activation(ft[j % 2][:], J, ACT.Identity, scale=cols[:, c:c + 1], bias=cols[:, c + 1:c + 2])
                else:
                    after(act, o_read, KINDS * n + j)
                    last = act.activation(R[:], J, ACT.Copy)
                last.then_inc(job_read, 1)

            def exp(n, u):
                L = S if u < SELF_U else SX
                act.wait_ge(shifted, UX * n + u + 1)
                after(act, turned, PIECES * n + piece_end(u - 2))
                kind, qt = u // BT, u % BT
                act.activation(prob[u % 2][:, 0:L], SC[u % 2][:, 0:L], ACT.Exp, scale=SCALE_X,
                               bias=nm[:, u % 4:u % 4 + 1], accum_out=rs[:, kind % 2, qt:qt + 1]).then_inc(exped, 1)

            def parts_hi(n, u):
                pair, q = u // 2, P * (u % 2)
                for j in range(1 if u < SELF_U else 2):
                    piece = piece_end(u - 1) + j
                    act.wait_ge(turned, PIECES * n + piece + 1)
                    after(act, pved, PAIRS * n + pair - 1)
                    act.activation(pth[pair % 2][:, 4 * j:4 * j + 4, q:q + P],
                                   PT[piece % 2].rearrange("p (k c) -> p k c", k=4), ACT.Copy).then_inc(hi, 1)

            for name in NEXT:
                read_job(name, 0, 0, job_number(name, 0, prologue=True))

            def step(g, n, b, first, last):
                for u in range(UX):
                    for slot in (SLOT_A, SLOT_B):
                        name = slot.get(u)
                        if name in jobs_of(first, last) and name[0] != "Y":
                            step_of_r = n - 1 if name == "R3" else n
                            read_job(name, n + 1, 1 - b, job_number(name, n, first, last), step_of_r)
                        if slot is SLOT_A and not (first and u == 0):
                            parts_hi(n if u else n - 1, (u - 1) % UX)
                    exp(n, u)

            def body(g, first, last):
                step(g, 2 * g, 0, first, False)
                step(g, 2 * g + 1, 1, False, last)

            loop(body)(act)
            parts_hi(STEPS - 1, UX - 1)
            read_job("R3", 0, 0, job_number("R2", STEPS - 1, last=True) + 1, STEPS - 1)

        @block.vector
        def _(dve):
            def split_lo(chunk, base, pieces):
                wh, wl = (w1h, w2h, w3h)[chunk - 1], (w1l, w2l, w3l)[chunk - 1]
                for i, (piece, k, c, scale) in enumerate(split_ops(chunk)):
                    if piece in pieces:
                        dve.wait_ge(w_hi, base + i + 1)
                        dve.scalar_tensor_tensor(out=wl[:, k, c], in0=wraw[:, k, c], scalar=scale, in1=wh[:, k, c],
                                                 op0=ALU.mult, op1=ALU.subtract).then_inc(w_lo, 1)

            wait = alone(dve, passed_dve)

            def block_stats(name, m, job):
                k, j = name[0], int(name[1])
                if k == "A":
                    blocks = [(c * BT + j, qr[:, j, DH * c:DH * (c + 1)]) for c in range(KINDS)]
                elif k == "B":
                    blocks = [(4 * BT + t, qr[:, t, 4 * DH:5 * DH]) for t in (2 * j, 2 * j + 1)]
                else:
                    blocks = [(5 * BT + t, kr[:, t, :]) for t in (2 * j, 2 * j + 1)]
                at = BLOCKS * m + sum(4 if x[0] == "A" else 2 for x in NEXT[:NEXT.index(name)])
                dve.wait_ge(job_read, job + 1)
                for i, a in blocks:
                    dve.bn_stats(stats[:, i, :], a).then_inc(s_stats, 1)
                for c, (i, a) in enumerate(blocks):
                    wait(s_stats, at + c + 1)
                    dve.bn_aggr(mv[:, i, :], stats[:, i, :]).then_inc(s_mv, 1)

            def deviations(m):
                dve.wait_ge(s_mv, BLOCKS * (m + 1))
                after(dve, applied, BLOCKS * m)
                rsqrt(dve, s_rsqrt, RSQRT_STEPS * m, mv[:, :, 1], half[:], rstd[:], tmp[:])
                dve.scalar_tensor_tensor(out=shift[:], in0=mv[:, :, 0], scalar=-1.0, in1=rstd[:],
                                         op0=ALU.mult, op1=ALU.mult).then_inc(s_shift, 1)

            def maxima(n, u):
                L, s = (S if u < SELF_U else SX), u % 4
                dve.wait_ge(scored, UX * n + u + 1)
                dve.tensor_reduce(mx[:, s:s + 1], SC[u % 2][:, 0:L], AX.X, ALU.max).then_inc(maxed, 1)
                dve.wait_ge(maxed, UX * n + u + 1)
                dve.tensor_scalar(nm[:, s:s + 1], mx[:, s:s + 1], -SCALE_X, None, ALU.mult).then_inc(shifted, 1)

            def parts_lo(n, u):
                pair, q = u // 2, P * (u % 2)
                for j in range(1 if u < SELF_U else 2):
                    piece = piece_end(u - 1) + j
                    dve.wait_ge(hi, PIECES * n + piece + 1)
                    dve.tensor_tensor(ptl[pair % 2][:, 4 * j:4 * j + 4, q:q + P],
                                      PT[piece % 2].rearrange("p (k c) -> p k c", k=4),
                                      pth[pair % 2][:, 4 * j:4 * j + 4, q:q + P], ALU.subtract).then_inc(lo, 1)

            def reciprocals(n, kind):
                dve.wait_ge(exped, UX * n + BT * (kind + 1))
                dve.reciprocal(ri[:, kind % 2, :], rs[:, kind % 2, :]).then_inc(recip, 1)

            def output(n, kind, r_job):
                count = KINDS * n + kind
                dve.wait_ge(job_read, r_job + 1)
                dve.wait_ge(pved, PAIRS * n + 2 * (kind + 1))
                after(dve, rounded, count)
                dve.scalar_tensor_tensor(out=y[:], in0=O, scalar=rsm[:, kind:kind + 1], in1=R[:], op0=ALU.mult,
                                         op1=ALU.mult).then_inc(o_read, 1)

            def output_round(n, kind):
                count = KINDS * n + kind
                dve.wait_ge(o_read, count + 1)
                round_fp8(dve, rounding, ROUND_STEPS * count, y[:], unit[:], total[:])

            def project_out(t, b, job):
                dve.wait_ge(job_done, job + 1)
                x = X[:, BT * b + t, :]
                dve.scalar_tensor_tensor(out=x, in0=J, scalar=psc[:], in1=x, op0=ALU.mult, op1=ALU.add)\
                    .then_inc(job_read, 1)

            dve.tensor_tensor(psc[:], cols[:, C_SCALAR + SC_PIN:C_SCALAR + SC_PIN + 1],
                              cols[:, C_SCALAR + SC_PW:C_SCALAR + SC_PW + 1], ALU.mult).then_inc(s_psc, 1)
            dve.wait_ge(s_psc, 1)
            split_lo(1, 0, range(KT))
            split_lo(2, W1N, range(KT))
            for name in NEXT:
                if name[0] != "T":
                    block_stats(name, 0, job_number(name, 0, prologue=True))
            deviations(0)

            STATS_AT = {1: ("A0", "A1"), 2: ("A2", "A3"), 3: ("B0",), 4: ("C0", "C1"), 5: ("B1", "C2"), 6: ("C3",)}

            def step(g, n, b, first, last, last_group):
                job = lambda name: job_number(name, n, first, last)
                for u in range(UX):
                    if u == 3 and not first:
                        output(n - 1, 3, job("R3"))
                    if u in (7, 11, 15):
                        output(n, u // 4 - 1, job(f"R{u // 4 - 1}"))
                    maxima(n, u)
                    for slot in (SLOT_A, SLOT_B):
                        name = slot.get(u)
                        if name and name[0] == "Y" and not first:
                            project_out(int(name[1]), 1 - b, job(name))
                        if slot is SLOT_A and not (first and u == 0):
                            parts_lo(n if u else n - 1, (u - 1) % UX)
                    if not last:
                        for name in STATS_AT.get(u, ()):
                            block_stats(name, n + 1, job(name))
                        if u == 7:
                            deviations(n + 1)
                    if u % 4 == 1 and not (first and u == 1):
                        reciprocals(n if u > 1 else n - 1, (u // 4 - 1) % KINDS)
                    if u == 3 and not first:
                        output_round(n - 1, 3)
                    if u == 4 and b == 0:
                        after(dve, o_read, KINDS * n)
                        dve.tensor_copy(rsm[:], rcols[:, bass.ds(C_SMOOTH + KINDS * g, KINDS)]).then_inc(s_rsm, 1)
                        dve.wait_ge(s_rsm, g + 1)
                    if u in (7, 11, 15):
                        output_round(n, u // 4 - 1)
                    if b == 0 and not last_group:
                        if u in (3, 4, 5, 6):
                            split_lo(1, w_base(g), (u - 3,))
                        if u in (9, 10, 11, 12):
                            split_lo(2, w_base(g) + W1N, (u - 9,))
                    if b == 0 and u >= 14:
                        split_lo(3, w_base(g) + (0 if last_group else W1N + W2N), (2 * u - 28, 2 * u - 27))

            def body(g, first, last):
                step(g, 2 * g, 0, first, False, last)
                step(g, 2 * g + 1, 1, False, last, last)

            loop(body)(dve)
            parts_lo(STEPS - 1, UX - 1)
            reciprocals(STEPS - 1, 3)
            r3 = job_number("R2", STEPS - 1, last=True) + 1
            output(STEPS - 1, 3, r3)
            output_round(STEPS - 1, 3)
            for t in range(BT):
                project_out(t, 1, r3 + 1 + t)

        @block.tensor
        def _(pe):
            def run_job(name, m, b, job, g_weights=None):
                k, j = name[0], int(name[1])
                if job_is_not_first(job):
                    pe.wait_ge(job_read, job)
                if k == "A":
                    tok = slice(S * b + P * j, S * b + P * (j + 1))
                    for s in range(2):
                        c = slice(256 * s, 256 * (s + 1))
                        for kt in range(KT):
                            pe.matmul(J[:, c], xq[:, s, kt, tok], w1h[:, kt, c], start=(kt == 0), stop=False)
                            last = pe.matmul(J[:, c], xq[:, s, kt, tok], w1l[:, kt, c], start=False, stop=(kt == KT - 1))
                elif k == "B":
                    for i in range(2):
                        tok = slice(S * b + P * (2 * j + i), S * b + P * (2 * j + i + 1))
                        for s in range(2):
                            o = J[:, 256 * i + DH * s:256 * i + DH * (s + 1)]
                            c = slice(DH * s, DH * (s + 1))
                            for kt in range(KT):
                                pe.matmul(o, xq[:, 2 + s, kt, tok], w2h[:, kt, c], start=(kt == 0), stop=False)
                                last = pe.matmul(o, xq[:, 2 + s, kt, tok], w2l[:, kt, c], start=False,
                                                 stop=(kt == KT - 1))
                elif k == "C":
                    for i in range(2):
                        tok = slice(SX * b + P * (2 * j + i), SX * b + P * (2 * j + i + 1))
                        for kt in range(KT):
                            last = three(pe, J[:, 256 * i:256 * (i + 1)], cxh[:, kt, tok], cxl[:, kt, tok],
                                         w2h[:, kt, 2 * DH:4 * DH], w2l[:, kt, 2 * DH:4 * DH], kt == 0, kt == KT - 1)
                elif k == "T":
                    pe.wait_ge(applied, BLOCKS * m + BT * (j + 1))
                    for t in range(BT):
                        src = qr[:, t, DH * j:DH * (j + 1)] if j < 5 else kr[:, BT * (j - 5) + t, :]
                        last = pe.transpose(J[:, P * t:P * (t + 1)], src, ident[:])
                elif k == "R":
                    pe.wait_ge(recip, KINDS * m + j + 1)
                    for t in range(BT):
                        last = pe.transpose(J[:, P * t:P * (t + 1)], ri[:, j % 2, t:t + 1].broadcast_to([P, P]), ident[:])
                else:
                    pe.wait_ge(rounded, KINDS * (m + 1))
                    for kind in range(KINDS):
                        c = cat[:, kind, P * j:P * (j + 1)]
                        pe.matmul(J, c, w3h[:, kind, :], start=(kind == 0), stop=False)
                        last = pe.matmul(J, c, w3l[:, kind, :], start=False, stop=(kind == KINDS - 1))
                last.then_inc(job_done, 1)

            def job_is_not_first(job):
                return not isinstance(job, int) or job > 0

            def scores(n, u, b):
                kind, qt = u // BT, u % BT
                after(pe, exped, UX * n + u - 1)
                q = slice(P * qt, P * (qt + 1))
                a, c = (kh[b], kl[b]) if u < SELF_U else (kxh[b], kxl[b])
                for j in range(1 if u < SELF_U else 2):
                    r = slice(S * j, S * (j + 1))
                    last = three(pe, SC[u % 2][:, r], qh[b][:, kind, q], ql[b][:, kind, q], a[:, r], c[:, r], True, True)
                last.then_inc(scored, 1)

            def turn(n, u):
                pe.wait_ge(exped, UX * n + u + 1)
                for j in range(1 if u < SELF_U else 2):
                    piece = piece_end(u - 1) + j
                    after(pe, lo, PIECES * n + piece - 1)
                    for k in range(4):
                        last = pe.transpose(PT[piece % 2][:, P * k:P * (k + 1)],
                                            prob[u % 2][:, P * (4 * j + k):P * (4 * j + k + 1)], ident[:])
                    last.then_inc(turned, 1)

            def product(n, u, b):
                pair = u // 2
                if pair == 0:
                    pe.wait_ge(v_lo, len(V_ORDER) * (n + 1))
                if pair % 2 == 0:
                    after(pe, o_read, KINDS * n + pair // 2)
                pe.wait_ge(lo, PIECES * n + piece_end(u))
                h, l, tiles = (vh[b], vl[b], BT) if u < SELF_U else (vxh[b], vxl[b], XT)
                c = slice(2 * P * (pair % 2), 2 * P * (pair % 2 + 1))
                for k in range(tiles):
                    last = three(pe, O[:, c], h[:, k, :], l[:, k, :], pth[pair % 2][:, k, :], ptl[pair % 2][:, k, :],
                                 k == 0, k == tiles - 1)
                last.then_inc(pved, 1)

            pe.wait_ge(w_lo, W1N + W2N)
            for name in NEXT:
                run_job(name, 0, 0, job_number(name, 0, prologue=True))

            def step(g, n, b, first, last):
                for u in range(UX):
                    if u == 0:
                        pe.wait_ge(t_lo, 7 * (n + 1))
                    scores(n, u, b)
                    for slot in (SLOT_A, SLOT_B):
                        name = slot.get(u)
                        if name in jobs_of(first, last):
                            if name[0] in "ABCT":
                                served, sb_ = n + 1, 1 - b
                            else:
                                served = n - 1 if name in LATE else n
                                sb_ = None
                            if b == 1 and name == "A0":
                                pe.wait_ge(w_lo, w_base(g) + W1N)
                            if b == 1 and name == "B0":
                                pe.wait_ge(w_lo, w_base(g) + W1N + W2N)
                            if b == 1 and name == "Y0":
                                pe.wait_ge(w_lo, w_base(g) + (W3N if last else WN))
                            run_job(name, served, sb_, job_number(name, n, first, last))
                        if slot is SLOT_A and not (first and u == 0):
                            turn(n if u else n - 1, (u - 1) % UX)
                    if u % 2 == 1 and not (first and u == 1):
                        product(n if u > 1 else n - 1, (u - 2) % UX, b if u > 1 else 1 - b)

            def body(g, first, last):
                step(g, 2 * g, 0, first, False)
                step(g, 2 * g + 1, 1, False, last)

            loop(body)(pe)
            turn(STEPS - 1, UX - 1)
            product(STEPS - 1, UX - 1, 1)
            r3 = job_number("R2", STEPS - 1, last=True) + 1
            run_job("R3", STEPS - 1, None, r3)
            for t in range(BT):
                run_job(f"Y{t}", STEPS - 1, None, r3 + 1 + t)


E = 8
FF = 1024
FT = FF // P
TOP_P = 0.9


def experts(nc, ins, sem, sb, bank, X, ident, out_d):
    n = norm_tiles(sem, sb, "n3")
    XTh, XTl = sb("eXTh", [P, KT, T], F16), sb("eXTl", [P, KT, T], F16)
    raw = [sb(f"raw_{x}", s, F32) for x, s in (("gate", [P, KT, FF]), ("up", [P, KT, FF]), ("down", [P, FT, D]))]
    wh = [sb(f"ewh_{x}", s, F16) for x, s in (("gate", [P, KT, FF]), ("up", [P, KT, FF]), ("down", [P, FT, D]))]
    wl = [sb(f"ewl_{x}", s, F16) for x, s in (("gate", [P, KT, FF]), ("up", [P, KT, FF]), ("down", [P, FT, D]))]
    sil = [sb(f"sil{i}", [P, S], F32) for i in range(2)]
    h = [sb(f"h{i}", [P, S], F32) for i in range(2)]
    hh = [sb(f"hh{i}", [P, FT, S], F16) for i in range(B)]
    hl = [sb(f"hl{i}", [P, FT, S], F16) for i in range(B)]
    rw, rwh, rwl = sb("rw", [P, KT, E], F32), sb("rwh", [P, KT, E], F16), sb("rwl", [P, KT, E], F16)
    logits, prob, before = (sb(x, [P, NT, E], F32) for x in ("logits", "eprob", "ebefore"))
    larger = sb("larger", [P, E, NT, E], F32)
    weight = sb("weight", [P, E, NT], F32)
    wcol = sb("wcol", [P, NT], F32)
    m8, s8, r8 = (sb(x, [P, NT], F32) for x in ("m8", "s8", "r8"))

    passed_sp, passed_pool = sem("e_passed_sp"), sem("e_passed_pool")
    raw_in = [sem(f"e_raw_in{i}") for i in range(3)]
    w_hi, w_lo = [sem(f"e_w_hi{i}") for i in range(3)], [sem(f"e_w_lo{i}") for i in range(3)]
    rw_in, rw_hi, rw_lo, routed, l_read, route, l_exp = (
        sem(f"e_{x}") for x in ("rw_in", "rw_hi", "rw_lo", "routed", "l_read", "route", "l_exp"))
    gated, upped, silu, made, h_hi, h_lo = (sem(f"e_{x}") for x in ("gated", "upped", "silu", "made", "h_hi", "h_lo"))
    down, added, s_wcol, stored = (sem(f"e_{x}") for x in ("down", "added", "wcol", "stored"))
    HT = B * FT
    PW = KT

    def piece(w, i, k):
        return w[i][:, k, :] if i < 2 else w[i][:, 2 * k:2 * k + 2, :]

    def loop(eng, body):
        body(0)
        with eng.Fori(1, E) as e:
            body(e)

    with nc.Block() as block:
        @block.sync
        def _(sp):
            wait = alone(sp, passed_sp)
            sp.dma_start(rw[:], ins["router"]).then_inc(rw_in, 16)

            def body(e):
                for i in range(3):
                    wait(w_lo[i], PW * e)
                    sp.dma_start(raw[i][:], ins[("gate", "up", "down")[i]][bass.ds(e, 1)]
                                 .rearrange("a p k n -> p (a k) n")).then_inc(raw_in[i], 16)

            loop(sp, body)
            for t in range(NT):
                wait(added, NT * (E - 1) + t + 1)
                sp.dma_start(out_d[t], X[:, t, :]).then_inc(stored, 16)
            wait(stored, 16 * NT)

        @block.gpsimd
        def _(pool):
            wait = alone(pool, passed_pool)
            def body(e):
                for i in range(HT):
                    half, f = i // FT, i % FT
                    wait(made, HT * e + i + 1)
                    if f == 0:
                        wait(down, NT * (e - 1) + BT * (half + 1))
                    pool.tensor_scalar(hh[half][:, f, :], h[i % 2][:], 1.0, 1.0, ALU.mult, ALU.mult).then_inc(h_hi, 1)
                    wait(h_hi, HT * e + i + 1)
                    pool.tensor_tensor(hl[half][:, f, :], h[i % 2][:], hh[half][:, f, :], ALU.subtract).then_inc(h_lo, 1)

            loop(pool, body)

        @block.scalar
        def _(act):
            def split_hi(e, i, k):
                act.wait_ge(raw_in[i], 16 * (e + 1))
                if k == 0:
                    after(act, upped if i < 2 else down, HT * e if i < 2 else NT * e)
                act.activation(piece(wh, i, k), piece(raw, i, k), ACT.Copy, scale=WS).then_inc(w_hi[i], 1)

            norm_scalar(act, n, X, XTh, bank)
            act.wait_ge(rw_in, 16)
            act.activation(rwh[:], rw[:], ACT.Copy, scale=WS).then_inc(rw_hi, 1)
            for i in range(2):
                for k in range(PW):
                    split_hi(0, i, k)
            act.wait_ge(routed, 1)
            act.activation(logits[:], bank[:, 4, 0:NT * E].rearrange("p (t e) -> p t e", t=NT), ACT.Copy, scale=1.0 / WS)\
                .then_inc(l_read, 1)
            act.wait_ge(route, 2)
            act.activation(prob[:], logits[:], ACT.Exp).then_inc(l_exp, 1)

            def body(e):
                for i in range(HT):
                    act.wait_ge(gated, HT * e + i + 1)
                    after(act, made, HT * e + i - 1)
                    act.activation(sil[i % 2][:], bank[:, 2 * (i % 2), :], ACT.Silu, scale=1.0 / WS).then_inc(silu, 1)
                    if 1 <= i <= PW:
                        split_hi(e, 2, i - 1)

            def next_weights(e):
                for i in range(2):
                    for k in range(PW):
                        split_hi(e, i, k)

            body(0)
            with act.Fori(1, E) as e:
                next_weights(e)
                body(e)

        @block.vector
        def _(dve):
            def split_lo(e, i, k):
                dve.wait_ge(w_hi[i], PW * e + k + 1)
                dve.scalar_tensor_tensor(out=piece(wl, i, k), in0=piece(raw, i, k), scalar=WS, in1=piece(wh, i, k),
                                         op0=ALU.mult, op1=ALU.subtract).then_inc(w_lo[i], 1)

            norm_vector(dve, n, X, XTh, XTl, bank, lambda t: None)
            dve.wait_ge(rw_hi, 1)
            dve.scalar_tensor_tensor(out=rwl[:], in0=rw[:], scalar=WS, in1=rwh[:], op0=ALU.mult, op1=ALU.subtract)\
                .then_inc(rw_lo, 1)
            for i in range(2):
                for k in range(PW):
                    split_lo(0, i, k)

            steps = 0

            def step(ins_):
                nonlocal steps
                ins_.then_inc(route, 1)
                steps += 1
                dve.wait_ge(route, steps)

            def wide(a):
                return a.unsqueeze(2).broadcast_to([P, NT, E])

            dve.wait_ge(l_read, 1)
            step(dve.tensor_reduce(m8[:], logits[:], AX.X, ALU.max))
            step(dve.tensor_tensor(logits[:], logits[:], wide(m8[:]), ALU.subtract))
            dve.wait_ge(l_exp, 1)
            step(dve.tensor_reduce(s8[:], prob[:], AX.X, ALU.add))
            step(dve.reciprocal(r8[:], s8[:]))
            step(dve.tensor_tensor(prob[:], prob[:], wide(r8[:]), ALU.mult))
            for e in range(E):
                mine = prob[:, :, e]
                if e:
                    dve.tensor_tensor(larger[:, e, :, 0:e], prob[:, :, 0:e],
                                      mine.unsqueeze(2).broadcast_to([P, NT, e]), ALU.is_ge).then_inc(route, 1)
                    steps += 1
                step(dve.tensor_tensor(larger[:, e, :, e:E], prob[:, :, e:E],
                                       mine.unsqueeze(2).broadcast_to([P, NT, E - e]), ALU.is_gt))
            step(dve.tensor_tensor(larger[:], larger[:], prob[:].unsqueeze(1).broadcast_to([P, E, NT, E]), ALU.mult))
            step(dve.tensor_reduce(before[:].rearrange("p t e -> p (t e)").rearrange("p (e t) -> p e t", e=E),
                                   larger[:], AX.X, ALU.add))
            kept = before[:].rearrange("p t e -> p (t e)").rearrange("p (e t) -> p e t", e=E)
            step(dve.tensor_scalar(kept, kept, TOP_P, 1.0 / WS ** 2, ALU.is_le, ALU.mult))
            step(dve.tensor_tensor(weight[:], kept, prob[:].rearrange("p t e -> p e t"), ALU.mult))

            def body(e):
                for i in range(HT):
                    dve.wait_ge(silu, HT * e + i + 1)
                    dve.wait_ge(upped, HT * e + i + 1)
                    after(dve, h_lo, HT * e + i - 1)
                    dve.tensor_tensor(h[i % 2][:], bank[:, 2 * (i % 2) + 1, :], sil[i % 2][:], ALU.mult).then_inc(made, 1)
                    if 2 <= i < 2 + PW:
                        split_lo(e, 2, i - 2)
                after(dve, added, NT * e)
                dve.tensor_copy(wcol[:], weight[:].rearrange("p e t -> p (e t)")[:, bass.ds(NT * e, NT)])\
                    .then_inc(s_wcol, 1)
                dve.wait_ge(s_wcol, e + 1)

            def add(e, t):
                dve.wait_ge(down, NT * e + t + 1)
                dve.scalar_tensor_tensor(out=X[:, t, :], in0=bank[:, 4 + t % 4, :], scalar=wcol[:, t:t + 1],
                                         in1=X[:, t, :], op0=ALU.mult, op1=ALU.add).then_inc(added, 1)

            body(0)
            with dve.Fori(1, E) as e:
                for i in range(2):
                    for k in range(PW):
                        split_lo(e, i, k)
                        add(e - 1, PW * i + k)
                body(e)
            for t in range(NT):
                add(E - 1, t)

        @block.tensor
        def _(pe):
            norm_tensor(pe, n, bank, ident)
            pe.wait_ge(rw_lo, 1)
            pe.wait_ge(n.s_lo, NT)
            for t in range(NT):
                for k in range(KT):
                    tok = slice(P * t, P * (t + 1))
                    last = three(pe, bank[:, 4, E * t:E * (t + 1)], XTh[:, k, tok], XTl[:, k, tok], rwh[:, k, :],
                                 rwl[:, k, :], k == 0, k == KT - 1)
            last.then_inc(routed, 1)

            def body(e):
                pe.wait_ge(w_lo[0], PW * (e + 1))
                pe.wait_ge(w_lo[1], PW * (e + 1))
                for i in range(HT):
                    half, f = i // FT, i % FT
                    after(pe, made, HT * e + i - 1)
                    for w, done in ((0, gated), (1, upped)):
                        for k in range(KT):
                            c = slice(P * f, P * (f + 1))
                            tok = slice(S * half, S * (half + 1))
                            last = three(pe, bank[:, 2 * (i % 2) + w, :], wh[w][:, k, c], wl[w][:, k, c],
                                         XTh[:, k, tok], XTl[:, k, tok], k == 0, k == KT - 1)
                        last.then_inc(done, 1)
                pe.wait_ge(w_lo[2], PW * (e + 1))
                for t in range(NT):
                    half = t // BT
                    if t % BT == 0:
                        pe.wait_ge(h_lo, HT * e + FT * (half + 1))
                    after(pe, added, NT * e + t - 3)
                    if isinstance(e, int) and e == 0 and t == 0:
                        pe.wait_ge(l_read, 1)
                    tok = slice(P * (t % BT), P * (t % BT + 1))
                    for f in range(FT):
                        last = three(pe, bank[:, 4 + t % 4, :], hh[half][:, f, tok], hl[half][:, f, tok],
                                     wh[2][:, f, :], wl[2][:, f, :], f == 0, f == FT - 1)
                    last.then_inc(down, 1)

            loop(pe, body)


def pack(x):
    c = np.ascontiguousarray
    rows = lambda w: w.reshape(-1, P, w.shape[-1]).transpose(1, 0, 2)
    wq, wk, wv = np.split(x["L0_attn_w_qkv"].T, 3, axis=1)
    bq, bk, bv = np.split(x["L0_attn_b_qkv"], 3)
    quad = lambda w: w.reshape(D, QUADS, P)
    per_part = lambda v: v.reshape(-1, P).T
    a = {
        "x": x["x"].reshape(T, D),
        "cols": cols(x),
        "w_qkv": np.stack([rows(np.concatenate([quad(w)[:, i] for w in (wq, wk, wv)], axis=1)) for i in range(QUADS)]),
        "b_qk": np.stack([np.stack([bq[P * i:P * (i + 1)], bk[P * i:P * (i + 1)]], axis=1) for i in range(QUADS)]),
        "b_v": np.stack([np.broadcast_to(bv[P * i:P * (i + 1)], (P, P)) for i in range(QUADS)]),
        "w_out": x["L0_attn_w_out"].T.reshape(QUADS, P, D),
        "bout": np.broadcast_to(x["L0_attn_b_out"], (P, D)),
    }
    xa = lambda name: x["L0_xattn_" + name]
    heads = lambda w: w.T.reshape(D, GROUPS, -1)
    wkx, wvx = np.split(xa("w_kv_x"), 2)
    wp = xa("wproj").T.reshape(2, GROUPS, HPG * DH, D)
    one = [np.concatenate([heads(xa(n)) for n in ("wq", "wqx")], axis=2),
           np.concatenate([heads(w) for w in (xa("wk"), xa("wv"), wkx, wvx)], axis=2)]
    a["w_group"] = np.stack([np.stack([rows(one[0][:, g]), rows(one[1][:, g]),
                                       rows(wp[:, g].reshape(KINDS * DH, D))]) for g in range(GROUPS)])
    for name in ("gate", "up", "down"):
        a[name] = np.stack([rows(w.T) for w in x["L0_ffn_" + name + "_w"]])
    a["router"] = rows(x["L0_ffn_router_w"].T)
    a["ctx"] = x["ctx_2048"].transpose(2, 0, 1).reshape(KT, P, B * SX)
    return {k: c(v) for k, v in a.items()}


def cols(x):
    xa = lambda name: x["L0_xattn_" + name]
    per_part = lambda v: v.reshape(-1, P).T
    smooth = xa("proj_smooth").reshape(2, GROUPS, HPG, P).transpose(3, 1, 0, 2).reshape(P, GROUPS * KINDS)
    return np.concatenate(
        [per_part(xa("ln_w")), per_part(xa("ln_b"))]
        + [per_part(xa(n + "_in_scale")) for n in ("q", "qx", "k", "v")]
        + [per_part(xa(n)) for h in ("qln", "kln", "qxln", "kxln") for n in (h + "_w", h + "_b")]
        + [smooth]
        + [np.broadcast_to(xa(n).reshape(1, 1), (P, 1))
           for n in ("wq_scale", "wqx_scale", "wk_scale", "wv_scale", "proj_in_scale", "proj_w_scale")], axis=1)


def kernel(**inputs):
    import concourse.bacc as bacc
    from concourse.bass_utils import run_bass_kernel_spmd

    nc = bacc.Bacc("TRN2", target_bir_lowering=False, num_devices=1)
    arrays, args = {}, {}
    for name, a in pack({k: np.asarray(v) for k, v in inputs.items()}).items():
        arrays[f"in_{name}"] = a
        args[name] = nc.dram_tensor(f"in_{name}", a.shape, mybir.dt.from_np(a.dtype), kind="ExternalInput").ap()
    out = nc.dram_tensor("out", (B, S, D), F32, kind="ExternalOutput").ap()
    build(nc, args, out)
    r = run_bass_kernel_spmd(nc, [arrays], core_ids=[0])
    return r.results[0]["out"]
```

```python
from contextlib import ExitStack

import numpy as np
import concourse.bass as bass
from concourse import mybir

ALU = mybir.AluOpType
ACT = mybir.ActivationFunctionType
AX = mybir.AxisListType
F32 = mybir.dt.float32
F16 = mybir.dt.float16
BF16 = mybir.dt.bfloat16
I32 = mybir.dt.int32
U16 = mybir.dt.uint16

P = 128
B, S, D = 2, 512, 512
T = B * S
NT = T // P
BT = S // P
KT = D // P
WS = 64.0
EPS = 1e-5
RSQRT_SEED = float(0x5F3759DF)
NEWTON = 3
RSQRT_STEPS = 3 + 3 * NEWTON

HD = 32
QUADS = 4
HQ = 4
SCALE_A = 1.0 / float(np.sqrt(HD))
UA = HQ * BT
TURN, PARTS, PV = 2, 3, 4
SLOT_Q, SLOT_K, SLOT_T, SLOT_V, SLOT_Y = (0, 1), (2, 3), 5, (6, 7), (9, 10, 11, 12)


def rsqrt(dve, sem, base, var, half, out, tmp):
    k = 0

    def step(ins):
        nonlocal k
        ins.then_inc(sem, 1)
        k += 1
        dve.wait_ge(sem, base + k)

    step(dve.tensor_scalar(half, var, EPS, None, ALU.add))
    step(dve.tensor_scalar(tmp.bitcast(I32), half.bitcast(I32), 1, None, ALU.arith_shift_right))
    step(dve.tensor_scalar(out.bitcast(I32), tmp.bitcast(I32), -1.0, RSQRT_SEED, ALU.mult, ALU.add))
    for _ in range(NEWTON):
        step(dve.tensor_tensor(tmp, out, out, ALU.mult))
        step(dve.scalar_tensor_tensor(out=tmp, in0=tmp, scalar=-0.5, in1=half, op0=ALU.mult, op1=ALU.mult))
        step(dve.scalar_tensor_tensor(out=out, in0=tmp, scalar=1.5, in1=out, op0=ALU.add, op1=ALU.mult))
    assert k == RSQRT_STEPS


def after(eng, sem, count):
    if not isinstance(count, int) or count > 0:
        eng.wait_ge(sem, count)


def alone(eng, passed):
    def wait(sem, count):
        after(eng, sem, count)
        if not isinstance(count, int):
            eng.sem_inc(passed)
    return wait


def build(nc, ins, out):
    x_d = ins["x"].rearrange("(t p) d -> t p d", p=P)
    out_d = out.rearrange("b (t p) d -> (b t) p d", p=P)
    top = ExitStack()

    def sem(name):
        return top.enter_context(nc.semaphore(name))

    def sbuf(ctx, name, shape, dt):
        return ctx.enter_context(nc.sbuf_tensor(name, shape, dt))

    with top:
        bank = top.enter_context(nc.psum_tensor("bank", [P, 8, 512], F32))
        X = sbuf(top, "X", [P, NT, D], F32)
        ident = sbuf(top, "ident", [P, P], F32)
        cols = sbuf(top, "cols", [P, ins["cols"].shape[1]], F32)

        with ExitStack() as ctx:
            XTh = sbuf(ctx, "XTh", [P, KT, T], F16)
            XTl = sbuf(ctx, "XTl", [P, KT, T], F16)
            with ExitStack() as c2:
                first_norm(nc, ins, sem, lambda n, s, d: sbuf(c2, n, s, d), bank, X, ident, cols, XTh, XTl, x_d)
            with ExitStack() as c2:
                causal_attention(nc, ins, sem, lambda n, s, d: sbuf(c2, n, s, d), bank, X, ident, XTh, XTl)
        with ExitStack() as ctx:
            rcols = sbuf(ctx, "rcols", [P, COLS], F32)
            xq = sbuf(ctx, "xq", [P, 4, KT, T], F16)
            cxh = sbuf(ctx, "cxh", [P, KT, B * SX], F16)
            cxl = sbuf(ctx, "cxl", [P, KT, B * SX], F16)
            with ExitStack() as c2:
                second_norm(nc, ins, sem, lambda n, s, d: sbuf(c2, n, s, d), bank, X, ident, cols, xq, cxh, cxl, rcols)
            with ExitStack() as c2:
                group_attention(nc, ins, sem, lambda n, s, d: sbuf(c2, n, s, d), bank, X, ident, cols, rcols, xq, cxh,
                                cxl)
        with ExitStack() as ctx:
            experts(nc, ins, sem, lambda n, s, d: sbuf(ctx, n, s, d), bank, X, ident, out_d)


def first_norm(nc, ins, sem, sb, bank, X, ident, cols, XTh, XTl, x_d):
    x_in = [sem(f"x_in{t}") for t in range(NT)]
    cols_in = sem("cols_in")
    id_set = sem("id_set")
    tiles = norm_tiles(sem, sb, "n1")
    with nc.Block() as block:
        @block.sync
        def _(sp):
            for t in range(NT):
                sp.dma_start(X[:, t, :], x_d[t]).then_inc(x_in[t], 16)
            sp.dma_start(cols[:], ins["cols"]).then_inc(cols_in, 16)
            sp.wait_ge(cols_in, 16)

        @block.gpsimd
        def _(pool):
            pool.memset(ident[:], 0.0).then_inc(id_set, 1)
            pool.wait_ge(id_set, 1)
            pool.affine_select(out=ident[:], in_=ident[:], compare_op=ALU.not_equal, fill=1.0, base=0,
                               pattern=[[-1, P]], channel_multiplier=1).then_inc(id_set, 1)

        @block.vector
        def _(dve):
            norm_vector(dve, tiles, X, XTh, XTl, bank, lambda t: dve.wait_ge(x_in[t], 16))

        @block.scalar
        def _(act):
            norm_scalar(act, tiles, X, XTh, bank)

        @block.tensor
        def _(pe):
            pe.wait_ge(id_set, 2)
            norm_tensor(pe, tiles, bank, ident)


class norm_tiles:

    def __init__(self, sem, sb, tag):
        self.stats = sb(f"stats_{tag}", [P, NT, 6], F32)
        self.mv = sb(f"mv_{tag}", [P, NT, 2], F32)
        self.half = sb(f"half_{tag}", [P, NT], F32)
        self.tmp = sb(f"tmp_{tag}", [P, NT], F32)
        self.rstd = sb(f"rstd_{tag}", [P, NT], F32)
        self.shift = sb(f"shift_{tag}", [P, NT], F32)
        self.xn = sb(f"xn_{tag}", [P, NT, D], F32)
        self.s_stats = sem(f"{tag}_stats")
        self.s_mv = sem(f"{tag}_mv")
        self.s_rsqrt = sem(f"{tag}_rsqrt")
        self.s_shift = sem(f"{tag}_shift")
        self.s_xn = sem(f"{tag}_xn")
        self.s_turned = sem(f"{tag}_turned")
        self.s_hi = sem(f"{tag}_hi")
        self.s_lo = sem(f"{tag}_lo")


def norm_stats(dve, n, src, arrived, base=0):
    for t in range(NT):
        arrived(t)
        dve.bn_stats(n.stats[:, t, :], src[:, t, :]).then_inc(n.s_stats, 1)
    for t in range(NT):
        dve.wait_ge(n.s_stats, NT * base + t + 1)
        dve.bn_aggr(n.mv[:, t, :], n.stats[:, t, :]).then_inc(n.s_mv, 1)
    dve.wait_ge(n.s_mv, NT * (base + 1))
    rsqrt(dve, n.s_rsqrt, RSQRT_STEPS * base, n.mv[:, :, 1], n.half[:], n.rstd[:], n.tmp[:])
    dve.scalar_tensor_tensor(out=n.shift[:], in0=n.mv[:, :, 0], scalar=-1.0, in1=n.rstd[:],
                             op0=ALU.mult, op1=ALU.mult).then_inc(n.s_shift, 1)


def norm_vector(dve, n, X, XTh, XTl, bank, arrived):
    norm_stats(dve, n, X, arrived)
    for t in range(NT):
        dve.wait_ge(n.s_hi, t + 1)
        dve.tensor_tensor(XTl[:, :, t * P:(t + 1) * P], bank[:, t % 2, :].rearrange("p (k c) -> p k c", k=KT),
                          XTh[:, :, t * P:(t + 1) * P], ALU.subtract).then_inc(n.s_lo, 1)


def norm_scalar(act, n, X, XTh, bank):
    act.wait_ge(n.s_shift, 1)
    for t in range(NT):
        act.activation(n.xn[:, t, :], X[:, t, :], ACT.Identity, scale=n.rstd[:, t:t + 1],
                       bias=n.shift[:, t:t + 1]).then_inc(n.s_xn, 1)
    for t in range(NT):
        act.wait_ge(n.s_turned, t + 1)
        act.activation(XTh[:, :, t * P:(t + 1) * P], bank[:, t % 2, :].rearrange("p (k c) -> p k c", k=KT),
                       ACT.Copy).then_inc(n.s_hi, 1)


def norm_tensor(pe, n, bank, ident):
    for t in range(NT):
        pe.wait_ge(n.s_xn, t + 1)
        if t >= 2:
            pe.wait_ge(n.s_lo, t - 1)
        for k in range(KT):
            ins = pe.transpose(bank[:, t % 2, k * P:(k + 1) * P], n.xn[:, t, k * P:(k + 1) * P], ident[:])
        ins.then_inc(n.s_turned, 1)


def three(pe, ps, ah, al, bh, bl, start, stop):
    pe.matmul(ps, ah, bh, start=start, stop=False)
    pe.matmul(ps, al, bh, start=False, stop=False)
    return pe.matmul(ps, ah, bl, start=False, stop=stop)


def causal_attention(nc, ins, sem, sb, bank, X, ident, XTh, XTl):
    STEPS = QUADS * B
    NQ = 3 * P
    wraw = sb("wraw", [P, KT, NQ], F32)
    woraw = sb("woraw", [P, D], F32)
    wh, wl = sb("wh", [P, KT, NQ], F16), sb("wl", [P, KT, NQ], F16)
    woh, wol = sb("woh", [P, D], F16), sb("wol", [P, D], F16)
    qkb = sb("qkb", [P, 2], F32)
    vb = sb("vb", [P, P], F32)
    bout = sb("bout", [P, D], F32)
    identb, mask = sb("identb", [P, P], BF16), sb("mask", [P, P], BF16)
    qf, kf, vf, af = (sb(x, [P, S], F32) for x in ("qf", "kf", "vf", "af"))
    qh, ql, kh, kl = ([sb(f"{x}{b}", [P, S], F16) for b in range(B)] for x in ("qh", "ql", "kh", "kl"))
    vh = [sb(f"vh{b}", [P, BT, P], F16) for b in range(B)]
    vl = [sb(f"vl{b}", [P, BT, P], F16) for b in range(B)]
    ao = [sb(f"ao{b}", [P, BT, P], F32) for b in range(B)]
    aoh, aol = sb("aoh", [P, S], F16), sb("aol", [P, S], F16)
    prob = [sb(f"prob{i}", [P, S], F32) for i in range(4)]
    pth = [sb(f"pth{i}", [P, S], F16) for i in range(4)]
    ptl = [sb(f"ptl{i}", [P, S], F16) for i in range(4)]
    nm, rs, ri = (sb(x, [P, UA], F32) for x in ("nm", "rs", "ri"))
    qbias = sb("qbias", [P, 1], F32)
    J_Q, J_K, J_T, J_V, J_Y = 1, 0, 1, 0, (1, 0, 1, 0)
    SC, PT, O, J = ([bank[:, i, :], bank[:, i + 1, :]] for i in (0, 2, 4, 6))

    passed_sp, passed_pool = sem("a_passed_sp"), sem("a_passed_pool")
    w_in, wo_in, b_in, c_in = sem("a_w_in"), sem("a_wo_in"), sem("a_b_in"), sem("a_c_in")
    set_up = sem("a_set_up")
    w_hi, w_lo, wo_hi, wo_lo = sem("a_w_hi"), sem("a_w_lo"), sem("a_wo_hi"), sem("a_wo_lo")
    q_ps, k_ps, v_ps, t_ps, y_ps = (sem(f"a_{x}_ps") for x in ("q", "k", "v", "t", "y"))
    q_f, k_f, v_f, t_f, y_f = (sem(f"a_{x}_f") for x in ("q", "k", "v", "t", "y"))
    q_h, k_h, v_h, t_h = (sem(f"a_{x}_h") for x in ("q", "k", "v", "t"))
    q_l, k_l, v_l, t_l = (sem(f"a_{x}_l") for x in ("q", "k", "v", "t"))
    bias_x, q_bias = sem("a_bias_x"), sem("a_q_bias")
    scored, maxed, exped, turned, hi, lo, pved, recip, o_f = (
        sem(f"a_{x}") for x in ("scored", "maxed", "exped", "turned", "hi", "lo", "pved", "recip", "o_f"))

    def loop(eng, body):
        body(0, first=True, last=False)
        with eng.Fori(1, QUADS - 1) as i:
            body(i, first=False, last=False)
        body(QUADS - 1, first=False, last=True)

    with nc.Block() as block:
        @block.sync
        def _(sp):
            wait = alone(sp, passed_sp)
            sp.dma_start(bout[:], ins["bout"]).then_inc(c_in, 16)

            def load_w(i, used):
                if used:
                    wait(w_lo, i)
                    wait(v_f, 2 * i)
                    wait(k_f, 2 * i)
                    wait(q_f, 2 * i)
                sp.dma_start(wraw[:], ins["w_qkv"][bass.ds(i, 1)].rearrange("a p k n -> p (a k) n")).then_inc(w_in, 16)
                sp.dma_start(qkb[:], ins["b_qk"][bass.ds(i, 1)].rearrange("a p n -> p (a n)")).then_inc(b_in, 16)
                sp.dma_start(vb[:], ins["b_v"][bass.ds(i, 1)].rearrange("a p n -> p (a n)")).then_inc(b_in, 16)

            def load_wo(i, used):
                if used:
                    wait(wo_lo, i)
                sp.dma_start(woraw[:], ins["w_out"][bass.ds(i, 1)].rearrange("a p n -> p (a n)")).then_inc(wo_in, 16)

            load_w(0, False)
            load_wo(0, False)

            def body(i, first, last):
                if not last:
                    load_w(i + 1, True)
                    load_wo(i + 1, True)

            loop(sp, body)

        @block.gpsimd
        def _(pool):
            wait = alone(pool, passed_pool)
            pool.memset(identb[:], 0.0).then_inc(set_up, 1)
            pool.memset(mask[:], 0.0).then_inc(set_up, 1)
            pool.wait_ge(set_up, 2)
            pool.affine_select(out=identb[:], in_=identb[:], compare_op=ALU.not_equal, fill=1.0, base=0,
                               pattern=[[-1, P]], channel_multiplier=1).then_inc(set_up, 1)
            pool.affine_select(out=mask[:], in_=mask[:], compare_op=ALU.is_ge, fill=-1e30, base=0,
                               pattern=[[-1, P]], channel_multiplier=1).then_inc(set_up, 1)

            def cast(dst, src, scale, done):
                pool.tensor_scalar(dst, src, scale, 1.0, ALU.mult, ALU.mult).then_inc(done, 1)

            def weights(i, used):
                wait(w_in, 16 * (i + 1))
                if used:
                    wait(v_ps, 2 * i)
                cast(wh[:], wraw[:], WS, w_hi)

            def out_weights(i, used):
                wait(wo_in, 16 * (i + 1))
                if used:
                    wait(y_ps, 4 * 2 * i)
                cast(woh[:], woraw[:], WS, wo_hi)

            def split(n, used, ready, src, h, l, h_done, l_done, free, free_at):
                wait(ready, n + 1)
                if used:
                    wait(free, free_at)
                cast(h, src[:], 1.0, h_done)
                wait(h_done, n + 1)
                pool.tensor_tensor(l, src[:], h, ALU.subtract).then_inc(l_done, 1)

            def project(n, b, used):
                split(n, used, q_f, qf, qh[b][:], ql[b][:], q_h, q_l, scored, UA * (n - 1))
                split(n, used, k_f, kf, kh[b][:], kl[b][:], k_h, k_l, scored, UA * (n - 1))

            def values(n, b, used):
                vhf, vlf = (x[b][:].rearrange("p k c -> p (k c)") for x in (vh, vl))
                split(n, used, v_f, vf, vhf, vlf, v_h, v_l, pved, UA * (n - 1))

            def outputs(n, used):
                split(n, used, t_f, af, aoh[:], aol[:], t_h, t_l, y_ps, 4 * n)

            weights(0, False)
            out_weights(0, False)
            project(0, 0, False)
            values(0, 0, False)

            def body(i, first, last):
                project(2 * i + 1, 1, not first)
                if not first:
                    outputs(2 * i - 1, True)
                values(2 * i + 1, 1, not first)
                if not last:
                    weights(i + 1, True)
                if not first:
                    out_weights(i, True)
                if not last:
                    project(2 * i + 2, 0, True)
                outputs(2 * i, not first)
                if not last:
                    values(2 * i + 2, 0, True)

            loop(pool, body)
            outputs(STEPS - 1, True)

        @block.scalar
        def _(act):
            def projected(n, used, ready, j, dst, scale, bias, done, l_done):
                act.wait_ge(ready, n + 1)
                if used:
                    act.wait_ge(l_done, n)
                act.activation(dst[:], J[j], ACT.Identity, scale=scale, bias=bias).then_inc(done, 1)

            def project_q(n, nq, used):
                act.wait_ge(b_in, 32 * (nq + 1))
                act.activation(qbias[:], qkb[:, 0:1], ACT.Copy, scale=SCALE_A).then_inc(q_bias, 1)
                act.wait_ge(q_bias, n + 1)
                projected(n, used, q_ps, J_Q, qf, SCALE_A / WS, qbias[:], q_f, q_l)

            def project_k(n, used):
                projected(n, used, k_ps, J_K, kf, 1.0 / WS, qkb[:, 1:2], k_f, k_l)

            def out_turned(n, used):
                act.wait_ge(t_ps, n + 1)
                if used:
                    act.wait_ge(t_l, n)
                act.activation(af[:], J[J_T], ACT.Copy).then_inc(t_f, 1)

            def exp(U, u, used):
                L = P * (u % BT + 1)
                act.wait_ge(maxed, U + 1)
                if used:
                    act.wait_ge(turned, U - 3)
                act.activation(prob[u % 4][:, 0:L], SC[u % 2][:, 0:L], ACT.Exp, bias=nm[:, u:u + 1],
                               accum_out=rs[:, u:u + 1]).then_inc(exped, 1)

            def part_hi(U, u, used):
                L = P * (u % BT + 1)
                act.wait_ge(turned, U + 1)
                if used:
                    act.wait_ge(pved, U - 3)
                act.activation(pth[u % 4][:, 0:L], PT[u % 2][:, 0:L], ACT.Copy).then_inc(hi, 1)

            project_q(0, 0, False)
            project_k(0, False)

            def body(i, first, last):
                step(i, 2 * i, first, False, first)
                step(i + 1, 2 * i + 1, False, last, first)

            def step(nq, n, first, last, first_quad):
                for u in range(UA):
                    U = UA * n + u
                    if not (first and u < PARTS):
                        part_hi(U - PARTS, u - PARTS, not (first and u - PARTS < 4))
                    exp(U, u, not (first and u < 4))
                    if u == SLOT_Q[-1] and not last:
                        project_q(n + 1, nq, True)
                    if u == SLOT_K[-1] and not last:
                        project_k(n + 1, True)
                    if u == SLOT_T and not first:
                        out_turned(n - 1, not first_quad)

            loop(act, body)
            end = UA * STEPS
            for U in range(end - PARTS, end):
                part_hi(U, U % UA, True)
            out_turned(STEPS - 1, True)

        @block.vector
        def _(dve):
            dve.wait_ge(c_in, 16)
            for t in range(NT):
                dve.tensor_tensor(X[:, t, :], X[:, t, :], bout[:], ALU.add).then_inc(bias_x, 1)

            def low(dst, raw, h, h_done, l_done, i):
                dve.wait_ge(h_done, i + 1)
                dve.scalar_tensor_tensor(out=dst[:], in0=raw[:], scalar=WS, in1=h[:], op0=ALU.mult,
                                         op1=ALU.subtract).then_inc(l_done, 1)

            def values(n, used, nq):
                dve.wait_ge(v_ps, n + 1)
                dve.wait_ge(b_in, 32 * (nq + 1))
                if used:
                    dve.wait_ge(v_l, n)
                dve.scalar_tensor_tensor(out=vf[:].rearrange("p (k c) -> p k c", k=BT),
                                         in0=J[J_V].rearrange("p (k c) -> p k c", k=BT), scalar=1.0 / WS,
                                         in1=vb[:].unsqueeze(1).broadcast_to([P, BT, P]),
                                         op0=ALU.mult, op1=ALU.add).then_inc(v_f, 1)

            def maxima(U, u):
                dve.wait_ge(scored, U + 1)
                dve.tensor_reduce(nm[:, u:u + 1], SC[u % 2][:, 0:P * (u % BT + 1)], AX.X, ALU.max,
                                  negate=True).then_inc(maxed, 1)

            def part_lo(U, u):
                L = P * (u % BT + 1)
                dve.wait_ge(hi, U + 1)
                dve.tensor_tensor(ptl[u % 4][:, 0:L], PT[u % 2][:, 0:L], pth[u % 4][:, 0:L],
                                  ALU.subtract).then_inc(lo, 1)

            def normalise(n, b, h, used):
                mine = slice(BT * h, BT * (h + 1))
                dve.wait_ge(exped, UA * n + BT * (h + 1))
                dve.reciprocal(ri[:, mine], rs[:, mine]).then_inc(recip, 1)
                dve.wait_ge(recip, HQ * n + h + 1)
                dve.wait_ge(pved, UA * n + BT * (h + 1))
                if used and h == 0:
                    dve.wait_ge(t_ps, n - 1)
                dve.tensor_tensor(ao[b][:, :, h * HD:(h + 1) * HD],
                                  O[h % 2][:, 0:BT * HD].rearrange("p (t c) -> p t c", t=BT),
                                  ri[:, mine].unsqueeze(2).broadcast_to([P, BT, HD]), ALU.mult).then_inc(o_f, 1)

            def project_out(n, t, b):
                dve.wait_ge(y_ps, 4 * n + t + 1)
                if isinstance(n, int) and n < 2 and t == 0:
                    dve.wait_ge(bias_x, NT)
                dve.scalar_tensor_tensor(out=X[:, BT * b + t, :], in0=J[J_Y[t]], scalar=1.0 / WS,
                                         in1=X[:, BT * b + t, :], op0=ALU.mult, op1=ALU.add).then_inc(y_f, 1)

            low(wl, wraw, wh, w_hi, w_lo, 0)
            low(wol, woraw, woh, wo_hi, wo_lo, 0)
            values(0, False, 0)

            def step(i, n, b, first, last, first_quad, last_quad):
                for u in range(UA):
                    U = UA * n + u
                    maxima(U, u)
                    if not (first and u < PARTS):
                        part_lo(U - PARTS, u - PARTS)
                    if u % BT == (PV + 1) % BT:
                        h = (u - PV - 1) // BT - 1
                        if h >= 0:
                            normalise(n, b, h, not first_quad)
                        elif not first:
                            normalise(n - 1, 1 - b, h + HQ, not first_quad)
                    if u in SLOT_Y and not first:
                        project_out(n - 1, SLOT_Y.index(u), 1 - b)
                    if u == SLOT_V[-1] and not last:
                        values(n + 1, True, i + b)
                    if u == UA - 2 and b == 0 and not last_quad:
                        low(wl, wraw, wh, w_hi, w_lo, i + 1)
                    if u == UA - 1 and b == 0 and not first:
                        low(wol, woraw, woh, wo_hi, wo_lo, i)

            def body(i, first, last):
                step(i, 2 * i, 0, first, False, first, last)
                step(i, 2 * i + 1, 1, False, last, first, last)

            loop(dve, body)
            end = UA * STEPS
            for U in range(end - PARTS, end):
                part_lo(U, U % UA)
            for h in range(HQ - 2, HQ):
                normalise(STEPS - 1, 1, h, True)
            for t in range(BT):
                project_out(STEPS - 1, t, 1)

        @block.tensor
        def _(pe):
            def projection(b, j, first_col, done, part=(0, 1)):
                for k in range(KT):
                    if k // (KT // 2) not in part:
                        continue
                    w = slice(first_col, first_col + P)
                    ins_ = three(pe, J[j], wh[:, k, w], wl[:, k, w], XTh[:, k, S * b:S * (b + 1)],
                                 XTl[:, k, S * b:S * (b + 1)], k == 0, k == KT - 1)
                    if k == KT - 1:
                        ins_.then_inc(done, 1)

            def values(b, part=(0, 1)):
                for t in range(BT):
                    if t // (BT // 2) not in part:
                        continue
                    tok = slice(S * b + P * t, S * b + P * (t + 1))
                    for k in range(KT):
                        ins_ = three(pe, J[J_V][:, P * t:P * (t + 1)], XTh[:, k, tok], XTl[:, k, tok],
                                     wh[:, k, 2 * P:3 * P], wl[:, k, 2 * P:3 * P], k == 0, k == KT - 1)
                    if t == BT - 1:
                        ins_.then_inc(v_ps, 1)

            def scores(n, U, u, b, used):
                h, qt = u // BT, u % BT
                L = P * (qt + 1)
                if u == 0:
                    pe.wait_ge(q_l, n + 1)
                    pe.wait_ge(k_l, n + 1)
                if used:
                    pe.wait_ge(exped, U - 1)
                head = slice(HD * h, HD * (h + 1))
                q = slice(P * qt, P * (qt + 1))
                three(pe, SC[u % 2][:, 0:L], qh[b][head, q], ql[b][head, q], kh[b][head, 0:L], kl[b][head, 0:L],
                      True, False)
                pe.matmul(SC[u % 2][:, L - P:L], identb[:], mask[:], start=False, stop=True).then_inc(scored, 1)

            def turn(U, u, used):
                pe.wait_ge(exped, U + 1)
                if used:
                    pe.wait_ge(lo, U - 1)
                for k in range(u % BT + 1):
                    ins_ = pe.transpose(PT[u % 2][:, P * k:P * (k + 1)], prob[u % 4][:, P * k:P * (k + 1)], ident[:])
                ins_.then_inc(turned, 1)

            def pv(n, U, u, b, used):
                u = u % UA
                h, qt = u // BT, u % BT
                if u == 0:
                    pe.wait_ge(v_l, n + 1)
                pe.wait_ge(lo, U + 1)
                if used and qt == 0:
                    pe.wait_ge(o_f, HQ * n + h - 1)
                for k in range(qt + 1):
                    ins_ = three(pe, O[h % 2][:, HD * qt:HD * (qt + 1)], pth[u % 4][:, P * k:P * (k + 1)],
                                 ptl[u % 4][:, P * k:P * (k + 1)], vh[b][:, k, HD * h:HD * (h + 1)],
                                 vl[b][:, k, HD * h:HD * (h + 1)], k == 0, k == qt)
                ins_.then_inc(pved, 1)

            def turn_out(n, b):
                pe.wait_ge(o_f, HQ * (n + 1))
                for t in range(BT):
                    ins_ = pe.transpose(J[J_T][:, P * t:P * (t + 1)], ao[b][:, t, :], ident[:])
                ins_.then_inc(t_ps, 1)

            def project_out(n, t):
                if t == 0:
                    pe.wait_ge(t_l, n + 1)
                tok = slice(P * t, P * (t + 1))
                three(pe, J[J_Y[t]], aoh[:, tok], aol[:, tok], woh[:], wol[:], True, True).then_inc(y_ps, 1)

            pe.wait_ge(set_up, 4)
            pe.wait_ge(w_lo, 1)
            projection(0, J_Q, 0, q_ps)
            projection(0, J_K, P, k_ps)
            pe.wait_ge(k_f, 1)
            values(0)

            def job(i, n, u, b, first, second, last):
                if u in SLOT_Q and not last:
                    if u == SLOT_Q[0]:
                        if b == 1:
                            pe.wait_ge(w_lo, i + 2)
                        pe.wait_ge(q_f, n + 1)
                        if not (first or second):
                            pe.wait_ge(y_f, 4 * (n - 2) + 3)
                    projection(1 - b, J_Q, 0, q_ps, (SLOT_Q.index(u),))
                if u in SLOT_K and not last:
                    if u == SLOT_K[0]:
                        pe.wait_ge(v_f, n + 1)
                        if not (first or second):
                            pe.wait_ge(y_f, 4 * (n - 1))
                    projection(1 - b, J_K, P, k_ps, (SLOT_K.index(u),))
                if u == SLOT_T and not first:
                    if not last:
                        pe.wait_ge(q_f, n + 2)
                    else:
                        pe.wait_ge(y_f, 4 * (n - 2) + 3)
                    turn_out(n - 1, 1 - b)
                if u in SLOT_V and not last:
                    if u == SLOT_V[0]:
                        pe.wait_ge(k_f, n + 2)
                    values(1 - b, (SLOT_V.index(u),))
                if u in SLOT_Y and not first:
                    t = SLOT_Y.index(u)
                    if t == 0:
                        if b == 1:
                            pe.wait_ge(wo_lo, i + 1)
                        pe.wait_ge(t_f, n)
                    elif t == 1:
                        if not last:
                            pe.wait_ge(v_f, n + 2)
                        else:
                            pe.wait_ge(y_f, 4 * (n - 1))
                    else:
                        pe.wait_ge(y_f, 4 * (n - 1) + t - 1)
                    project_out(n - 1, t)

            def step(i, n, b, first, second, last):
                for u in range(UA):
                    U = UA * n + u
                    scores(n, U, u, b, not (first and u < 2))
                    job(i, n, u, b, first, second, last)
                    if not (first and u < TURN):
                        turn(U - TURN, u - TURN, not (first and u - TURN < 2))
                    if not (first and u < PV):
                        before = 1 if u < PV else 0
                        pv(n - before, U - PV, u - PV, (b + before) % 2, not (first and u - PV < 2 * BT))

            def body(i, first, last):
                step(i, 2 * i, 0, first, False, False)
                step(i, 2 * i + 1, 1, False, first, last)

            loop(pe, body)
            end = UA * STEPS
            for U in range(end, end + PV):
                if U - TURN < end:
                    turn(U - TURN, (U - TURN) % UA, True)
                pv(STEPS - 1, U - PV, (U - PV) % UA, 1, True)
            pe.wait_ge(y_f, 4 * (STEPS - 1))
            turn_out(STEPS - 1, 1)
            for t in range(BT):
                if t == 0:
                    pe.wait_ge(t_f, STEPS)
                else:
                    pe.wait_ge(y_f, 4 * (STEPS - 1) + max(t - 1, 0))
                project_out(STEPS - 1, t)



GROUPS = 8
HPG = 2
DH = 128
SX = 1024
XT = SX // P
SCALE_X = 1.0 / float(np.sqrt(DH))
KINDS = 2 * HPG
UX = KINDS * BT
SELF_U = HPG * BT
PIECES = SELF_U + 2 * (UX - SELF_U)
PAIRS = UX // 2
BLOCKS = KINDS * BT + BT + XT
FP8_MAX = 448.0

C_LNW, C_LNB, C_IN, C_HEAD, C_SMOOTH, C_SCALAR = 0, 4, 8, 24, 32, 64
COLS = 70
SC_Q, SC_QX, SC_K, SC_V, SC_PIN, SC_PW = range(6)


def round_fp8(dve, sem, base, y, unit, total):
    dve.tensor_scalar(y, y, FP8_MAX, -FP8_MAX, ALU.min, ALU.max).then_inc(sem, 1)
    dve.wait_ge(sem, base + 1)
    dve.tensor_scalar(unit.bitcast(U16), y.bitcast(U16), 0x7F80, 0x40, ALU.bitwise_and, ALU.bitwise_or).then_inc(sem, 1)
    dve.wait_ge(sem, base + 2)
    dve.tensor_scalar(unit, unit, 1.5 * 2.0 ** -6, 2.0 ** 20, ALU.max, ALU.mult).then_inc(sem, 1)
    dve.wait_ge(sem, base + 3)
    dve.tensor_tensor(total, y, unit, ALU.add).then_inc(sem, 1)


ROUND_STEPS = 4


def second_norm(nc, ins, sem, sb, bank, X, ident, cols, xq, cxh, cxl, rcols):
    n = norm_tiles(sem, sb, "n2")
    L = [sb(f"L{i}", [P, S], F32) for i in range(2)]
    y = [sb(f"y{i}", [P, 4, S], BF16) for i in range(2)]
    unit = [sb(f"unit{i}", [P, 4, S], BF16) for i in range(2)]
    total = [sb(f"total{i}", [P, 4, S], F32) for i in range(2)]
    craw = [sb(f"craw{i}", [P, B * SX], F32) for i in range(2)]
    c_in = [sem(f"b_c_in{i}") for i in range(2)]
    c_hi, c_lo, s_rcols = sem("b_c_hi"), sem("b_c_lo"), sem("b_rcols")
    L_f, y_f, r_dve, r_pool = sem("b_L_f"), sem("b_y_f"), sem("b_r_dve"), sem("b_r_pool")
    with nc.Block() as block:
        @block.sync
        def _(sp):
            for k in range(KT):
                if k >= 2:
                    sp.wait_ge(c_lo, k - 1)
                sp.dma_start(craw[k % 2][:], ins["ctx"][k]).then_inc(c_in[k % 2], 16)

        @block.scalar
        def _(act):
            for k in range(2):
                act.wait_ge(c_in[k], 16)
                act.activation(cxh[:, k, :], craw[k][:], ACT.Copy).then_inc(c_hi, 1)
            for again in range(2):
                act.wait_ge(n.s_shift, again + 1)
                for t in range(NT):
                    act.activation(n.xn[:, t, :], (X, n.xn)[again][:, t, :], ACT.Identity, scale=n.rstd[:, t:t + 1],
                                   bias=n.shift[:, t:t + 1]).then_inc(n.s_xn, 1)
            act.wait_ge(s_rcols, 2)
            for j in range(B * KT):
                k = j % KT
                act.wait_ge(n.s_turned, j + 1)
                act.activation(L[j % 2][:], bank[:, j % 2, :], ACT.Identity, scale=cols[:, C_LNW + k:C_LNW + k + 1],
                               bias=cols[:, C_LNB + k:C_LNB + k + 1]).then_inc(L_f, 1)
                act.wait_ge(L_f, j + 1)
                if j >= 2:
                    act.wait_ge(r_pool, j - 1)
                for s in range(4):
                    c = C_IN + 4 * s + k
                    act.activation(y[j % 2][:, s, :], L[j % 2][:], ACT.Copy, scale=rcols[:, c:c + 1]).then_inc(y_f, 1)
                if j in (1, 3):
                    kk = 2 + j // 2
                    act.wait_ge(c_in[kk % 2], 32)
                    act.activation(cxh[:, kk, :], craw[kk % 2][:], ACT.Copy).then_inc(c_hi, 1)

        @block.vector
        def _(dve):
            for c in (slice(C_IN, C_IN + 4 * KT), slice(C_SMOOTH, C_SMOOTH + GROUPS * KINDS)):
                dve.reciprocal(rcols[:, c], cols[:, c]).then_inc(s_rcols, 1)
            norm_stats(dve, n, X, lambda t: None)
            norm_stats(dve, n, n.xn, lambda t: dve.wait_ge(n.s_xn, t + 1), base=1)

            def ctx_lo(k):
                dve.wait_ge(c_hi, k + 1)
                dve.tensor_tensor(cxl[:, k, :], craw[k % 2][:], cxh[:, k, :], ALU.subtract).then_inc(c_lo, 1)

            ctx_lo(0)
            ctx_lo(1)
            for j in range(B * KT):
                dve.wait_ge(y_f, 4 * (j + 1))
                round_fp8(dve, r_dve, ROUND_STEPS * j, y[j % 2][:], unit[j % 2][:], total[j % 2][:])
                if j in (2, 4):
                    ctx_lo(1 + j // 2)

        @block.gpsimd
        def _(pool):
            for j in range(B * KT):
                b, k = j // KT, j % KT
                pool.wait_ge(r_dve, ROUND_STEPS * (j + 1))
                pool.tensor_tensor(xq[:, :, k, S * b:S * (b + 1)], total[j % 2][:], unit[j % 2][:],
                                   ALU.subtract).then_inc(r_pool, 1)

        @block.tensor
        def _(pe):
            pe.wait_ge(n.s_xn, 2 * NT)
            for j in range(B * KT):
                b, k = j // KT, j % KT
                if j >= 2:
                    pe.wait_ge(L_f, j - 1)
                for t in range(BT):
                    ins_ = pe.transpose(bank[:, j % 2, P * t:P * (t + 1)],
                                        n.xn[:, BT * b + t, P * k:P * (k + 1)], ident[:])
                ins_.then_inc(n.s_turned, 1)


JOBS = ("A0 A1 A2 A3 B0 R3 C0 C1 B1 C2 C3 Y0 Y1 R0 Y2 Y3 T0 R1 T1 T2 T3 T4 T5 T6 R2").split()
SLOT_A = {0: "A0", 1: "A2", 2: "B0", 3: "C0", 4: "B1", 5: "C3", 6: "Y1", 7: "Y2", 10: "T0", 11: "T1", 12: "T3", 13: "T5"}
SLOT_B = {0: "A1", 1: "A3", 2: "R3", 3: "C1", 4: "C2", 5: "Y0", 6: "R0", 7: "Y3", 10: "R1", 11: "T2", 12: "T4",
          13: "T6", 14: "R2"}
V_ORDER = ("B0", "C0", "C1", "B1", "C2", "C3")
NEXT = [j for j in JOBS if j[0] in "ABCT"]
LATE = [j for j in JOBS if j[0] == "Y"] + ["R3"]


def jobs_of(first, last):
    return [j for j in JOBS if not (first and j in LATE) and not (last and j in NEXT)]


def job_number(name, n, first=False, last=False, prologue=False):
    if prologue:
        return NEXT.index(name)
    if first:
        return len(NEXT) + jobs_of(True, False).index(name)
    return len(NEXT) - len(LATE) + len(JOBS) * n + jobs_of(False, last).index(name)


def piece_end(u):
    if u < 0:
        return piece_end(u + UX) - PIECES
    return u + 1 if u < SELF_U else SELF_U + 2 * (u + 1 - SELF_U)


def group_attention(nc, ins, sem, sb, bank, X, ident, cols, rcols, xq, cxh, cxl):
    STEPS = GROUPS * B
    wraw = sb("xwraw", [P, KT, S], F32)
    w1h, w1l, w2h, w2l, w3h, w3l = (sb(f"x{x}", [P, KT, S], F16) for x in ("w1h", "w1l", "w2h", "w2l", "w3h", "w3l"))
    qr = sb("qr", [P, BT, 5 * DH], F32)
    kr = sb("kr", [P, XT, DH], F32)
    stats, mv = sb("xstats", [P, BLOCKS, 6], F32), sb("xmv", [P, BLOCKS, 2], F32)
    half, tmp, rstd, shift = (sb(f"x{x}", [P, BLOCKS], F32) for x in ("half", "tmp", "rstd", "shift"))
    ft = [sb(f"ft{i}", [P, S], F32) for i in range(2)]
    vt = [ft[i][:, 0:2 * DH].rearrange("p (t c) -> p t c", t=2) for i in range(2)]
    qh, ql = ([sb(f"x{x}{b}", [P, KINDS, S], F16) for b in range(B)] for x in ("qh", "ql"))
    kh, kl = ([sb(f"x{x}{b}", [P, S], F16) for b in range(B)] for x in ("kh", "kl"))
    kxh, kxl = ([sb(f"{x}{b}", [P, SX], F16) for b in range(B)] for x in ("kxh", "kxl"))
    vh, vl = ([sb(f"x{x}{b}", [P, BT, DH], F16) for b in range(B)] for x in ("vh", "vl"))
    vxh, vxl = ([sb(f"{x}{b}", [P, XT, DH], F16) for b in range(B)] for x in ("vxh", "vxl"))
    prob = [sb(f"xprob{i}", [P, SX], F32) for i in range(2)]
    pth, ptl = ([sb(f"x{x}{i}", [P, XT, 2 * P], F16) for i in range(2)] for x in ("pth", "ptl"))
    nm = sb("xnm", [P, 4], F32)
    hcols = sb("hcols", [P, 8], F32)
    rs, ri = sb("xrs", [P, 2, BT], F32), sb("xri", [P, 2, BT], F32)
    R = sb("R", [P, S], F32)
    y, unit, total = sb("xy", [P, S], BF16), sb("xunit", [P, S], BF16), sb("xtotal", [P, S], F32)
    cat = sb("cat", [P, KINDS, S], F16)
    rsm = sb("rsm", [P, KINDS], F32)
    psc = sb("psc", [P, 1], F32)
    SC = [bank[:, 2 * i:2 * i + 2, :].rearrange("p a c -> p (a c)") for i in range(2)]
    PT, O, J = [bank[:, 4, :], bank[:, 5, :]], bank[:, 6, :], bank[:, 7, :]

    passed_sp, passed_pool, passed_dve = sem("x_passed_sp"), sem("x_passed_pool"), sem("x_passed_dve")
    w_in = sem("x_w_in")
    w_hi, w_lo = sem("x_w_hi"), sem("x_w_lo")
    job_done, job_read = sem("x_job_done"), sem("x_job_read")
    s_stats, s_mv, s_rsqrt, s_shift, applied = (sem(f"x_{x}") for x in ("stats", "mv", "rsqrt", "shift", "applied"))
    t_hi, t_lo, v_hi, v_lo = (sem(f"x_{x}") for x in ("t_hi", "t_lo", "v_hi", "v_lo"))
    scored, maxed, exped, turned, hi, lo, pved, recip = (
        sem(f"x_{x}") for x in ("scored", "maxed", "exped", "turned", "hi", "lo", "pved", "recip"))
    o_read, rounding, rounded, s_rsm, s_psc, s_hcols = (
        sem(f"x_{x}") for x in ("o_read", "rounding", "rounded", "rsm", "psc", "hcols"))
    W1N, W2N, W3N = 2 * KT, 3 * KT, KT
    WN = W1N + W2N + W3N

    def w_base(g):
        return W1N + W2N + WN * g

    def loop(body):
        def run(eng):
            body(0, True, False)
            with eng.Fori(1, GROUPS - 1) as g:
                body(g, False, False)
            body(GROUPS - 1, False, True)
        return run

    def split_ops(chunk):
        if chunk == 1:
            return [(k, k, slice(256 * s, 256 * (s + 1)), cols[:, C_IN + 4 * s + k:C_IN + 4 * s + k + 1])
                    for k in range(KT) for s in range(2)]
        if chunk == 2:
            return [x for k in range(KT) for x in
                    [(k, k, slice(DH * s, DH * (s + 1)), cols[:, C_IN + 8 + 4 * s + k:C_IN + 9 + 4 * s + k])
                     for s in range(2)] + [(k, k, slice(2 * DH, 4 * DH), WS)]]
        return [(k, k, slice(0, S), 1.0) for k in range(KT)]

    with nc.Block() as block:
        @block.sync
        def _(sp):
            wait = alone(sp, passed_sp)
            def load(chunk, g, before):
                wait(w_lo, before)
                sp.dma_start(wraw[:], ins["w_group"][bass.ds(g, 1), chunk - 1].rearrange("a p k n -> p (a k) n"))\
                    .then_inc(w_in, 16)

            load(1, 0, 0)
            load(2, 0, W1N)

            def body(g, first, last):
                if not last:
                    load(1, g + 1, w_base(g))
                    load(2, g + 1, w_base(g) + W1N)
                    load(3, g, w_base(g) + W1N + W2N)
                else:
                    load(3, g, w_base(g))

            loop(body)(sp)

        @block.gpsimd
        def _(pool):
            wait = alone(pool, passed_pool)
            def split_hi(chunk, loaded, free, count):
                wait(w_in, 16 * loaded)
                wait(free, count)
                wh = (w1h, w2h, w3h)[chunk - 1]
                for _, k, c, scale in split_ops(chunk):
                    pool.tensor_scalar(wh[:, k, c], wraw[:, k, c], scale, 1.0, ALU.mult, ALU.mult).then_inc(w_hi, 1)

            def values(name, m, b, job):
                v = V_ORDER.index(name)
                j = int(name[1])
                h, l = (vh, vl) if name[0] == "B" else (vxh, vxl)
                wait(job_read, job + 1)
                wait(pved, PAIRS * (m - 1))
                pool.tensor_scalar(h[b][:, 2 * j:2 * j + 2, :], vt[v % 2], 1.0, 1.0, ALU.mult, ALU.mult)\
                    .then_inc(v_hi, 1)
                wait(v_hi, len(V_ORDER) * m + v + 1)
                pool.tensor_tensor(l[b][:, 2 * j:2 * j + 2, :], vt[v % 2], h[b][:, 2 * j:2 * j + 2, :],
                                   ALU.subtract).then_inc(v_lo, 1)

            def apply(m):
                wait(s_shift, m + 1)
                for i in range(BLOCKS):
                    if i < 5 * BT:
                        c, t = i // BT, i % BT
                        a = qr[:, t, DH * c:DH * (c + 1)]
                    else:
                        a = kr[:, i - 5 * BT, :]
                    pool.tensor_scalar(a, a, rstd[:, i:i + 1], shift[:, i:i + 1], ALU.mult, ALU.add)\
                        .then_inc(applied, 1)

            def turned_parts(i, m, b, job):
                if i < 4:
                    h, l = qh[b][:, i, :], ql[b][:, i, :]
                elif i == 4:
                    h, l = kh[b][:], kl[b][:]
                else:
                    half_ = slice(S * (i - 5), S * (i - 4))
                    h, l = kxh[b][:, half_], kxl[b][:, half_]
                wait(job_read, job + 1)
                if i == 0:
                    wait(scored, UX * (m - 1))
                pool.tensor_scalar(h, ft[i % 2][:], 1.0, 1.0, ALU.mult, ALU.mult).then_inc(t_hi, 1)
                wait(t_hi, 7 * m + i + 1)
                pool.tensor_tensor(l, ft[i % 2][:], h, ALU.subtract).then_inc(t_lo, 1)

            def quantised(n, kind, cat_read=0):
                count = KINDS * n + kind + 1
                wait(rounding, ROUND_STEPS * count)
                wait(job_done, cat_read)
                pool.tensor_tensor(cat[:, kind, :], total[:], unit[:], ALU.subtract).then_inc(rounded, 1)

            split_hi(1, 1, None, 0)
            split_hi(2, 2, None, 0)
            for name in V_ORDER:
                values(name, 0, 0, job_number(name, 0, prologue=True))
            apply(0)
            for i in range(7):
                turned_parts(i, 0, 0, job_number(f"T{i}", 0, prologue=True))

            def step(g, n, b, first, last, last_group):
                job = lambda name: job_number(name, n, first, last)
                for u in range(UX):
                    if not last:
                        for name in [x for x in (SLOT_A.get(u), SLOT_B.get(u)) if x in V_ORDER]:
                            values(name, n + 1, 1 - b, job(name))
                    if u == 3 and not first:
                        quantised(n - 1, 3)
                    if b == 0 and not last_group:
                        if u == 2:
                            split_hi(1, 3 * g + 3, job_done, job("A3") + 1)
                    if u == 6 and not last:
                        apply(n + 1)
                    if u == 7:
                        if b == 0 and not last_group:
                            split_hi(2, 3 * g + 4, job_done, job("C3") + 1)
                        quantised(n, 0, 0 if first else job("Y3") + 1)
                    if b == 0 and u == 13:
                        split_hi(3, 3 * g + 5 if not last_group else 3 * g + 3, job_done,
                                 job("Y3") + 1 if not first else 0)
                    for name in (SLOT_A.get(u), SLOT_B.get(u)):
                        if not last and name and name[0] == "T":
                            turned_parts(int(name[1]), n + 1, 1 - b, job(name))
                    if u in (11, 15):
                        quantised(n, (u - 7) // 4)

            def body(g, first, last):
                step(g, 2 * g, 0, first, False, last)
                step(g, 2 * g + 1, 1, False, last, last)

            loop(body)(pool)
            quantised(STEPS - 1, 3)

        @block.scalar
        def _(act):
            def read_job(name, m, b, job, n=0):
                k, j = name[0], int(name[1])
                act.wait_ge(job_done, job + 1)
                if k == "A":
                    for s, c in enumerate((SC_Q, SC_QX)):
                        r = slice(256 * s, 256 * (s + 1))
                        last = act.activation(qr[:, j, r], J[:, r], ACT.Copy, scale=cols[:, C_SCALAR + c:C_SCALAR + c + 1])
                elif k in "BC":
                    v = V_ORDER.index(name)
                    after(act, v_lo, len(V_ORDER) * m + v - 1)
                    if v == 0:
                        after(act, t_lo, 7 * m)
                    Jv = J.rearrange("p (t s c) -> p t s c", t=2, s=2)
                    if k == "B":
                        act.activation(qr[:, 2 * j:2 * j + 2, 4 * DH:5 * DH], Jv[:, :, 0, :], ACT.Copy,
                                       scale=cols[:, C_SCALAR + SC_K:C_SCALAR + SC_K + 1])
                        last = act.activation(vt[v % 2], Jv[:, :, 1, :], ACT.Copy,
                                              scale=cols[:, C_SCALAR + SC_V:C_SCALAR + SC_V + 1])
                    else:
                        act.activation(kr[:, 2 * j:2 * j + 2, :], Jv[:, :, 0, :], ACT.Copy, scale=1.0 / WS)
                        last = act.activation(vt[v % 2], Jv[:, :, 1, :], ACT.Copy, scale=1.0 / WS)
                elif k == "T":
                    c = (0, 0, 4, 4, 2, 6, 6)[j]
                    after(act, t_lo, 7 * m + j - 1 if j >= 2 else 7 * m)
                    if j == 0:
                        act.wait_ge(v_lo, len(V_ORDER) * (m + 1))
                    last = act.activation(ft[j % 2][:], J, ACT.Identity, scale=hcols[:, c:c + 1], bias=hcols[:, c + 1:c + 2])
                else:
                    after(act, o_read, KINDS * n + j)
                    last = act.activation(R[:], J, ACT.Copy)
                last.then_inc(job_read, 1)

            def exp(n, u):
                L = S if u < SELF_U else SX
                act.wait_ge(maxed, UX * n + u + 1)
                after(act, turned, PIECES * n + piece_end(u - 2))
                kind, qt = u // BT, u % BT
                act.activation(prob[u % 2][:, 0:L], SC[u % 2][:, 0:L], ACT.Exp,
                               bias=nm[:, u % 4:u % 4 + 1], accum_out=rs[:, kind % 2, qt:qt + 1]).then_inc(exped, 1)

            def parts_hi(n, u):
                pair, q = u // 2, P * (u % 2)
                for j in range(1 if u < SELF_U else 2):
                    piece = piece_end(u - 1) + j
                    act.wait_ge(turned, PIECES * n + piece + 1)
                    after(act, pved, PAIRS * n + pair - 1)
                    act.activation(pth[pair % 2][:, 4 * j:4 * j + 4, q:q + P],
                                   PT[piece % 2].rearrange("p (k c) -> p k c", k=4), ACT.Copy).then_inc(hi, 1)

            act.wait_ge(s_hcols, 3)
            for name in NEXT:
                read_job(name, 0, 0, job_number(name, 0, prologue=True))

            def step(g, n, b, first, last):
                for u in range(UX):
                    for slot in (SLOT_A, SLOT_B):
                        name = slot.get(u)
                        if name in jobs_of(first, last) and name[0] != "Y":
                            step_of_r = n - 1 if name == "R3" else n
                            read_job(name, n + 1, 1 - b, job_number(name, n, first, last), step_of_r)
                        if slot is SLOT_A and not (first and u < 2):
                            parts_hi(n if u >= 2 else n - 1, (u - 2) % UX)
                    exp(n, u)

            def body(g, first, last):
                step(g, 2 * g, 0, first, False)
                step(g, 2 * g + 1, 1, False, last)

            loop(body)(act)
            for u in (UX - 2, UX - 1):
                parts_hi(STEPS - 1, u)
            read_job("R3", 0, 0, job_number("R2", STEPS - 1, last=True) + 1, STEPS - 1)

        @block.vector
        def _(dve):
            def split_lo(chunk, base, pieces):
                wh, wl = (w1h, w2h, w3h)[chunk - 1], (w1l, w2l, w3l)[chunk - 1]
                for i, (piece, k, c, scale) in enumerate(split_ops(chunk)):
                    if piece in pieces:
                        dve.wait_ge(w_hi, base + i + 1)
                        dve.scalar_tensor_tensor(out=wl[:, k, c], in0=wraw[:, k, c], scalar=scale, in1=wh[:, k, c],
                                                 op0=ALU.mult, op1=ALU.subtract).then_inc(w_lo, 1)

            wait = alone(dve, passed_dve)

            def block_stats(name, m, job):
                k, j = name[0], int(name[1])
                if k == "A":
                    blocks = [(c * BT + j, qr[:, j, DH * c:DH * (c + 1)]) for c in range(KINDS)]
                elif k == "B":
                    blocks = [(4 * BT + t, qr[:, t, 4 * DH:5 * DH]) for t in (2 * j, 2 * j + 1)]
                else:
                    blocks = [(5 * BT + t, kr[:, t, :]) for t in (2 * j, 2 * j + 1)]
                at = BLOCKS * m + sum(4 if x[0] == "A" else 2 for x in NEXT[:NEXT.index(name)])
                dve.wait_ge(job_read, job + 1)
                for i, a in blocks:
                    dve.bn_stats(stats[:, i, :], a).then_inc(s_stats, 1)
                for c, (i, a) in enumerate(blocks):
                    wait(s_stats, at + c + 1)
                    dve.bn_aggr(mv[:, i, :], stats[:, i, :]).then_inc(s_mv, 1)

            def deviations(m):
                dve.wait_ge(s_mv, BLOCKS * (m + 1))
                after(dve, applied, BLOCKS * m)
                rsqrt(dve, s_rsqrt, RSQRT_STEPS * m, mv[:, :, 1], half[:], rstd[:], tmp[:])
                dve.scalar_tensor_tensor(out=shift[:], in0=mv[:, :, 0], scalar=-1.0, in1=rstd[:],
                                         op0=ALU.mult, op1=ALU.mult).then_inc(s_shift, 1)

            def maxima(n, u):
                L, s = (S if u < SELF_U else SX), u % 4
                dve.wait_ge(scored, UX * n + u + 1)
                dve.tensor_reduce(nm[:, s:s + 1], SC[u % 2][:, 0:L], AX.X, ALU.max, negate=True).then_inc(maxed, 1)

            def parts_lo(n, u):
                pair, q = u // 2, P * (u % 2)
                for j in range(1 if u < SELF_U else 2):
                    piece = piece_end(u - 1) + j
                    dve.wait_ge(hi, PIECES * n + piece + 1)
                    dve.tensor_tensor(ptl[pair % 2][:, 4 * j:4 * j + 4, q:q + P],
                                      PT[piece % 2].rearrange("p (k c) -> p k c", k=4),
                                      pth[pair % 2][:, 4 * j:4 * j + 4, q:q + P], ALU.subtract).then_inc(lo, 1)

            def reciprocals(n, kind):
                dve.wait_ge(exped, UX * n + BT * (kind + 1))
                dve.reciprocal(ri[:, kind % 2, :], rs[:, kind % 2, :]).then_inc(recip, 1)

            def output(n, kind, r_job):
                count = KINDS * n + kind
                dve.wait_ge(job_read, r_job + 1)
                dve.wait_ge(pved, PAIRS * n + 2 * (kind + 1))
                after(dve, rounded, count)
                dve.scalar_tensor_tensor(out=y[:], in0=O, scalar=rsm[:, kind:kind + 1], in1=R[:], op0=ALU.mult,
                                         op1=ALU.mult).then_inc(o_read, 1)

            def output_round(n, kind):
                count = KINDS * n + kind
                dve.wait_ge(o_read, count + 1)
                round_fp8(dve, rounding, ROUND_STEPS * count, y[:], unit[:], total[:])

            def project_out(t, b, job):
                dve.wait_ge(job_done, job + 1)
                x = X[:, BT * b + t, :]
                dve.scalar_tensor_tensor(out=x, in0=J, scalar=psc[:], in1=x, op0=ALU.mult, op1=ALU.add)\
                    .then_inc(job_read, 1)

            dve.tensor_tensor(psc[:], cols[:, C_SCALAR + SC_PIN:C_SCALAR + SC_PIN + 1],
                              cols[:, C_SCALAR + SC_PW:C_SCALAR + SC_PW + 1], ALU.mult).then_inc(s_psc, 1)
            dve.wait_ge(s_psc, 1)
            dve.tensor_copy(hcols[:], cols[:, C_HEAD:C_HEAD + 8]).then_inc(s_hcols, 1)
            dve.wait_ge(s_hcols, 1)
            for c in (0, 4):
                dve.tensor_scalar(hcols[:, c:c + 2], cols[:, C_HEAD + c:C_HEAD + c + 2], SCALE_X, None,
                                  ALU.mult).then_inc(s_hcols, 1)
            split_lo(1, 0, range(KT))
            split_lo(2, W1N, range(KT))
            for name in NEXT:
                if name[0] != "T":
                    block_stats(name, 0, job_number(name, 0, prologue=True))
            deviations(0)

            STATS_AT = {1: ("A0", "A1"), 2: ("A2", "A3"), 3: ("B0",), 4: ("C0", "C1"), 5: ("B1", "C2"), 6: ("C3",)}

            def step(g, n, b, first, last, last_group):
                job = lambda name: job_number(name, n, first, last)
                for u in range(UX):
                    maxima(n, u)
                    for slot in (SLOT_A, SLOT_B):
                        name = slot.get(u)
                        if name and name[0] == "Y" and not first:
                            project_out(int(name[1]), 1 - b, job(name))
                        if slot is SLOT_A and not (first and u < 2):
                            parts_lo(n if u >= 2 else n - 1, (u - 2) % UX)
                    if not last:
                        for name in STATS_AT.get(u, ()):
                            block_stats(name, n + 1, job(name))
                        if u == 6:
                            deviations(n + 1)
                    if u % 4 == 1 and not (first and u == 1):
                        reciprocals(n if u > 1 else n - 1, (u // 4 - 1) % KINDS)
                    if u == 3 and not first:
                        output(n - 1, 3, job("R3"))
                        output_round(n - 1, 3)
                    if u == 4 and b == 0:
                        after(dve, o_read, KINDS * n)
                        dve.tensor_copy(rsm[:], rcols[:, bass.ds(C_SMOOTH + KINDS * g, KINDS)]).then_inc(s_rsm, 1)
                        dve.wait_ge(s_rsm, g + 1)
                    if u in (7, 11, 15):
                        output(n, u // 4 - 1, job(f"R{u // 4 - 1}"))
                        output_round(n, u // 4 - 1)
                    if b == 0 and not last_group:
                        if u in (3, 4, 5, 6):
                            split_lo(1, w_base(g), (u - 3,))
                        if u in (9, 10, 11, 12):
                            split_lo(2, w_base(g) + W1N, (u - 9,))
                    if b == 0 and u >= 14:
                        split_lo(3, w_base(g) + (0 if last_group else W1N + W2N), (2 * u - 28, 2 * u - 27))

            def body(g, first, last):
                step(g, 2 * g, 0, first, False, last)
                step(g, 2 * g + 1, 1, False, last, last)

            loop(body)(dve)
            for u in (UX - 2, UX - 1):
                parts_lo(STEPS - 1, u)
            reciprocals(STEPS - 1, 3)
            r3 = job_number("R2", STEPS - 1, last=True) + 1
            output(STEPS - 1, 3, r3)
            output_round(STEPS - 1, 3)
            for t in range(BT):
                project_out(t, 1, r3 + 1 + t)

        @block.tensor
        def _(pe):
            def run_job(name, m, b, job, g_weights=None):
                k, j = name[0], int(name[1])
                if job_is_not_first(job):
                    pe.wait_ge(job_read, job)
                if k == "A":
                    tok = slice(S * b + P * j, S * b + P * (j + 1))
                    for s in range(2):
                        c = slice(256 * s, 256 * (s + 1))
                        for kt in range(KT):
                            pe.matmul(J[:, c], xq[:, s, kt, tok], w1h[:, kt, c], start=(kt == 0), stop=False)
                            last = pe.matmul(J[:, c], xq[:, s, kt, tok], w1l[:, kt, c], start=False, stop=(kt == KT - 1))
                elif k == "B":
                    for i in range(2):
                        tok = slice(S * b + P * (2 * j + i), S * b + P * (2 * j + i + 1))
                        for s in range(2):
                            o = J[:, 256 * i + DH * s:256 * i + DH * (s + 1)]
                            c = slice(DH * s, DH * (s + 1))
                            for kt in range(KT):
                                pe.matmul(o, xq[:, 2 + s, kt, tok], w2h[:, kt, c], start=(kt == 0), stop=False)
                                last = pe.matmul(o, xq[:, 2 + s, kt, tok], w2l[:, kt, c], start=False,
                                                 stop=(kt == KT - 1))
                elif k == "C":
                    for i in range(2):
                        tok = slice(SX * b + P * (2 * j + i), SX * b + P * (2 * j + i + 1))
                        for kt in range(KT):
                            last = three(pe, J[:, 256 * i:256 * (i + 1)], cxh[:, kt, tok], cxl[:, kt, tok],
                                         w2h[:, kt, 2 * DH:4 * DH], w2l[:, kt, 2 * DH:4 * DH], kt == 0, kt == KT - 1)
                elif k == "T":
                    pe.wait_ge(applied, BLOCKS * m + BT * (j + 1))
                    for t in range(BT):
                        src = qr[:, t, DH * j:DH * (j + 1)] if j < 5 else kr[:, BT * (j - 5) + t, :]
                        last = pe.transpose(J[:, P * t:P * (t + 1)], src, ident[:])
                elif k == "R":
                    pe.wait_ge(recip, KINDS * m + j + 1)
                    for t in range(BT):
                        last = pe.transpose(J[:, P * t:P * (t + 1)], ri[:, j % 2, t:t + 1].broadcast_to([P, P]), ident[:])
                else:
                    pe.wait_ge(rounded, KINDS * (m + 1))
                    for kind in range(KINDS):
                        c = cat[:, kind, P * j:P * (j + 1)]
                        pe.matmul(J, c, w3h[:, kind, :], start=(kind == 0), stop=False)
                        last = pe.matmul(J, c, w3l[:, kind, :], start=False, stop=(kind == KINDS - 1))
                last.then_inc(job_done, 1)

            def job_is_not_first(job):
                return not isinstance(job, int) or job > 0

            def scores(n, u, b):
                kind, qt = u // BT, u % BT
                after(pe, exped, UX * n + u - 1)
                q = slice(P * qt, P * (qt + 1))
                a, c = (kh[b], kl[b]) if u < SELF_U else (kxh[b], kxl[b])
                for j in range(1 if u < SELF_U else 2):
                    r = slice(S * j, S * (j + 1))
                    last = three(pe, SC[u % 2][:, r], qh[b][:, kind, q], ql[b][:, kind, q], a[:, r], c[:, r], True, True)
                last.then_inc(scored, 1)

            def turn(n, u):
                pe.wait_ge(exped, UX * n + u + 1)
                for j in range(1 if u < SELF_U else 2):
                    piece = piece_end(u - 1) + j
                    after(pe, lo, PIECES * n + piece - 1)
                    for k in range(4):
                        last = pe.transpose(PT[piece % 2][:, P * k:P * (k + 1)],
                                            prob[u % 2][:, P * (4 * j + k):P * (4 * j + k + 1)], ident[:])
                    last.then_inc(turned, 1)

            def product(n, u, b):
                pair = u // 2
                if pair == 0:
                    pe.wait_ge(v_lo, len(V_ORDER) * (n + 1))
                if pair % 2 == 0:
                    after(pe, o_read, KINDS * n + pair // 2)
                pe.wait_ge(lo, PIECES * n + piece_end(u))
                h, l, tiles = (vh[b], vl[b], BT) if u < SELF_U else (vxh[b], vxl[b], XT)
                c = slice(2 * P * (pair % 2), 2 * P * (pair % 2 + 1))
                for k in range(tiles):
                    last = three(pe, O[:, c], h[:, k, :], l[:, k, :], pth[pair % 2][:, k, :], ptl[pair % 2][:, k, :],
                                 k == 0, k == tiles - 1)
                last.then_inc(pved, 1)

            pe.wait_ge(w_lo, W1N + W2N)
            for name in NEXT:
                run_job(name, 0, 0, job_number(name, 0, prologue=True))

            def step(g, n, b, first, last):
                for u in range(UX):
                    if u == 0:
                        pe.wait_ge(t_lo, 7 * (n + 1))
                    scores(n, u, b)
                    for slot in (SLOT_A, SLOT_B):
                        name = slot.get(u)
                        if name in jobs_of(first, last):
                            if name[0] in "ABCT":
                                served, sb_ = n + 1, 1 - b
                            else:
                                served = n - 1 if name in LATE else n
                                sb_ = None
                            if b == 1 and name == "A0":
                                pe.wait_ge(w_lo, w_base(g) + W1N)
                            if b == 1 and name == "B0":
                                pe.wait_ge(w_lo, w_base(g) + W1N + W2N)
                            if b == 1 and name == "Y0":
                                pe.wait_ge(w_lo, w_base(g) + (W3N if last else WN))
                            run_job(name, served, sb_, job_number(name, n, first, last))
                        if slot is SLOT_A and not (first and u < 2):
                            turn(n if u >= 2 else n - 1, (u - 2) % UX)
                    if u % 2 == 0 and not (first and u < 4):
                        product(n if u >= 4 else n - 1, (u - 3) % UX, b if u >= 4 else 1 - b)

            def body(g, first, last):
                step(g, 2 * g, 0, first, False)
                step(g, 2 * g + 1, 1, False, last)

            loop(body)(pe)
            turn(STEPS - 1, UX - 2)
            product(STEPS - 1, UX - 3, 1)
            turn(STEPS - 1, UX - 1)
            product(STEPS - 1, UX - 1, 1)
            r3 = job_number("R2", STEPS - 1, last=True) + 1
            run_job("R3", STEPS - 1, None, r3)
            for t in range(BT):
                run_job(f"Y{t}", STEPS - 1, None, r3 + 1 + t)


E = 8
FF = 1024
FT = FF // P
TOP_P = 0.9


def experts(nc, ins, sem, sb, bank, X, ident, out_d):
    n = norm_tiles(sem, sb, "n3")
    XTh, XTl = sb("eXTh", [P, KT, T], F16), sb("eXTl", [P, KT, T], F16)
    raw = [sb(f"raw_{x}", s, F32) for x, s in (("gate", [P, KT, FF]), ("up", [P, KT, FF]), ("down", [P, FT, D]))]
    wh = [sb(f"ewh_{x}", s, F16) for x, s in (("gate", [P, KT, FF]), ("up", [P, KT, FF]), ("down", [P, FT, D]))]
    wl = [sb(f"ewl_{x}", s, F16) for x, s in (("gate", [P, KT, FF]), ("up", [P, KT, FF]), ("down", [P, FT, D]))]
    sil = [sb(f"sil{i}", [P, S], F32) for i in range(2)]
    h = [sb(f"h{i}", [P, S], F32) for i in range(2)]
    hh = [sb(f"hh{i}", [P, FT, S], F16) for i in range(B)]
    hl = [sb(f"hl{i}", [P, FT, S], F16) for i in range(B)]
    rw, rwh, rwl = sb("rw", [P, KT, E], F32), sb("rwh", [P, KT, E], F16), sb("rwl", [P, KT, E], F16)
    logits, prob, before = (sb(x, [P, NT, E], F32) for x in ("logits", "eprob", "ebefore"))
    larger = sb("larger", [P, E, NT, E], F32)
    weight = sb("weight", [P, E, NT], F32)
    wcol = sb("wcol", [P, NT], F32)
    m8, s8, r8 = (sb(x, [P, NT], F32) for x in ("m8", "s8", "r8"))

    passed_sp, passed_pool = sem("e_passed_sp"), sem("e_passed_pool")
    raw_in = [sem(f"e_raw_in{i}") for i in range(3)]
    w_hi, w_lo = [sem(f"e_w_hi{i}") for i in range(3)], [sem(f"e_w_lo{i}") for i in range(3)]
    rw_in, rw_hi, rw_lo, routed, l_read, route, l_exp = (
        sem(f"e_{x}") for x in ("rw_in", "rw_hi", "rw_lo", "routed", "l_read", "route", "l_exp"))
    gated, upped, silu, made, h_hi, h_lo = (sem(f"e_{x}") for x in ("gated", "upped", "silu", "made", "h_hi", "h_lo"))
    down, added, s_wcol, stored = (sem(f"e_{x}") for x in ("down", "added", "wcol", "stored"))
    HT = B * FT
    PW = KT

    def piece(w, i, k):
        return w[i][:, k, :] if i < 2 else w[i][:, 2 * k:2 * k + 2, :]

    def loop(eng, body):
        body(0)
        with eng.Fori(1, E) as e:
            body(e)

    with nc.Block() as block:
        @block.sync
        def _(sp):
            wait = alone(sp, passed_sp)
            sp.dma_start(rw[:], ins["router"]).then_inc(rw_in, 16)

            def body(e):
                for i in range(3):
                    wait(w_lo[i], PW * e)
                    sp.dma_start(raw[i][:], ins[("gate", "up", "down")[i]][bass.ds(e, 1)]
                                 .rearrange("a p k n -> p (a k) n")).then_inc(raw_in[i], 16)

            loop(sp, body)
            for t in range(NT):
                wait(added, NT * (E - 1) + t + 1)
                sp.dma_start(out_d[t], X[:, t, :]).then_inc(stored, 16)
            wait(stored, 16 * NT)

        @block.gpsimd
        def _(pool):
            wait = alone(pool, passed_pool)
            def body(e):
                for i in range(HT):
                    half, f = i // FT, i % FT
                    wait(made, HT * e + i + 1)
                    if f == 0:
                        wait(down, NT * (e - 1) + BT * (half + 1))
                    pool.tensor_scalar(hh[half][:, f, :], h[i % 2][:], 1.0, 1.0, ALU.mult, ALU.mult).then_inc(h_hi, 1)
                    wait(h_hi, HT * e + i + 1)
                    pool.tensor_tensor(hl[half][:, f, :], h[i % 2][:], hh[half][:, f, :], ALU.subtract).then_inc(h_lo, 1)

            loop(pool, body)

        @block.scalar
        def _(act):
            def split_hi(e, i, k):
                act.wait_ge(raw_in[i], 16 * (e + 1))
                if k == 0:
                    after(act, upped if i < 2 else down, HT * e if i < 2 else NT * e)
                act.activation(piece(wh, i, k), piece(raw, i, k), ACT.Copy, scale=WS).then_inc(w_hi[i], 1)

            norm_scalar(act, n, X, XTh, bank)
            act.wait_ge(rw_in, 16)
            act.activation(rwh[:], rw[:], ACT.Copy, scale=WS).then_inc(rw_hi, 1)
            for i in range(2):
                for k in range(PW):
                    split_hi(0, i, k)
            act.wait_ge(routed, 1)
            act.activation(logits[:], bank[:, 4, 0:NT * E].rearrange("p (t e) -> p t e", t=NT), ACT.Copy, scale=1.0 / WS)\
                .then_inc(l_read, 1)
            act.wait_ge(route, 2)
            act.activation(prob[:], logits[:], ACT.Exp).then_inc(l_exp, 1)

            def body(e):
                for i in range(HT):
                    act.wait_ge(gated, HT * e + i + 1)
                    after(act, made, HT * e + i - 1)
                    act.activation(sil[i % 2][:], bank[:, 2 * (i % 2), :], ACT.Silu, scale=1.0 / WS).then_inc(silu, 1)
                    if 1 <= i <= PW:
                        split_hi(e, 2, i - 1)

            def next_weights(e):
                for i in range(2):
                    for k in range(PW):
                        split_hi(e, i, k)

            body(0)
            with act.Fori(1, E) as e:
                next_weights(e)
                body(e)

        @block.vector
        def _(dve):
            def split_lo(e, i, k):
                dve.wait_ge(w_hi[i], PW * e + k + 1)
                dve.scalar_tensor_tensor(out=piece(wl, i, k), in0=piece(raw, i, k), scalar=WS, in1=piece(wh, i, k),
                                         op0=ALU.mult, op1=ALU.subtract).then_inc(w_lo[i], 1)

            norm_vector(dve, n, X, XTh, XTl, bank, lambda t: None)
            dve.wait_ge(rw_hi, 1)
            dve.scalar_tensor_tensor(out=rwl[:], in0=rw[:], scalar=WS, in1=rwh[:], op0=ALU.mult, op1=ALU.subtract)\
                .then_inc(rw_lo, 1)
            for i in range(2):
                for k in range(PW):
                    split_lo(0, i, k)

            steps = 0

            def step(ins_):
                nonlocal steps
                ins_.then_inc(route, 1)
                steps += 1
                dve.wait_ge(route, steps)

            def wide(a):
                return a.unsqueeze(2).broadcast_to([P, NT, E])

            dve.wait_ge(l_read, 1)
            step(dve.tensor_reduce(m8[:], logits[:], AX.X, ALU.max))
            step(dve.tensor_tensor(logits[:], logits[:], wide(m8[:]), ALU.subtract))
            dve.wait_ge(l_exp, 1)
            step(dve.tensor_reduce(s8[:], prob[:], AX.X, ALU.add))
            step(dve.reciprocal(r8[:], s8[:]))
            step(dve.tensor_tensor(prob[:], prob[:], wide(r8[:]), ALU.mult))
            for e in range(E):
                mine = prob[:, :, e]
                if e:
                    dve.tensor_tensor(larger[:, e, :, 0:e], prob[:, :, 0:e],
                                      mine.unsqueeze(2).broadcast_to([P, NT, e]), ALU.is_ge).then_inc(route, 1)
                    steps += 1
                step(dve.tensor_tensor(larger[:, e, :, e:E], prob[:, :, e:E],
                                       mine.unsqueeze(2).broadcast_to([P, NT, E - e]), ALU.is_gt))
            step(dve.tensor_tensor(larger[:], larger[:], prob[:].unsqueeze(1).broadcast_to([P, E, NT, E]), ALU.mult))
            step(dve.tensor_reduce(before[:].rearrange("p t e -> p (t e)").rearrange("p (e t) -> p e t", e=E),
                                   larger[:], AX.X, ALU.add))
            kept = before[:].rearrange("p t e -> p (t e)").rearrange("p (e t) -> p e t", e=E)
            step(dve.tensor_scalar(kept, kept, TOP_P, 1.0 / WS ** 2, ALU.is_le, ALU.mult))
            step(dve.tensor_tensor(weight[:], kept, prob[:].rearrange("p t e -> p e t"), ALU.mult))

            def body(e):
                for i in range(HT):
                    dve.wait_ge(silu, HT * e + i + 1)
                    dve.wait_ge(upped, HT * e + i + 1)
                    after(dve, h_lo, HT * e + i - 1)
                    dve.tensor_tensor(h[i % 2][:], bank[:, 2 * (i % 2) + 1, :], sil[i % 2][:], ALU.mult).then_inc(made, 1)
                    if 2 <= i < 2 + PW:
                        split_lo(e, 2, i - 2)
                after(dve, added, NT * e)
                dve.tensor_copy(wcol[:], weight[:].rearrange("p e t -> p (e t)")[:, bass.ds(NT * e, NT)])\
                    .then_inc(s_wcol, 1)
                dve.wait_ge(s_wcol, e + 1)

            def add(e, t):
                dve.wait_ge(down, NT * e + t + 1)
                dve.scalar_tensor_tensor(out=X[:, t, :], in0=bank[:, 4 + t % 4, :], scalar=wcol[:, t:t + 1],
                                         in1=X[:, t, :], op0=ALU.mult, op1=ALU.add).then_inc(added, 1)

            body(0)
            with dve.Fori(1, E) as e:
                for i in range(2):
                    for k in range(PW):
                        split_lo(e, i, k)
                        add(e - 1, PW * i + k)
                body(e)
            for t in range(NT):
                add(E - 1, t)

        @block.tensor
        def _(pe):
            norm_tensor(pe, n, bank, ident)
            pe.wait_ge(rw_lo, 1)
            pe.wait_ge(n.s_lo, NT)
            for t in range(NT):
                for k in range(KT):
                    tok = slice(P * t, P * (t + 1))
                    last = three(pe, bank[:, 4, E * t:E * (t + 1)], XTh[:, k, tok], XTl[:, k, tok], rwh[:, k, :],
                                 rwl[:, k, :], k == 0, k == KT - 1)
            last.then_inc(routed, 1)

            def body(e):
                pe.wait_ge(w_lo[0], PW * (e + 1))
                pe.wait_ge(w_lo[1], PW * (e + 1))
                for i in range(HT):
                    half, f = i // FT, i % FT
                    after(pe, made, HT * e + i - 1)
                    for w, done in ((0, gated), (1, upped)):
                        for k in range(KT):
                            c = slice(P * f, P * (f + 1))
                            tok = slice(S * half, S * (half + 1))
                            last = three(pe, bank[:, 2 * (i % 2) + w, :], wh[w][:, k, c], wl[w][:, k, c],
                                         XTh[:, k, tok], XTl[:, k, tok], k == 0, k == KT - 1)
                        last.then_inc(done, 1)
                pe.wait_ge(w_lo[2], PW * (e + 1))
                for t in range(NT):
                    half = t // BT
                    if t % BT == 0:
                        pe.wait_ge(h_lo, HT * e + FT * (half + 1))
                    after(pe, added, NT * e + t - 3)
                    if isinstance(e, int) and e == 0 and t == 0:
                        pe.wait_ge(l_read, 1)
                    tok = slice(P * (t % BT), P * (t % BT + 1))
                    for f in range(FT):
                        last = three(pe, bank[:, 4 + t % 4, :], hh[half][:, f, tok], hl[half][:, f, tok],
                                     wh[2][:, f, :], wl[2][:, f, :], f == 0, f == FT - 1)
                    last.then_inc(down, 1)

            loop(pe, body)


def pack(x):
    c = np.ascontiguousarray
    rows = lambda w: w.reshape(-1, P, w.shape[-1]).transpose(1, 0, 2)
    wq, wk, wv = np.split(x["L0_attn_w_qkv"].T, 3, axis=1)
    bq, bk, bv = np.split(x["L0_attn_b_qkv"], 3)
    quad = lambda w: w.reshape(D, QUADS, P)
    per_part = lambda v: v.reshape(-1, P).T
    a = {
        "x": x["x"].reshape(T, D),
        "cols": cols(x),
        "w_qkv": np.stack([rows(np.concatenate([quad(w)[:, i] for w in (wq, wk, wv)], axis=1)) for i in range(QUADS)]),
        "b_qk": np.stack([np.stack([bq[P * i:P * (i + 1)], bk[P * i:P * (i + 1)]], axis=1) for i in range(QUADS)]),
        "b_v": np.stack([np.broadcast_to(bv[P * i:P * (i + 1)], (P, P)) for i in range(QUADS)]),
        "w_out": x["L0_attn_w_out"].T.reshape(QUADS, P, D),
        "bout": np.broadcast_to(x["L0_attn_b_out"], (P, D)),
    }
    xa = lambda name: x["L0_xattn_" + name]
    heads = lambda w: w.T.reshape(D, GROUPS, -1)
    wkx, wvx = np.split(xa("w_kv_x"), 2)
    wp = xa("wproj").T.reshape(2, GROUPS, HPG * DH, D)
    one = [np.concatenate([heads(xa(n)) for n in ("wq", "wqx")], axis=2),
           np.concatenate([heads(w) for w in (xa("wk"), xa("wv"), wkx, wvx)], axis=2)]
    a["w_group"] = np.stack([np.stack([rows(one[0][:, g]), rows(one[1][:, g]),
                                       rows(wp[:, g].reshape(KINDS * DH, D))]) for g in range(GROUPS)])
    for name in ("gate", "up", "down"):
        a[name] = np.stack([rows(w.T) for w in x["L0_ffn_" + name + "_w"]])
    a["router"] = rows(x["L0_ffn_router_w"].T)
    a["ctx"] = x["ctx_2048"].transpose(2, 0, 1).reshape(KT, P, B * SX)
    return {k: c(v) for k, v in a.items()}


def cols(x):
    xa = lambda name: x["L0_xattn_" + name]
    per_part = lambda v: v.reshape(-1, P).T
    smooth = xa("proj_smooth").reshape(2, GROUPS, HPG, P).transpose(3, 1, 0, 2).reshape(P, GROUPS * KINDS)
    return np.concatenate(
        [per_part(xa("ln_w")), per_part(xa("ln_b"))]
        + [per_part(xa(n + "_in_scale")) for n in ("q", "qx", "k", "v")]
        + [per_part(xa(n)) for h in ("qln", "kln", "qxln", "kxln") for n in (h + "_w", h + "_b")]
        + [smooth]
        + [np.broadcast_to(xa(n).reshape(1, 1), (P, 1))
           for n in ("wq_scale", "wqx_scale", "wk_scale", "wv_scale", "proj_in_scale", "proj_w_scale")], axis=1)


def kernel(**inputs):
    import concourse.bacc as bacc
    from concourse.bass_utils import run_bass_kernel_spmd

    nc = bacc.Bacc("TRN2", target_bir_lowering=False, num_devices=1)
    arrays, args = {}, {}
    for name, a in pack({k: np.asarray(v) for k, v in inputs.items()}).items():
        arrays[f"in_{name}"] = a
        args[name] = nc.dram_tensor(f"in_{name}", a.shape, mybir.dt.from_np(a.dtype), kind="ExternalInput").ap()
    out = nc.dram_tensor("out", (B, S, D), F32, kind="ExternalOutput").ap()
    build(nc, args, out)
    r = run_bass_kernel_spmd(nc, [arrays], core_ids=[0])
    return r.results[0]["out"]
```

```python
from contextlib import ExitStack

import numpy as np
import concourse.bass as bass
from concourse import mybir

ALU = mybir.AluOpType
ACT = mybir.ActivationFunctionType
AX = mybir.AxisListType
F32 = mybir.dt.float32
F16 = mybir.dt.float16
BF16 = mybir.dt.bfloat16
I32 = mybir.dt.int32
U16 = mybir.dt.uint16

P = 128
B, S, D = 2, 512, 512
T = B * S
NT = T // P
BT = S // P
KT = D // P
WS = 64.0
EPS = 1e-5
RSQRT_SEED = float(0x5F3759DF)
NEWTON = 3
RSQRT_STEPS = 3 + 3 * NEWTON

HD = 32
QUADS = 4
HQ = 4
SCALE_A = 1.0 / float(np.sqrt(HD))
UA = HQ * BT
TURN, PARTS, PV = 2, 3, 4
SLOT_Q, SLOT_K, SLOT_T, SLOT_V, SLOT_Y = (0, 1), (2, 3), 7, (5, 6), (10, 11, 12, 13)


def rsqrt(dve, sem, base, var, half, out, tmp):
    k = 0

    def step(ins):
        nonlocal k
        ins.then_inc(sem, 1)
        k += 1
        dve.wait_ge(sem, base + k)

    step(dve.tensor_scalar(half, var, EPS, None, ALU.add))
    step(dve.tensor_scalar(tmp.bitcast(I32), half.bitcast(I32), 1, None, ALU.arith_shift_right))
    step(dve.tensor_scalar(out.bitcast(I32), tmp.bitcast(I32), -1.0, RSQRT_SEED, ALU.mult, ALU.add))
    for _ in range(NEWTON):
        step(dve.tensor_tensor(tmp, out, out, ALU.mult))
        step(dve.scalar_tensor_tensor(out=tmp, in0=tmp, scalar=-0.5, in1=half, op0=ALU.mult, op1=ALU.mult))
        step(dve.scalar_tensor_tensor(out=out, in0=tmp, scalar=1.5, in1=out, op0=ALU.add, op1=ALU.mult))
    assert k == RSQRT_STEPS


def after(eng, sem, count):
    if not isinstance(count, int) or count > 0:
        eng.wait_ge(sem, count)


def alone(eng, passed):
    def wait(sem, count):
        after(eng, sem, count)
        if not isinstance(count, int):
            eng.sem_inc(passed)
    return wait


def build(nc, ins, out):
    x_d = ins["x"].rearrange("(t p) d -> t p d", p=P)
    out_d = out.rearrange("b (t p) d -> (b t) p d", p=P)
    top = ExitStack()

    def sem(name):
        return top.enter_context(nc.semaphore(name))

    def sbuf(ctx, name, shape, dt):
        return ctx.enter_context(nc.sbuf_tensor(name, shape, dt))

    with top:
        bank = top.enter_context(nc.psum_tensor("bank", [P, 8, 512], F32))
        X = sbuf(top, "X", [P, NT, D], F32)
        ident = sbuf(top, "ident", [P, P], F32)
        cols = sbuf(top, "cols", [P, ins["cols"].shape[1]], F32)
        rows3 = norm_rows(sem, lambda n, s, d: sbuf(top, n, s, d), "n3")

        with ExitStack() as ctx:
            rows2 = norm_rows(sem, lambda n, s, d: sbuf(ctx, n, s, d), "n2")
            rcols = sbuf(ctx, "rcols", [P, COLS], F32)
            cxh = sbuf(ctx, "cxh", [P, KT, B * SX], F16)
            cxl = sbuf(ctx, "cxl", [P, KT, B * SX], F16)
            gw = [sbuf(ctx, f"x{x}", [P, KT, S], F16) for x in ("w1h", "w1l", "w2h", "w2l")]
            with ExitStack() as c1:
                XTh = sbuf(c1, "XTh", [P, KT, T], F16)
                XTl = sbuf(c1, "XTl", [P, KT, T], F16)
                w = quad_weights(sem, lambda n, s, d: sbuf(c1, n, s, d))
                with ExitStack() as c2:
                    first_norm(nc, ins, sem, lambda n, s, d: sbuf(c2, n, s, d), bank, X, ident, cols, XTh, XTl, x_d, w)
                with ExitStack() as c2:
                    causal_attention(nc, ins, sem, lambda n, s, d: sbuf(c2, n, s, d), bank, X, ident, cols, XTh, XTl,
                                     w, cxh, cxl, gw, rows2)
            xq = sbuf(ctx, "xq", [P, 4, KT, T], F16)
            with ExitStack() as c2:
                second_norm(nc, ins, sem, lambda n, s, d: sbuf(c2, n, s, d), bank, X, ident, cols, xq, rcols,
                            rows2)
            with ExitStack() as c2:
                group_attention(nc, ins, sem, lambda n, s, d: sbuf(c2, n, s, d), bank, X, ident, cols, rcols, xq, cxh,
                                cxl, gw, rows3)
        with ExitStack() as ctx:
            experts(nc, ins, sem, lambda n, s, d: sbuf(ctx, n, s, d), bank, X, ident, out_d, rows3)


class quad_weights:

    def __init__(self, sem, sb):
        self.raw = sb("wraw", [P, KT, 3 * P], F32)
        self.h, self.l = sb("wh", [P, KT, 3 * P], F16), sb("wl", [P, KT, 3 * P], F16)
        self.loaded, self.hi, self.lo = sem("a_w_in"), sem("a_w_hi"), sem("a_w_lo")

    def load(self, sp, src):
        sp.dma_start(self.raw[:], src.rearrange("a p k n -> p (a k) n")).then_inc(self.loaded, 16)

    def split_hi(self, pool):
        pool.tensor_scalar(self.h[:], self.raw[:], WS, 1.0, ALU.mult, ALU.mult).then_inc(self.hi, 1)

    def split_lo(self, dve, i):
        dve.wait_ge(self.hi, i + 1)
        dve.scalar_tensor_tensor(out=self.l[:], in0=self.raw[:], scalar=WS, in1=self.h[:], op0=ALU.mult,
                                 op1=ALU.subtract).then_inc(self.lo, 1)


def group_split_ops(cols, chunk):
    if chunk == 1:
        return [(k, k, slice(256 * s, 256 * (s + 1)), cols[:, C_IN + 4 * s + k:C_IN + 4 * s + k + 1])
                for k in range(KT) for s in range(2)]
    if chunk == 2:
        return [x for k in range(KT) for x in
                [(k, k, slice(DH * s, DH * (s + 1)), cols[:, C_IN + 8 + 4 * s + k:C_IN + 9 + 4 * s + k])
                 for s in range(2)] + [(k, k, slice(2 * DH, 4 * DH), WS)]]
    return [(k, k, slice(0, S), 1.0) for k in range(KT)]


def first_norm(nc, ins, sem, sb, bank, X, ident, cols, XTh, XTl, x_d, w):
    x_in = [sem(f"x_in{t}") for t in range(NT)]
    cols_in = sem("cols_in")
    id_set = sem("id_set")
    rows = norm_rows(sem, sb, "n1")
    tiles = norm_tiles(sem, sb, "n1", rows)
    with nc.Block() as block:
        @block.sync
        def _(sp):
            for t in range(NT):
                sp.dma_start(X[:, t, :], x_d[t]).then_inc(x_in[t], 16)
            w.load(sp, ins["w_qkv"][0:1])
            sp.dma_start(cols[:], ins["cols"]).then_inc(cols_in, 16)
            sp.wait_ge(cols_in, 16)

        @block.gpsimd
        def _(pool):
            pool.memset(ident[:], 0.0).then_inc(id_set, 1)
            pool.wait_ge(id_set, 1)
            pool.affine_select(out=ident[:], in_=ident[:], compare_op=ALU.not_equal, fill=1.0, base=0,
                               pattern=[[-1, P]], channel_multiplier=1).then_inc(id_set, 1)
            pool.wait_ge(w.loaded, 16)
            w.split_hi(pool)

        @block.vector
        def _(dve):
            norm_stats(dve, rows, X, lambda t: dve.wait_ge(x_in[t], 16))
            w.split_lo(dve, 0)
            norm_lo(dve, tiles, XTh, XTl, bank)

        @block.scalar
        def _(act):
            norm_scalar(act, tiles, X, XTh, bank)

        @block.tensor
        def _(pe):
            pe.wait_ge(id_set, 2)
            norm_tensor(pe, tiles, bank, ident)


class norm_rows:

    def __init__(self, sem, sb, tag):
        self.stats = sb(f"stats_{tag}", [P, NT, 6], F32)
        self.mv = sb(f"mv_{tag}", [P, NT, 2], F32)
        self.half = sb(f"half_{tag}", [P, NT], F32)
        self.tmp = sb(f"tmp_{tag}", [P, NT], F32)
        self.rstd = sb(f"rstd_{tag}", [P, NT], F32)
        self.shift = sb(f"shift_{tag}", [P, NT], F32)
        self.s_stats = sem(f"{tag}_stats")
        self.s_mv = sem(f"{tag}_mv")
        self.s_rsqrt = sem(f"{tag}_rsqrt")
        self.s_shift = sem(f"{tag}_shift")


class norm_tiles:

    def __init__(self, sem, sb, tag, rows):
        self.rstd, self.shift, self.s_shift = rows.rstd, rows.shift, rows.s_shift
        self.xn = sb(f"xn_{tag}", [P, NT, D], F32)
        self.s_xn = sem(f"{tag}_xn")
        self.s_turned = sem(f"{tag}_turned")
        self.s_hi = sem(f"{tag}_hi")
        self.s_lo = sem(f"{tag}_lo")


def norm_stats(dve, n, src, arrived, use=0):
    for t in range(NT):
        arrived(t)
        tile_stats(dve, n, src, t)
        if (t + 1) % BT == 0:
            finish_stats(dve, n, t // BT, use)


def tile_stats(dve, n, src, t):
    dve.bn_stats(n.stats[:, t, :], src[:, t, :]).then_inc(n.s_stats, 1)


def finish_stats(dve, n, b, use=0):
    tiles = slice(BT * b, BT * (b + 1))
    for t in range(BT * b, BT * (b + 1)):
        dve.wait_ge(n.s_stats, NT * use + t + 1)
        dve.bn_aggr(n.mv[:, t, :], n.stats[:, t, :]).then_inc(n.s_mv, 1)
    dve.wait_ge(n.s_mv, NT * use + BT * (b + 1))
    rsqrt(dve, n.s_rsqrt, RSQRT_STEPS * (B * use + b), n.mv[:, tiles, 1], n.half[:, tiles], n.rstd[:, tiles],
          n.tmp[:, tiles])
    dve.scalar_tensor_tensor(out=n.shift[:, tiles], in0=n.mv[:, tiles, 0], scalar=-1.0, in1=n.rstd[:, tiles],
                             op0=ALU.mult, op1=ALU.mult).then_inc(n.s_shift, 1)


def norm_lo(dve, n, XTh, XTl, bank):
    for t in range(NT):
        dve.wait_ge(n.s_hi, t + 1)
        dve.tensor_tensor(XTl[:, :, t * P:(t + 1) * P], bank[:, t % 2, :].rearrange("p (k c) -> p k c", k=KT),
                          XTh[:, :, t * P:(t + 1) * P], ALU.subtract).then_inc(n.s_lo, 1)


def norm_scalar(act, n, X, XTh, bank):
    for b in range(B):
        tiles = range(BT * b, BT * (b + 1))
        act.wait_ge(n.s_shift, b + 1)
        for t in tiles:
            act.activation(n.xn[:, t, :], X[:, t, :], ACT.Identity, scale=n.rstd[:, t:t + 1],
                           bias=n.shift[:, t:t + 1]).then_inc(n.s_xn, 1)
        for t in tiles:
            act.wait_ge(n.s_turned, t + 1)
            act.activation(XTh[:, :, t * P:(t + 1) * P], bank[:, t % 2, :].rearrange("p (k c) -> p k c", k=KT),
                           ACT.Copy).then_inc(n.s_hi, 1)


def norm_tensor(pe, n, bank, ident):
    for t in range(NT):
        pe.wait_ge(n.s_xn, t + 1)
        if t >= 2:
            pe.wait_ge(n.s_lo, t - 1)
        for k in range(KT):
            ins = pe.transpose(bank[:, t % 2, k * P:(k + 1) * P], n.xn[:, t, k * P:(k + 1) * P], ident[:])
        ins.then_inc(n.s_turned, 1)


def three(pe, ps, ah, al, bh, bl, start, stop):
    pe.matmul(ps, ah, bh, start=start, stop=False)
    pe.matmul(ps, al, bh, start=False, stop=False)
    return pe.matmul(ps, ah, bl, start=False, stop=stop)


def causal_attention(nc, ins, sem, sb, bank, X, ident, cols, XTh, XTl, w, cxh, cxl, gw, rows2):
    STEPS = QUADS * B
    wh, wl, w_in, w_hi, w_lo = w.h, w.l, w.loaded, w.hi, w.lo
    craw = [sb(f"craw{i}", [P, B * SX], F32) for i in range(2)]
    gwraw = [sb(f"gwraw{i}", [P, KT, S], F32) for i in range(2)]
    woraw = sb("woraw", [P, D], F32)
    woh, wol = sb("woh", [P, D], F16), sb("wol", [P, D], F16)
    qkb = sb("qkb", [P, 2], F32)
    vb = sb("vb", [P, P], F32)
    bout = sb("bout", [P, D], F32)
    identb, mask = sb("identb", [P, P], BF16), sb("mask", [P, P], BF16)
    qf, kf, vf, af = (sb(x, [P, S], F32) for x in ("qf", "kf", "vf", "af"))
    qh, ql, kh, kl = ([sb(f"{x}{b}", [P, S], F16) for b in range(B)] for x in ("qh", "ql", "kh", "kl"))
    vh = [sb(f"vh{b}", [P, BT, P], F16) for b in range(B)]
    vl = [sb(f"vl{b}", [P, BT, P], F16) for b in range(B)]
    ao = [sb(f"ao{b}", [P, BT, P], F32) for b in range(B)]
    aoh, aol = sb("aoh", [P, S], F16), sb("aol", [P, S], F16)
    prob = [sb(f"prob{i}", [P, S], F32) for i in range(4)]
    pth = [sb(f"pth{i}", [P, S], F16) for i in range(4)]
    ptl = [sb(f"ptl{i}", [P, S], F16) for i in range(4)]
    nm, rs, ri = (sb(x, [P, UA], F32) for x in ("nm", "rs", "ri"))
    qbias = sb("qbias", [P, 1], F32)
    J_Q, J_K, J_T, J_V, J_Y = 1, 0, 1, 0, (1, 0, 1, 0)
    SC, PT, O, J = ([bank[:, i, :], bank[:, i + 1, :]] for i in (0, 2, 4, 6))

    passed_sp, passed_pool = sem("a_passed_sp"), sem("a_passed_pool")
    wo_in, b_in, c_in = sem("a_wo_in"), sem("a_b_in"), sem("a_c_in")
    ctx_in = [sem(f"a_ctx_in{i}") for i in range(2)]
    ctx_hi, ctx_lo, gw_in, gw_hi, gw_lo = (sem(f"a_{x}") for x in ("ctx_hi", "ctx_lo", "gw_in", "gw_hi", "gw_lo"))
    set_up = sem("a_set_up")
    wo_hi, wo_lo = sem("a_wo_hi"), sem("a_wo_lo")
    q_ps, k_ps, v_ps, t_ps, y_ps = (sem(f"a_{x}_ps") for x in ("q", "k", "v", "t", "y"))
    q_f, k_f, v_f, t_f, y_f = (sem(f"a_{x}_f") for x in ("q", "k", "v", "t", "y"))
    q_h, k_h, v_h, t_h = (sem(f"a_{x}_h") for x in ("q", "k", "v", "t"))
    q_l, k_l, v_l, t_l = (sem(f"a_{x}_l") for x in ("q", "k", "v", "t"))
    bias_x, q_bias = sem("a_bias_x"), sem("a_q_bias")
    scored, maxed, exped, turned, hi, lo, pved, recip, o_f = (
        sem(f"a_{x}") for x in ("scored", "maxed", "exped", "turned", "hi", "lo", "pved", "recip", "o_f"))

    def loop(eng, body):
        body(0, first=True, last=False)
        with eng.Fori(1, QUADS - 1) as i:
            body(i, first=False, last=False)
        body(QUADS - 1, first=False, last=True)

    with nc.Block() as block:
        @block.sync
        def _(sp):
            wait = alone(sp, passed_sp)
            sp.dma_start(bout[:], ins["bout"]).then_inc(c_in, 16)

            def load_w(i, used):
                if used:
                    wait(w_lo, i)
                    wait(v_f, 2 * i)
                    wait(k_f, 2 * i)
                    wait(q_f, 2 * i)
                    w.load(sp, ins["w_qkv"][bass.ds(i, 1)])
                sp.dma_start(qkb[:], ins["b_qk"][bass.ds(i, 1)].rearrange("a p n -> p (a n)")).then_inc(b_in, 16)
                sp.dma_start(vb[:], ins["b_v"][bass.ds(i, 1)].rearrange("a p n -> p (a n)")).then_inc(b_in, 16)

            def load_wo(i, used):
                if used:
                    wait(wo_lo, i)
                sp.dma_start(woraw[:], ins["w_out"][bass.ds(i, 1)].rearrange("a p n -> p (a n)")).then_inc(wo_in, 16)

            load_w(0, False)
            load_wo(0, False)

            def load_ctx(k):
                if k >= 2:
                    sp.wait_ge(ctx_lo, k - 1)
                sp.dma_start(craw[k % 2][:], ins["ctx"][k]).then_inc(ctx_in[k % 2], 16)

            for c in range(2):
                sp.dma_start(gwraw[c][:], ins["w_group"][0:1, c].rearrange("a p k n -> p (a k) n")).then_inc(gw_in, 16)
            load_ctx(0)
            load_ctx(1)

            def body(i, first, last):
                if not last:
                    load_w(i + 1, True)
                    load_wo(i + 1, True)
                if first:
                    load_ctx(2)
                    load_ctx(3)

            loop(sp, body)

        @block.gpsimd
        def _(pool):
            wait = alone(pool, passed_pool)
            pool.memset(identb[:], 0.0).then_inc(set_up, 1)
            pool.memset(mask[:], 0.0).then_inc(set_up, 1)
            pool.wait_ge(set_up, 2)
            pool.affine_select(out=identb[:], in_=identb[:], compare_op=ALU.not_equal, fill=1.0, base=0,
                               pattern=[[-1, P]], channel_multiplier=1).then_inc(set_up, 1)
            pool.affine_select(out=mask[:], in_=mask[:], compare_op=ALU.is_ge, fill=-1e30, base=0,
                               pattern=[[-1, P]], channel_multiplier=1).then_inc(set_up, 1)

            def cast(dst, src, scale, done):
                pool.tensor_scalar(dst, src, scale, 1.0, ALU.mult, ALU.mult).then_inc(done, 1)

            def weights(i):
                wait(w_in, 16 * (i + 1))
                wait(v_ps, 2 * i)
                w.split_hi(pool)

            def out_weights(i, used):
                wait(wo_in, 16 * (i + 1))
                if used:
                    wait(y_ps, 4 * 2 * i)
                cast(woh[:], woraw[:], WS, wo_hi)

            def split(n, used, ready, src, h, l, h_done, l_done, free, free_at):
                wait(ready, n + 1)
                if used:
                    wait(free, free_at)
                cast(h, src[:], 1.0, h_done)
                wait(h_done, n + 1)
                pool.tensor_tensor(l, src[:], h, ALU.subtract).then_inc(l_done, 1)

            def project(n, b, used):
                split(n, used, q_f, qf, qh[b][:], ql[b][:], q_h, q_l, scored, UA * (n - 1))
                split(n, used, k_f, kf, kh[b][:], kl[b][:], k_h, k_l, scored, UA * (n - 1))

            def values(n, b, used):
                vhf, vlf = (x[b][:].rearrange("p k c -> p (k c)") for x in (vh, vl))
                split(n, used, v_f, vf, vhf, vlf, v_h, v_l, pved, UA * (n - 1))

            def outputs(n, used):
                split(n, used, t_f, af, aoh[:], aol[:], t_h, t_l, y_ps, 4 * n)

            out_weights(0, False)
            project(0, 0, False)
            values(0, 0, False)

            def group_weights_hi():
                pool.wait_ge(gw_in, 32)
                for c in range(2):
                    for _, k, part, scale in group_split_ops(cols, c + 1):
                        pool.tensor_scalar(gw[2 * c][:, k, part], gwraw[c][:, k, part], scale, 1.0, ALU.mult,
                                           ALU.mult).then_inc(gw_hi, 1)

            def context(k):
                pool.wait_ge(ctx_in[k % 2], 16 * (k // 2 + 1))
                cast(cxh[:, k, :], craw[k % 2][:], 1.0, ctx_hi)
                pool.wait_ge(ctx_hi, k + 1)
                pool.tensor_tensor(cxl[:, k, :], craw[k % 2][:], cxh[:, k, :], ALU.subtract).then_inc(ctx_lo, 1)

            def body(i, first, last):
                project(2 * i + 1, 1, not first)
                values(2 * i + 1, 1, not first)
                if not first:
                    outputs(2 * i - 1, True)
                if not last:
                    weights(i + 1)
                if first:
                    group_weights_hi()
                else:
                    out_weights(i, True)
                if not last:
                    project(2 * i + 2, 0, True)
                if not last:
                    values(2 * i + 2, 0, True)
                outputs(2 * i, not first)
                if first:
                    context(0)
                    context(1)
                if last:
                    context(2)
                    context(3)

            loop(pool, body)
            outputs(STEPS - 1, True)

        @block.scalar
        def _(act):
            def projected(n, used, ready, j, dst, scale, bias, done, l_done):
                act.wait_ge(ready, n + 1)
                if used:
                    act.wait_ge(l_done, n)
                act.activation(dst[:], J[j], ACT.Identity, scale=scale, bias=bias).then_inc(done, 1)

            def project_q(n, nq, used):
                act.wait_ge(b_in, 32 * (nq + 1))
                act.activation(qbias[:], qkb[:, 0:1], ACT.Copy, scale=SCALE_A).then_inc(q_bias, 1)
                act.wait_ge(q_bias, n + 1)
                projected(n, used, q_ps, J_Q, qf, SCALE_A / WS, qbias[:], q_f, q_l)

            def project_k(n, used):
                projected(n, used, k_ps, J_K, kf, 1.0 / WS, qkb[:, 1:2], k_f, k_l)

            def out_turned(n, used):
                act.wait_ge(t_ps, n + 1)
                if used:
                    act.wait_ge(t_l, n)
                act.activation(af[:], J[J_T], ACT.Copy).then_inc(t_f, 1)

            def exp(U, u, used):
                L = P * (u % BT + 1)
                act.wait_ge(maxed, U + 1)
                if used:
                    act.wait_ge(turned, U - 3)
                act.activation(prob[u % 4][:, 0:L], SC[u % 2][:, 0:L], ACT.Exp, bias=nm[:, u:u + 1],
                               accum_out=rs[:, u:u + 1]).then_inc(exped, 1)

            def part_hi(U, u, used):
                L = P * (u % BT + 1)
                act.wait_ge(turned, U + 1)
                if used:
                    act.wait_ge(pved, U - 3)
                act.activation(pth[u % 4][:, 0:L], PT[u % 2][:, 0:L], ACT.Copy).then_inc(hi, 1)

            project_q(0, 0, False)
            project_k(0, False)

            def body(i, first, last):
                step(i, 2 * i, first, False, first)
                step(i + 1, 2 * i + 1, False, last, first)

            def step(nq, n, first, last, first_quad):
                for u in range(UA):
                    U = UA * n + u
                    if not (first and u < PARTS):
                        part_hi(U - PARTS, u - PARTS, not (first and u - PARTS < 4))
                    exp(U, u, not (first and u < 4))
                    if u == SLOT_Q[-1] and not last:
                        project_q(n + 1, nq, True)
                    if u == SLOT_K[-1] and not last:
                        project_k(n + 1, True)
                    if u == SLOT_T and not first:
                        out_turned(n - 1, not first_quad)

            loop(act, body)
            end = UA * STEPS
            for U in range(end - PARTS, end):
                part_hi(U, U % UA, True)
            out_turned(STEPS - 1, True)

        @block.vector
        def _(dve):
            dve.wait_ge(c_in, 16)
            for t in range(NT):
                dve.tensor_tensor(X[:, t, :], X[:, t, :], bout[:], ALU.add).then_inc(bias_x, 1)

            def low(dst, raw, h, h_done, l_done, i):
                dve.wait_ge(h_done, i + 1)
                dve.scalar_tensor_tensor(out=dst[:], in0=raw[:], scalar=WS, in1=h[:], op0=ALU.mult,
                                         op1=ALU.subtract).then_inc(l_done, 1)

            def values(n, used, nq):
                dve.wait_ge(v_ps, n + 1)
                dve.wait_ge(b_in, 32 * (nq + 1))
                if used:
                    dve.wait_ge(v_l, n)
                dve.scalar_tensor_tensor(out=vf[:].rearrange("p (k c) -> p k c", k=BT),
                                         in0=J[J_V].rearrange("p (k c) -> p k c", k=BT), scalar=1.0 / WS,
                                         in1=vb[:].unsqueeze(1).broadcast_to([P, BT, P]),
                                         op0=ALU.mult, op1=ALU.add).then_inc(v_f, 1)

            def maxima(U, u):
                dve.wait_ge(scored, U + 1)
                dve.tensor_reduce(nm[:, u:u + 1], SC[u % 2][:, 0:P * (u % BT + 1)], AX.X, ALU.max,
                                  negate=True).then_inc(maxed, 1)

            def part_lo(U, u):
                L = P * (u % BT + 1)
                dve.wait_ge(hi, U + 1)
                dve.tensor_tensor(ptl[u % 4][:, 0:L], PT[u % 2][:, 0:L], pth[u % 4][:, 0:L],
                                  ALU.subtract).then_inc(lo, 1)

            def normalise(n, b, h, used):
                mine = slice(BT * h, BT * (h + 1))
                dve.wait_ge(exped, UA * n + BT * (h + 1))
                dve.reciprocal(ri[:, mine], rs[:, mine]).then_inc(recip, 1)
                dve.wait_ge(recip, HQ * n + h + 1)
                dve.wait_ge(pved, UA * n + BT * (h + 1))
                if used and h == 0:
                    dve.wait_ge(t_ps, n - 1)
                dve.tensor_tensor(ao[b][:, :, h * HD:(h + 1) * HD],
                                  O[h % 2][:, 0:BT * HD].rearrange("p (t c) -> p t c", t=BT),
                                  ri[:, mine].unsqueeze(2).broadcast_to([P, BT, HD]), ALU.mult).then_inc(o_f, 1)

            def project_out(n, t, b):
                dve.wait_ge(y_ps, 4 * n + t + 1)
                if isinstance(n, int) and n < 2 and t == 0:
                    dve.wait_ge(bias_x, NT)
                dve.scalar_tensor_tensor(out=X[:, BT * b + t, :], in0=J[J_Y[t]], scalar=1.0 / WS,
                                         in1=X[:, BT * b + t, :], op0=ALU.mult, op1=ALU.add).then_inc(y_f, 1)

            low(wol, woraw, woh, wo_hi, wo_lo, 0)
            values(0, False, 0)

            def step(i, n, b, first, last, first_quad, last_quad):
                for u in range(UA):
                    U = UA * n + u
                    maxima(U, u)
                    if not (first and u < PARTS):
                        part_lo(U - PARTS, u - PARTS)
                    if u % BT == (PV + 1) % BT:
                        h = (u - PV - 1) // BT - 1
                        if h >= 0:
                            normalise(n, b, h, not first_quad)
                        elif not first:
                            normalise(n - 1, 1 - b, h + HQ, not first_quad)
                    if u in SLOT_Y and not first:
                        project_out(n - 1, SLOT_Y.index(u), 1 - b)
                    if u == SLOT_V[-1] and not last:
                        values(n + 1, True, i + b)
                    if first_quad and b == 1 and u in GROUP_WEIGHTS_AT:
                        group_weights_lo(GROUP_WEIGHTS_AT.index(u))
                    if u == UA - 2 and b == 0 and not last_quad:
                        w.split_lo(dve, i + 1)
                    if u == UA - 1 and b == 0 and not first:
                        low(wol, woraw, woh, wo_hi, wo_lo, i)

            GROUP_WEIGHTS_AT = (1, 2, 3, 5, 6, 7, 14, 15)

            def group_weights_lo(p):
                c = p // KT
                ops = group_split_ops(cols, c + 1)
                before = 0 if c == 0 else len(group_split_ops(cols, 1))
                for j, (piece, k, part, scale) in enumerate(ops):
                    if piece == p % KT:
                        dve.wait_ge(gw_hi, before + j + 1)
                        dve.scalar_tensor_tensor(out=gw[2 * c + 1][:, k, part], in0=gwraw[c][:, k, part], scalar=scale,
                                                 in1=gw[2 * c][:, k, part], op0=ALU.mult,
                                                 op1=ALU.subtract).then_inc(gw_lo, 1)

            def body(i, first, last):
                step(i, 2 * i, 0, first, False, first, last)
                step(i, 2 * i + 1, 1, False, last, first, last)

            loop(dve, body)
            end = UA * STEPS
            for U in range(end - PARTS, end):
                part_lo(U, U % UA)
            for h in range(HQ - 2, HQ):
                normalise(STEPS - 1, 1, h, True)
            dve.wait_ge(y_f, 4 * (STEPS - 1))
            for t in range(BT):
                tile_stats(dve, rows2, X, t)
            finish_stats(dve, rows2, 0)
            for t in range(BT):
                project_out(STEPS - 1, t, 1)
            for t in range(BT):
                dve.wait_ge(y_f, 4 * (STEPS - 1) + t + 1)
                tile_stats(dve, rows2, X, BT + t)
            finish_stats(dve, rows2, 1)

        @block.tensor
        def _(pe):
            def projection(b, j, first_col, done, part=(0, 1)):
                for k in range(KT):
                    if k // (KT // 2) not in part:
                        continue
                    w = slice(first_col, first_col + P)
                    ins_ = three(pe, J[j], wh[:, k, w], wl[:, k, w], XTh[:, k, S * b:S * (b + 1)],
                                 XTl[:, k, S * b:S * (b + 1)], k == 0, k == KT - 1)
                    if k == KT - 1:
                        ins_.then_inc(done, 1)

            def values(b, part=(0, 1)):
                for t in range(BT):
                    if t // (BT // 2) not in part:
                        continue
                    tok = slice(S * b + P * t, S * b + P * (t + 1))
                    for k in range(KT):
                        ins_ = three(pe, J[J_V][:, P * t:P * (t + 1)], XTh[:, k, tok], XTl[:, k, tok],
                                     wh[:, k, 2 * P:3 * P], wl[:, k, 2 * P:3 * P], k == 0, k == KT - 1)
                    if t == BT - 1:
                        ins_.then_inc(v_ps, 1)

            def scores(n, U, u, b, used):
                h, qt = u // BT, u % BT
                L = P * (qt + 1)
                if u == 0:
                    pe.wait_ge(q_l, n + 1)
                    pe.wait_ge(k_l, n + 1)
                if used:
                    pe.wait_ge(exped, U - 1)
                head = slice(HD * h, HD * (h + 1))
                q = slice(P * qt, P * (qt + 1))
                three(pe, SC[u % 2][:, 0:L], qh[b][head, q], ql[b][head, q], kh[b][head, 0:L], kl[b][head, 0:L],
                      True, False)
                pe.matmul(SC[u % 2][:, L - P:L], identb[:], mask[:], start=False, stop=True).then_inc(scored, 1)

            def turn(U, u, used):
                pe.wait_ge(exped, U + 1)
                if used:
                    pe.wait_ge(lo, U - 1)
                for k in range(u % BT + 1):
                    ins_ = pe.transpose(PT[u % 2][:, P * k:P * (k + 1)], prob[u % 4][:, P * k:P * (k + 1)], ident[:])
                ins_.then_inc(turned, 1)

            def pv(n, U, u, b, used):
                u = u % UA
                h, qt = u // BT, u % BT
                if u == 0:
                    pe.wait_ge(v_l, n + 1)
                pe.wait_ge(lo, U + 1)
                if used and qt == 0:
                    pe.wait_ge(o_f, HQ * n + h - 1)
                for k in range(qt + 1):
                    ins_ = three(pe, O[h % 2][:, HD * qt:HD * (qt + 1)], pth[u % 4][:, P * k:P * (k + 1)],
                                 ptl[u % 4][:, P * k:P * (k + 1)], vh[b][:, k, HD * h:HD * (h + 1)],
                                 vl[b][:, k, HD * h:HD * (h + 1)], k == 0, k == qt)
                ins_.then_inc(pved, 1)

            def turn_out(n, b):
                pe.wait_ge(o_f, HQ * (n + 1))
                for t in range(BT):
                    ins_ = pe.transpose(J[J_T][:, P * t:P * (t + 1)], ao[b][:, t, :], ident[:])
                ins_.then_inc(t_ps, 1)

            def project_out(n, t):
                if t == 0:
                    pe.wait_ge(t_l, n + 1)
                tok = slice(P * t, P * (t + 1))
                three(pe, J[J_Y[t]], aoh[:, tok], aol[:, tok], woh[:], wol[:], True, True).then_inc(y_ps, 1)

            pe.wait_ge(set_up, 4)
            pe.wait_ge(w_lo, 1)
            projection(0, J_Q, 0, q_ps)
            projection(0, J_K, P, k_ps)
            pe.wait_ge(k_f, 1)
            values(0)

            def job(i, n, u, b, first, second, last):
                if u in SLOT_Q and not last:
                    if u == SLOT_Q[0]:
                        if b == 1:
                            pe.wait_ge(w_lo, i + 2)
                        pe.wait_ge(q_f, n + 1)
                        if not (first or second):
                            pe.wait_ge(y_f, 4 * (n - 2) + 3)
                    projection(1 - b, J_Q, 0, q_ps, (SLOT_Q.index(u),))
                if u in SLOT_K and not last:
                    if u == SLOT_K[0]:
                        pe.wait_ge(v_f, n + 1)
                        if not (first or second):
                            pe.wait_ge(y_f, 4 * (n - 1))
                    projection(1 - b, J_K, P, k_ps, (SLOT_K.index(u),))
                if u == SLOT_T and not first:
                    if not last:
                        pe.wait_ge(q_f, n + 2)
                    else:
                        pe.wait_ge(y_f, 4 * (n - 2) + 3)
                    turn_out(n - 1, 1 - b)
                if u in SLOT_V and not last:
                    if u == SLOT_V[0]:
                        pe.wait_ge(k_f, n + 2)
                    values(1 - b, (SLOT_V.index(u),))
                if u in SLOT_Y and not first:
                    t = SLOT_Y.index(u)
                    if t == 0:
                        if b == 1:
                            pe.wait_ge(wo_lo, i + 1)
                        pe.wait_ge(t_f, n)
                    elif t == 1:
                        if not last:
                            pe.wait_ge(v_f, n + 2)
                        else:
                            pe.wait_ge(y_f, 4 * (n - 1))
                    else:
                        pe.wait_ge(y_f, 4 * (n - 1) + t - 1)
                    project_out(n - 1, t)

            def step(i, n, b, first, second, last):
                for u in range(UA):
                    U = UA * n + u
                    scores(n, U, u, b, not (first and u < 2))
                    job(i, n, u, b, first, second, last)
                    if not (first and u < TURN):
                        turn(U - TURN, u - TURN, not (first and u - TURN < 2))
                    if not (first and u < PV):
                        before = 1 if u < PV else 0
                        pv(n - before, U - PV, u - PV, (b + before) % 2, not (first and u - PV < 2 * BT))

            def body(i, first, last):
                step(i, 2 * i, 0, first, False, False)
                step(i, 2 * i + 1, 1, False, first, last)

            loop(pe, body)
            end = UA * STEPS
            for U in range(end, end + PV):
                if U - TURN < end:
                    turn(U - TURN, (U - TURN) % UA, True)
                pv(STEPS - 1, U - PV, (U - PV) % UA, 1, True)
            pe.wait_ge(y_f, 4 * (STEPS - 1))
            turn_out(STEPS - 1, 1)
            for t in range(BT):
                if t == 0:
                    pe.wait_ge(t_f, STEPS)
                else:
                    pe.wait_ge(y_f, 4 * (STEPS - 1) + max(t - 1, 0))
                project_out(STEPS - 1, t)



GROUPS = 8
HPG = 2
DH = 128
SX = 1024
XT = SX // P
SCALE_X = 1.0 / float(np.sqrt(DH))
KINDS = 2 * HPG
UX = KINDS * BT
SELF_U = HPG * BT
PIECES = SELF_U + 2 * (UX - SELF_U)
PAIRS = UX // 2
BLOCKS = KINDS * BT + BT + XT
FP8_MAX = 448.0

C_LNW, C_LNB, C_IN, C_HEAD, C_SMOOTH, C_SCALAR = 0, 4, 8, 24, 32, 64
COLS = 70
SC_Q, SC_QX, SC_K, SC_V, SC_PIN, SC_PW = range(6)


def round_fp8(dve, sem, base, y, unit, total):
    dve.tensor_scalar(y, y, FP8_MAX, -FP8_MAX, ALU.min, ALU.max).then_inc(sem, 1)
    dve.wait_ge(sem, base + 1)
    dve.tensor_scalar(unit.bitcast(U16), y.bitcast(U16), 0x7F80, 0x40, ALU.bitwise_and, ALU.bitwise_or).then_inc(sem, 1)
    dve.wait_ge(sem, base + 2)
    dve.tensor_scalar(unit, unit, 1.5 * 2.0 ** -6, 2.0 ** 20, ALU.max, ALU.mult).then_inc(sem, 1)
    dve.wait_ge(sem, base + 3)
    dve.tensor_tensor(total, y, unit, ALU.add).then_inc(sem, 1)


ROUND_STEPS = 4


def second_norm(nc, ins, sem, sb, bank, X, ident, cols, xq, rcols, rows2):
    n = norm_tiles(sem, sb, "n2", rows2)
    L = [sb(f"L{i}", [P, S], F32) for i in range(2)]
    y = [sb(f"y{i}", [P, 4, S], BF16) for i in range(2)]
    unit = [sb(f"unit{i}", [P, 4, S], BF16) for i in range(2)]
    total = [sb(f"total{i}", [P, 4, S], F32) for i in range(2)]
    s_rcols = sem("b_rcols")
    L_f, y_f, r_dve, r_pool = sem("b_L_f"), sem("b_y_f"), sem("b_r_dve"), sem("b_r_pool")
    with nc.Block() as block:
        @block.scalar
        def _(act):
            for again in range(2):
                for t in range(NT):
                    if t % BT == 0:
                        act.wait_ge(n.s_shift, B * again + t // BT + 1)
                    act.activation(n.xn[:, t, :], (X, n.xn)[again][:, t, :], ACT.Identity, scale=n.rstd[:, t:t + 1],
                                   bias=n.shift[:, t:t + 1]).then_inc(n.s_xn, 1)
            act.wait_ge(s_rcols, 2)
            for j in range(B * KT):
                k = j % KT
                act.wait_ge(n.s_turned, j + 1)
                act.activation(L[j % 2][:], bank[:, j % 2, :], ACT.Identity, scale=cols[:, C_LNW + k:C_LNW + k + 1],
                               bias=cols[:, C_LNB + k:C_LNB + k + 1]).then_inc(L_f, 1)
                act.wait_ge(L_f, j + 1)
                if j >= 2:
                    act.wait_ge(r_dve, ROUND_STEPS * (j - 1))
                for s in range(4):
                    c = C_IN + 4 * s + k
                    act.activation(y[j % 2][:, s, :], L[j % 2][:], ACT.Copy, scale=rcols[:, c:c + 1]).then_inc(y_f, 1)

        @block.vector
        def _(dve):
            for c in (slice(C_IN, C_IN + 4 * KT), slice(C_SMOOTH, C_SMOOTH + GROUPS * KINDS)):
                dve.reciprocal(rcols[:, c], cols[:, c]).then_inc(s_rcols, 1)
            norm_stats(dve, rows2, n.xn, lambda t: dve.wait_ge(n.s_xn, t + 1), use=1)

            for j in range(B * KT):
                dve.wait_ge(y_f, 4 * (j + 1))
                if j >= 2:
                    dve.wait_ge(r_pool, j - 1)
                round_fp8(dve, r_dve, ROUND_STEPS * j, y[j % 2][:], unit[j % 2][:], total[j % 2][:])

        @block.gpsimd
        def _(pool):
            for j in range(B * KT):
                b, k = j // KT, j % KT
                pool.wait_ge(r_dve, ROUND_STEPS * (j + 1))
                pool.tensor_tensor(xq[:, :, k, S * b:S * (b + 1)], total[j % 2][:], unit[j % 2][:],
                                   ALU.subtract).then_inc(r_pool, 1)

        @block.tensor
        def _(pe):
            for j in range(B * KT):
                b, k = j // KT, j % KT
                if k == 0:
                    pe.wait_ge(n.s_xn, NT + BT * (b + 1))
                if j >= 2:
                    pe.wait_ge(L_f, j - 1)
                for t in range(BT):
                    ins_ = pe.transpose(bank[:, j % 2, P * t:P * (t + 1)],
                                        n.xn[:, BT * b + t, P * k:P * (k + 1)], ident[:])
                ins_.then_inc(n.s_turned, 1)


JOBS = ("A0 A1 A2 A3 B0 R3 C0 C1 B1 C2 C3 R0 Y0 Y1 Y2 Y3 R1 T0 T1 T2 T3 T4 T5 T6 R2").split()
SLOT_A = {0: "A0", 1: "A2", 2: "B0", 3: "C0", 4: "B1", 5: "C3", 6: "R0", 7: "Y0", 8: "Y2", 10: "R1", 11: "T1", 12: "T3", 13: "T5"}
SLOT_B = {0: "A1", 1: "A3", 2: "R3", 3: "C1", 4: "C2", 7: "Y1", 8: "Y3", 10: "T0", 11: "T2", 12: "T4",
          13: "T6", 14: "R2"}
APPLY_AT = {7: range(0, BT), 9: range(BT, 10), 10: range(10, 4 * BT)}
POOL_APPLIES = range(4 * BT, BLOCKS)
V_ORDER = ("B0", "C0", "C1", "B1", "C2", "C3")
NEXT = [j for j in JOBS if j[0] in "ABCT"]
LATE = [j for j in JOBS if j[0] == "Y"] + ["R3"]


def jobs_of(first, last):
    return [j for j in JOBS if not (first and j in LATE) and not (last and j in NEXT)]


def job_number(name, n, first=False, last=False, prologue=False):
    if prologue:
        return NEXT.index(name)
    if first:
        return len(NEXT) + jobs_of(True, False).index(name)
    return jobs_before(n) + jobs_of(False, last).index(name)


def jobs_before(n):
    return len(NEXT) - len(LATE) + len(JOBS) * n


def piece_end(u):
    if u < 0:
        return piece_end(u + UX) - PIECES
    return u + 1 if u < SELF_U else SELF_U + 2 * (u + 1 - SELF_U)


def group_attention(nc, ins, sem, sb, bank, X, ident, cols, rcols, xq, cxh, cxl, gw, rows3):
    STEPS = GROUPS * B
    wraw = sb("xwraw", [P, KT, S], F32)
    w1h, w1l, w2h, w2l = gw
    w3h, w3l = (sb(f"x{x}", [P, KT, S], F16) for x in ("w3h", "w3l"))
    qr = sb("qr", [P, BT, 5 * DH], F32)
    kr = sb("kr", [P, XT, DH], F32)
    stats, mv = sb("xstats", [P, BLOCKS, 6], F32), sb("xmv", [P, BLOCKS, 2], F32)
    half, tmp, rstd, shift = (sb(f"x{x}", [P, BLOCKS], F32) for x in ("half", "tmp", "rstd", "shift"))
    ft = [sb(f"ft{i}", [P, S], F32) for i in range(2)]
    vt = [ft[i][:, 0:2 * DH].rearrange("p (t c) -> p t c", t=2) for i in range(2)]
    qh, ql = ([sb(f"x{x}{b}", [P, KINDS, S], F16) for b in range(B)] for x in ("qh", "ql"))
    kh, kl = ([sb(f"x{x}{b}", [P, S], F16) for b in range(B)] for x in ("kh", "kl"))
    kxh, kxl = ([sb(f"{x}{b}", [P, SX], F16) for b in range(B)] for x in ("kxh", "kxl"))
    vh, vl = ([sb(f"x{x}{b}", [P, BT, DH], F16) for b in range(B)] for x in ("vh", "vl"))
    vxh, vxl = ([sb(f"{x}{b}", [P, XT, DH], F16) for b in range(B)] for x in ("vxh", "vxl"))
    prob = [sb(f"xprob{i}", [P, SX], F32) for i in range(2)]
    pth, ptl = ([sb(f"x{x}{i}", [P, XT, 2 * P], F16) for i in range(2)] for x in ("pth", "ptl"))
    nm = sb("xnm", [P, 4], F32)
    hcols = sb("hcols", [P, 8], F32)
    rs, ri = sb("xrs", [P, 2, BT], F32), sb("xri", [P, 2, BT], F32)
    R = sb("R", [P, S], F32)
    y, unit, total = sb("xy", [P, S], BF16), sb("xunit", [P, S], BF16), sb("xtotal", [P, S], F32)
    cat = sb("cat", [P, KINDS, S], F16)
    rsm = sb("rsm", [P, KINDS], F32)
    psc = sb("psc", [P, 1], F32)
    SC = [bank[:, 2 * i:2 * i + 2, :].rearrange("p a c -> p (a c)") for i in range(2)]
    PT, O = [bank[:, 4, :], bank[:, 5, :]], bank[:, 6, :]
    JOB, JOBS_FIRST = bank[:, 7, :], (bank[:, 7, :], O)

    passed_sp, passed_pool, passed_dve = sem("x_passed_sp"), sem("x_passed_pool"), sem("x_passed_dve")
    w_in = sem("x_w_in")
    w_hi, w_lo = sem("x_w_hi"), sem("x_w_lo")
    job_done, job_read = sem("x_job_done"), sem("x_job_read")
    s_stats, s_mv, s_rsqrt, s_shift, applied, applied_pool = (
        sem(f"x_{x}") for x in ("stats", "mv", "rsqrt", "shift", "applied", "applied_pool"))
    t_hi, t_lo, v_hi, v_lo = (sem(f"x_{x}") for x in ("t_hi", "t_lo", "v_hi", "v_lo"))
    scored, maxed, exped, turned, hi, lo, pved, recip = (
        sem(f"x_{x}") for x in ("scored", "maxed", "exped", "turned", "hi", "lo", "pved", "recip"))
    o_read, rounding, rounded, s_rsm, s_psc, s_hcols, y_added = (
        sem(f"x_{x}") for x in ("o_read", "rounding", "rounded", "rsm", "psc", "hcols", "y_added"))
    W1N, W2N, W3N = 2 * KT, 3 * KT, KT
    WN = W1N + W2N + W3N

    def w_base(g):
        return WN * g

    def loop(body):
        def run(eng):
            body(0, True, False)
            with eng.Fori(1, GROUPS - 1) as g:
                body(g, False, False)
            body(GROUPS - 1, False, True)
        return run

    def norm_block(i):
        if i < 5 * BT:
            return qr[:, i % BT, DH * (i // BT):DH * (i // BT + 1)]
        return kr[:, i - 5 * BT, :]

    def split_ops(chunk):
        return group_split_ops(cols, chunk)

    with nc.Block() as block:
        @block.sync
        def _(sp):
            wait = alone(sp, passed_sp)
            def load(chunk, g, before):
                wait(w_lo, before)
                sp.dma_start(wraw[:], ins["w_group"][bass.ds(g, 1), chunk - 1].rearrange("a p k n -> p (a k) n"))\
                    .then_inc(w_in, 16)

            def body(g, first, last):
                if not last:
                    load(1, g + 1, w_base(g))
                    load(2, g + 1, w_base(g) + W1N)
                    load(3, g, w_base(g) + W1N + W2N)
                else:
                    load(3, g, w_base(g))

            loop(body)(sp)

        @block.gpsimd
        def _(pool):
            wait = alone(pool, passed_pool)
            def split_hi(chunk, loaded, free, count, pieces=range(KT)):
                if 0 in pieces:
                    wait(w_in, 16 * loaded)
                    wait(free, count)
                wh = (w1h, w2h, w3h)[chunk - 1]
                for _, k, c, scale in [x for x in split_ops(chunk) if x[0] in pieces]:
                    pool.tensor_scalar(wh[:, k, c], wraw[:, k, c], scale, 1.0, ALU.mult, ALU.mult).then_inc(w_hi, 1)

            def values(name, m, b, job):
                v = V_ORDER.index(name)
                j = int(name[1])
                h, l = (vh, vl) if name[0] == "B" else (vxh, vxl)
                wait(job_read, job + 1)
                wait(pved, PAIRS * (m - 1))
                pool.tensor_scalar(h[b][:, 2 * j:2 * j + 2, :], vt[v % 2], 1.0, 1.0, ALU.mult, ALU.mult)\
                    .then_inc(v_hi, 1)
                wait(v_hi, len(V_ORDER) * m + v + 1)
                pool.tensor_tensor(l[b][:, 2 * j:2 * j + 2, :], vt[v % 2], h[b][:, 2 * j:2 * j + 2, :],
                                   ALU.subtract).then_inc(v_lo, 1)

            def apply(m):
                wait(s_shift, m + 1)
                for i in POOL_APPLIES:
                    pool.tensor_scalar(norm_block(i), norm_block(i), rstd[:, i:i + 1], shift[:, i:i + 1], ALU.mult, ALU.add)\
                        .then_inc(applied_pool, 1)

            def turned_parts(i, m, b, job):
                if i < 4:
                    h, l = qh[b][:, i, :], ql[b][:, i, :]
                elif i == 4:
                    h, l = kh[b][:], kl[b][:]
                else:
                    half_ = slice(S * (i - 5), S * (i - 4))
                    h, l = kxh[b][:, half_], kxl[b][:, half_]
                wait(job_read, job + 1)
                if i == 0:
                    wait(scored, UX * (m - 1))
                pool.tensor_scalar(h, ft[i % 2][:], 1.0, 1.0, ALU.mult, ALU.mult).then_inc(t_hi, 1)
                wait(t_hi, 7 * m + i + 1)
                pool.tensor_tensor(l, ft[i % 2][:], h, ALU.subtract).then_inc(t_lo, 1)

            def project_out(n, t, b, job):
                wait(job_read, job + 1)
                x = X[:, BT * b + t, :]
                pool.tensor_tensor(x, x, ft[t % 2][:], ALU.add).then_inc(y_added, 1)

            def quantised(n, kind, cat_read=0):
                count = KINDS * n + kind + 1
                wait(rounding, ROUND_STEPS * count)
                wait(job_done, cat_read)
                pool.tensor_tensor(cat[:, kind, :], total[:], unit[:], ALU.subtract).then_inc(rounded, 1)

            for name in V_ORDER:
                values(name, 0, 0, job_number(name, 0, prologue=True))
            apply(0)
            for i in range(7):
                turned_parts(i, 0, 0, job_number(f"T{i}", 0, prologue=True))

            def step(g, n, b, first, last, last_group, first_group):
                job = lambda name: job_number(name, n, first, last)
                for u in range(UX):
                    if not last:
                        for name in [x for x in (SLOT_A.get(u), SLOT_B.get(u)) if x in V_ORDER]:
                            values(name, n + 1, 1 - b, job(name))
                    if u in (0, 4) and not first:
                        quantised(n - 1, 2 + u // 4)
                    if b == 1 and u == 0:
                        split_hi(3, 3 * g + 3 if not last_group else 3 * g + 1, job_done,
                                 jobs_before(n - 1) + jobs_of(False, False).index("Y3") + 1 if not first_group else 0)
                    if b == 0 and not last_group:
                        if u == 2:
                            split_hi(1, 3 * g + 1, job_done, job("A3") + 1)
                    for name in (SLOT_A.get(u), SLOT_B.get(u)):
                        if name and name[0] == "Y" and not first:
                            project_out(n - 1, int(name[1]), 1 - b, job(name))
                    if u == 7 and b == 0 and not last_group:
                        split_hi(2, 3 * g + 2, job_done, job("C3") + 1, (0, 1))
                    if u == 9 and not last:
                        apply(n + 1)
                    if u == 11:
                        quantised(n, 0, 0 if first else job("Y3") + 1)
                    for name in (SLOT_A.get(u), SLOT_B.get(u)):
                        if not last and name and name[0] == "T":
                            turned_parts(int(name[1]), n + 1, 1 - b, job(name))
                    if u == 12:
                        quantised(n, 1)
                    if b == 0 and u == 14 and not last_group:
                        split_hi(2, 0, None, 0, (2, 3))

            def body(g, first, last):
                step(g, 2 * g, 0, first, False, last, first)
                step(g, 2 * g + 1, 1, False, last, last, first)

            loop(body)(pool)
            quantised(STEPS - 1, 2)
            quantised(STEPS - 1, 3)
            r3 = job_number("R2", STEPS - 1, last=True) + 1
            for t in range(BT):
                project_out(STEPS - 1, t, 1, r3 + 1 + t)

        @block.scalar
        def _(act):
            def read_job(name, m, b, job, n=0, v_made=False, prologue=False):
                k, j = name[0], int(name[1])
                J = JOBS_FIRST[job % 2] if prologue else JOB
                act.wait_ge(job_done, job + 1)
                if k == "A":
                    for s, c in enumerate((SC_Q, SC_QX)):
                        r = slice(256 * s, 256 * (s + 1))
                        last = act.activation(qr[:, j, r], J[:, r], ACT.Copy, scale=cols[:, C_SCALAR + c:C_SCALAR + c + 1])
                elif k in "BC":
                    v = V_ORDER.index(name)
                    after(act, v_lo, len(V_ORDER) * m + v - 1)
                    if v == 0:
                        after(act, t_lo, 7 * m)
                    Jv = J.rearrange("p (t s c) -> p t s c", t=2, s=2)
                    if k == "B":
                        act.activation(qr[:, 2 * j:2 * j + 2, 4 * DH:5 * DH], Jv[:, :, 0, :], ACT.Copy,
                                       scale=cols[:, C_SCALAR + SC_K:C_SCALAR + SC_K + 1])
                        last = act.activation(vt[v % 2], Jv[:, :, 1, :], ACT.Copy,
                                              scale=cols[:, C_SCALAR + SC_V:C_SCALAR + SC_V + 1])
                    else:
                        act.activation(kr[:, 2 * j:2 * j + 2, :], Jv[:, :, 0, :], ACT.Copy, scale=1.0 / WS)
                        last = act.activation(vt[v % 2], Jv[:, :, 1, :], ACT.Copy, scale=1.0 / WS)
                elif k == "T":
                    c = (0, 0, 4, 4, 2, 6, 6)[j]
                    after(act, t_lo, 7 * m + j - 1 if j >= 2 else 7 * m)
                    if j == 0:
                        act.wait_ge(v_lo, len(V_ORDER) * (m + 1))
                        after(act, y_added, BT * (m - 1))
                    last = act.activation(ft[j % 2][:], J, ACT.Identity, scale=hcols[:, c:c + 1], bias=hcols[:, c + 1:c + 2])
                elif k == "Y":
                    after(act, y_added, BT * n + max(j - 1, 0))
                    if j == 0 and v_made:
                        act.wait_ge(v_lo, len(V_ORDER) * (m + 1))
                    last = act.activation(ft[j % 2][:], J, ACT.Copy, scale=psc[:])
                else:
                    after(act, o_read, KINDS * n + j)
                    last = act.activation(R[:], J, ACT.Copy)
                last.then_inc(job_read, 1)

            def exp(n, u):
                L = S if u < SELF_U else SX
                act.wait_ge(maxed, UX * n + u + 1)
                after(act, turned, PIECES * n + piece_end(u - 2))
                kind, qt = u // BT, u % BT
                act.activation(prob[u % 2][:, 0:L], SC[u % 2][:, 0:L], ACT.Exp,
                               bias=nm[:, u % 4:u % 4 + 1], accum_out=rs[:, kind % 2, qt:qt + 1]).then_inc(exped, 1)

            def parts_hi(n, u):
                pair, q = u // 2, P * (u % 2)
                for j in range(1 if u < SELF_U else 2):
                    piece = piece_end(u - 1) + j
                    act.wait_ge(turned, PIECES * n + piece + 1)
                    after(act, pved, PAIRS * n + pair - 1)
                    act.activation(pth[pair % 2][:, 4 * j:4 * j + 4, q:q + P],
                                   PT[piece % 2].rearrange("p (k c) -> p k c", k=4), ACT.Copy).then_inc(hi, 1)

            act.wait_ge(s_psc, 1)
            act.wait_ge(s_hcols, 3)
            for name in NEXT:
                read_job(name, 0, 0, job_number(name, 0, prologue=True), prologue=True)

            def step(g, n, b, first, last):
                for u in range(UX):
                    for slot in (SLOT_A, SLOT_B):
                        name = slot.get(u)
                        if name in jobs_of(first, last):
                            served = n - 1 if name in LATE else n
                            read_job(name, n + 1, 1 - b, job_number(name, n, first, last), served, not last)
                        if slot is SLOT_A and not (first and u < 2):
                            parts_hi(n if u >= 2 else n - 1, (u - 2) % UX)
                    exp(n, u)

            def body(g, first, last):
                step(g, 2 * g, 0, first, False)
                step(g, 2 * g + 1, 1, False, last)

            loop(body)(act)
            for u in (UX - 2, UX - 1):
                parts_hi(STEPS - 1, u)
            r3 = job_number("R2", STEPS - 1, last=True) + 1
            for i, name in enumerate(("R3", "Y0", "Y1", "Y2", "Y3")):
                read_job(name, 0, 0, r3 + i, STEPS - 1)

        @block.vector
        def _(dve):
            def split_lo(chunk, base, pieces):
                wh, wl = (w1h, w2h, w3h)[chunk - 1], (w1l, w2l, w3l)[chunk - 1]
                for i, (piece, k, c, scale) in enumerate(split_ops(chunk)):
                    if piece in pieces:
                        dve.wait_ge(w_hi, base + i + 1)
                        dve.scalar_tensor_tensor(out=wl[:, k, c], in0=wraw[:, k, c], scalar=scale, in1=wh[:, k, c],
                                                 op0=ALU.mult, op1=ALU.subtract).then_inc(w_lo, 1)

            wait = alone(dve, passed_dve)

            def block_stats(name, m, job):
                k, j = name[0], int(name[1])
                if k == "A":
                    blocks = [(c * BT + j, qr[:, j, DH * c:DH * (c + 1)]) for c in range(KINDS)]
                elif k == "B":
                    blocks = [(4 * BT + t, qr[:, t, 4 * DH:5 * DH]) for t in (2 * j, 2 * j + 1)]
                else:
                    blocks = [(5 * BT + t, kr[:, t, :]) for t in (2 * j, 2 * j + 1)]
                at = BLOCKS * m + sum(4 if x[0] == "A" else 2 for x in NEXT[:NEXT.index(name)])
                dve.wait_ge(job_read, job + 1)
                for i, a in blocks:
                    dve.bn_stats(stats[:, i, :], a).then_inc(s_stats, 1)
                for c, (i, a) in enumerate(blocks):
                    wait(s_stats, at + c + 1)
                    dve.bn_aggr(mv[:, i, :], stats[:, i, :]).then_inc(s_mv, 1)

            def deviations(m):
                dve.wait_ge(s_mv, BLOCKS * (m + 1))
                after(dve, applied_pool, len(POOL_APPLIES) * m)
                rsqrt(dve, s_rsqrt, RSQRT_STEPS * m, mv[:, :, 1], half[:], rstd[:], tmp[:])
                dve.scalar_tensor_tensor(out=shift[:], in0=mv[:, :, 0], scalar=-1.0, in1=rstd[:],
                                         op0=ALU.mult, op1=ALU.mult).then_inc(s_shift, 1)

            def apply(m, blocks):
                if 0 in blocks:
                    dve.wait_ge(s_shift, m + 1)
                for i in blocks:
                    a = norm_block(i)
                    dve.tensor_scalar(a, a, rstd[:, i:i + 1], shift[:, i:i + 1], ALU.mult, ALU.add).then_inc(applied, 1)

            def maxima(n, u):
                L, s = (S if u < SELF_U else SX), u % 4
                dve.wait_ge(scored, UX * n + u + 1)
                dve.tensor_reduce(nm[:, s:s + 1], SC[u % 2][:, 0:L], AX.X, ALU.max, negate=True).then_inc(maxed, 1)

            def parts_lo(n, u):
                pair, q = u // 2, P * (u % 2)
                for j in range(1 if u < SELF_U else 2):
                    piece = piece_end(u - 1) + j
                    dve.wait_ge(hi, PIECES * n + piece + 1)
                    dve.tensor_tensor(ptl[pair % 2][:, 4 * j:4 * j + 4, q:q + P],
                                      PT[piece % 2].rearrange("p (k c) -> p k c", k=4),
                                      pth[pair % 2][:, 4 * j:4 * j + 4, q:q + P], ALU.subtract).then_inc(lo, 1)

            def reciprocals(n, kind):
                dve.wait_ge(exped, UX * n + BT * (kind + 1))
                dve.reciprocal(ri[:, kind % 2, :], rs[:, kind % 2, :]).then_inc(recip, 1)

            def output(n, kind, r_job):
                count = KINDS * n + kind
                dve.wait_ge(job_read, r_job + 1)
                dve.wait_ge(pved, PAIRS * n + 2 * (kind + 1))
                after(dve, rounded, count)
                dve.scalar_tensor_tensor(out=y[:], in0=O, scalar=rsm[:, kind:kind + 1], in1=R[:], op0=ALU.mult,
                                         op1=ALU.mult).then_inc(o_read, 1)

            def output_round(n, kind):
                count = KINDS * n + kind
                dve.wait_ge(o_read, count + 1)
                round_fp8(dve, rounding, ROUND_STEPS * count, y[:], unit[:], total[:])

            dve.tensor_tensor(psc[:], cols[:, C_SCALAR + SC_PIN:C_SCALAR + SC_PIN + 1],
                              cols[:, C_SCALAR + SC_PW:C_SCALAR + SC_PW + 1], ALU.mult).then_inc(s_psc, 1)
            dve.wait_ge(s_psc, 1)
            dve.tensor_copy(hcols[:], cols[:, C_HEAD:C_HEAD + 8]).then_inc(s_hcols, 1)
            dve.wait_ge(s_hcols, 1)
            for c in (0, 4):
                dve.tensor_scalar(hcols[:, c:c + 2], cols[:, C_HEAD + c:C_HEAD + c + 2], SCALE_X, None,
                                  ALU.mult).then_inc(s_hcols, 1)
            for name in NEXT:
                if name[0] != "T":
                    block_stats(name, 0, job_number(name, 0, prologue=True))
            deviations(0)
            apply(0, range(0, 4 * BT))

            STATS_AT = {1: ("A0", "A1"), 2: ("A2", "A3"), 3: ("B0",), 4: ("C0", "C1"), 5: ("B1", "C2"), 6: ("C3",)}

            def step(g, n, b, first, last, last_group):
                job = lambda name: job_number(name, n, first, last)
                for u in range(UX):
                    if u in (0, 4) and not first:
                        output(n - 1, 2 + u // 4, job("R3") if u else jobs_before(n) - 1)
                    if u in (8, 12):
                        output(n, u // 4 - 2, job(f"R{u // 4 - 2}"))
                    maxima(n, u)
                    if u % 4 == 1 and not (first and u == 1):
                        reciprocals(n if u > 1 else n - 1, (u // 4 - 1) % KINDS)
                    if not (first and u < 2):
                        parts_lo(n if u >= 2 else n - 1, (u - 2) % UX)
                    if not last:
                        for name in STATS_AT.get(u, ()):
                            block_stats(name, n + 1, job(name))
                        if u == 6:
                            deviations(n + 1)
                        if u in APPLY_AT:
                            apply(n + 1, APPLY_AT[u])
                    if u in (0, 4) and not first:
                        output_round(n - 1, 2 + u // 4)
                    if u == 4 and b == 0:
                        after(dve, o_read, KINDS * n)
                        dve.tensor_copy(rsm[:], rcols[:, bass.ds(C_SMOOTH + KINDS * g, KINDS)]).then_inc(s_rsm, 1)
                        dve.wait_ge(s_rsm, g + 1)
                    if u in (8, 12):
                        output_round(n, u // 4 - 2)
                    if b == 0 and not last_group:
                        if u in (3, 4, 5):
                            split_lo(1, w_base(g), (0, 1, 2, 3)[u - 3:u - 2] if u < 5 else (2, 3))
                        if u in (9, 10, 14, 15):
                            split_lo(2, w_base(g) + W1N, ((9, 10, 14, 15).index(u),))
                    if b == 1 and u in (1, 2):
                        split_lo(3, w_base(g) + (0 if last_group else W1N + W2N), (2 * u - 2, 2 * u - 1))

            def body(g, first, last):
                step(g, 2 * g, 0, first, False, last)
                step(g, 2 * g + 1, 1, False, last, last)

            loop(body)(dve)
            output(STEPS - 1, 2, job_number("R2", STEPS - 1, last=True))
            output_round(STEPS - 1, 2)
            for u in (UX - 2, UX - 1):
                parts_lo(STEPS - 1, u)
            reciprocals(STEPS - 1, 3)
            r3 = job_number("R2", STEPS - 1, last=True) + 1
            output(STEPS - 1, 3, r3)
            output_round(STEPS - 1, 3)
            norm_stats(dve, rows3, X, lambda t: dve.wait_ge(y_added, BT * (STEPS - 1) + max(0, t - BT + 1)))

        @block.tensor
        def _(pe):
            def run_job(name, m, b, job, prologue=False):
                k, j = name[0], int(name[1])
                J = JOBS_FIRST[job % 2] if prologue else JOB
                after(pe, job_read, job - 1 if prologue else job)
                if k == "A":
                    tok = slice(S * b + P * j, S * b + P * (j + 1))
                    for s in range(2):
                        c = slice(256 * s, 256 * (s + 1))
                        for kt in range(KT):
                            pe.matmul(J[:, c], xq[:, s, kt, tok], w1h[:, kt, c], start=(kt == 0), stop=False)
                            last = pe.matmul(J[:, c], xq[:, s, kt, tok], w1l[:, kt, c], start=False, stop=(kt == KT - 1))
                elif k == "B":
                    for i in range(2):
                        tok = slice(S * b + P * (2 * j + i), S * b + P * (2 * j + i + 1))
                        for s in range(2):
                            o = J[:, 256 * i + DH * s:256 * i + DH * (s + 1)]
                            c = slice(DH * s, DH * (s + 1))
                            for kt in range(KT):
                                pe.matmul(o, xq[:, 2 + s, kt, tok], w2h[:, kt, c], start=(kt == 0), stop=False)
                                last = pe.matmul(o, xq[:, 2 + s, kt, tok], w2l[:, kt, c], start=False,
                                                 stop=(kt == KT - 1))
                elif k == "C":
                    for i in range(2):
                        tok = slice(SX * b + P * (2 * j + i), SX * b + P * (2 * j + i + 1))
                        for kt in range(KT):
                            last = three(pe, J[:, 256 * i:256 * (i + 1)], cxh[:, kt, tok], cxl[:, kt, tok],
                                         w2h[:, kt, 2 * DH:4 * DH], w2l[:, kt, 2 * DH:4 * DH], kt == 0, kt == KT - 1)
                elif k == "T":
                    if j < 4:
                        pe.wait_ge(applied, 4 * BT * m + BT * (j + 1))
                    else:
                        pe.wait_ge(applied_pool, len(POOL_APPLIES) * m + BT * (j - 3))
                    for t in range(BT):
                        src = qr[:, t, DH * j:DH * (j + 1)] if j < 5 else kr[:, BT * (j - 5) + t, :]
                        last = pe.transpose(J[:, P * t:P * (t + 1)], src, ident[:])
                elif k == "R":
                    pe.wait_ge(recip, KINDS * m + j + 1)
                    for t in range(BT):
                        last = pe.transpose(J[:, P * t:P * (t + 1)], ri[:, j % 2, t:t + 1].broadcast_to([P, P]), ident[:])
                else:
                    pe.wait_ge(rounded, KINDS * (m + 1))
                    for kind in range(KINDS):
                        c = cat[:, kind, P * j:P * (j + 1)]
                        pe.matmul(J, c, w3h[:, kind, :], start=(kind == 0), stop=False)
                        last = pe.matmul(J, c, w3l[:, kind, :], start=False, stop=(kind == KINDS - 1))
                last.then_inc(job_done, 1)

            def scores(n, u, b):
                kind, qt = u // BT, u % BT
                after(pe, exped, UX * n + u - 1)
                q = slice(P * qt, P * (qt + 1))
                a, c = (kh[b], kl[b]) if u < SELF_U else (kxh[b], kxl[b])
                for j in range(1 if u < SELF_U else 2):
                    r = slice(S * j, S * (j + 1))
                    last = three(pe, SC[u % 2][:, r], qh[b][:, kind, q], ql[b][:, kind, q], a[:, r], c[:, r], True, True)
                last.then_inc(scored, 1)

            def turn(n, u):
                pe.wait_ge(exped, UX * n + u + 1)
                for j in range(1 if u < SELF_U else 2):
                    piece = piece_end(u - 1) + j
                    after(pe, lo, PIECES * n + piece - 1)
                    for k in range(4):
                        last = pe.transpose(PT[piece % 2][:, P * k:P * (k + 1)],
                                            prob[u % 2][:, P * (4 * j + k):P * (4 * j + k + 1)], ident[:])
                    last.then_inc(turned, 1)

            def product(n, u, b, halves=(0, 1)):
                pair = u // 2
                if 0 in halves:
                    if pair == 0:
                        pe.wait_ge(v_lo, len(V_ORDER) * (n + 1))
                    if pair % 2 == 0:
                        after(pe, o_read, KINDS * n + pair // 2)
                    pe.wait_ge(lo, PIECES * n + piece_end(u))
                h, l, tiles = (vh[b], vl[b], BT) if u < SELF_U else (vxh[b], vxl[b], XT)
                c = slice(2 * P * (pair % 2), 2 * P * (pair % 2 + 1))
                for k in range(tiles):
                    if k // (tiles // 2) in halves:
                        last = three(pe, O[:, c], h[:, k, :], l[:, k, :], pth[pair % 2][:, k, :],
                                     ptl[pair % 2][:, k, :], k == 0, k == tiles - 1)
                if 1 in halves:
                    last.then_inc(pved, 1)

            for name in NEXT:
                run_job(name, 0, 0, job_number(name, 0, prologue=True), prologue=True)

            def step(g, n, b, first, last):
                for u in range(UX):
                    if u == 0:
                        pe.wait_ge(t_lo, 7 * n + 5)
                    if u == SELF_U:
                        pe.wait_ge(t_lo, 7 * (n + 1))
                    scores(n, u, b)
                    for slot in (SLOT_A, SLOT_B):
                        name = slot.get(u)
                        if name in jobs_of(first, last):
                            if name[0] in "ABCT":
                                served, sb_ = n + 1, 1 - b
                            else:
                                served = n - 1 if name in LATE else n
                                sb_ = None
                            if b == 1 and name == "A0":
                                pe.wait_ge(w_lo, w_base(g) + W1N)
                            if b == 1 and name == "B0":
                                pe.wait_ge(w_lo, w_base(g) + W1N + W2N)
                            if b == 1 and name == "Y0":
                                pe.wait_ge(w_lo, w_base(g) + (W3N if last else WN))
                            run_job(name, served, sb_, job_number(name, n, first, last))
                        if slot is SLOT_A and not (first and u < 2):
                            turn(n if u >= 2 else n - 1, (u - 2) % UX)
                        if slot is SLOT_A and not (first and u < 4):
                            product(n if u >= 4 else n - 1, (u - 3 - u % 2) % UX, b if u >= 4 else 1 - b, (u % 2,))

            def body(g, first, last):
                step(g, 2 * g, 0, first, False)
                step(g, 2 * g + 1, 1, False, last)

            loop(body)(pe)
            turn(STEPS - 1, UX - 2)
            product(STEPS - 1, UX - 3, 1)
            turn(STEPS - 1, UX - 1)
            product(STEPS - 1, UX - 1, 1)
            r3 = job_number("R2", STEPS - 1, last=True) + 1
            run_job("R3", STEPS - 1, None, r3)
            for t in range(BT):
                run_job(f"Y{t}", STEPS - 1, None, r3 + 1 + t)


E = 8
FF = 1024
FT = FF // P
TOP_P = 0.9


def experts(nc, ins, sem, sb, bank, X, ident, out_d, rows3):
    n = norm_tiles(sem, sb, "n3", rows3)
    XTh, XTl = sb("eXTh", [P, KT, T], F16), sb("eXTl", [P, KT, T], F16)
    raw = [sb(f"raw_{x}", s, F32) for x, s in (("gate", [P, KT, FF]), ("up", [P, KT, FF]), ("down", [P, FT, D]))]
    wh = [sb(f"ewh_{x}", s, F16) for x, s in (("gate", [P, KT, FF]), ("up", [P, KT, FF]), ("down", [P, FT, D]))]
    wl = [sb(f"ewl_{x}", s, F16) for x, s in (("gate", [P, KT, FF]), ("up", [P, KT, FF]), ("down", [P, FT, D]))]
    sil = [sb(f"sil{i}", [P, S], F32) for i in range(2)]
    h = [sb(f"h{i}", [P, S], F32) for i in range(2)]
    hh = [sb(f"hh{i}", [P, FT, S], F16) for i in range(B)]
    hl = [sb(f"hl{i}", [P, FT, S], F16) for i in range(B)]
    rw, rwh, rwl = sb("rw", [P, KT, E], F32), sb("rwh", [P, KT, E], F16), sb("rwl", [P, KT, E], F16)
    logits, prob, before = (sb(x, [P, NT, E], F32) for x in ("logits", "eprob", "ebefore"))
    larger = sb("larger", [P, E, NT, E], F32)
    weight = sb("weight", [P, E, NT], F32)
    wcol = sb("wcol", [P, NT], F32)
    m8, s8, r8 = (sb(x, [P, NT], F32) for x in ("m8", "s8", "r8"))

    passed_sp, passed_pool = sem("e_passed_sp"), sem("e_passed_pool")
    raw_in = [sem(f"e_raw_in{i}") for i in range(3)]
    w_hi, w_lo = [sem(f"e_w_hi{i}") for i in range(3)], [sem(f"e_w_lo{i}") for i in range(3)]
    rw_in, rw_hi, rw_lo, routed, l_read, route, l_exp = (
        sem(f"e_{x}") for x in ("rw_in", "rw_hi", "rw_lo", "routed", "l_read", "route", "l_exp"))
    gated, upped, silu, made, h_hi, h_lo = (sem(f"e_{x}") for x in ("gated", "upped", "silu", "made", "h_hi", "h_lo"))
    down, added, s_wcol, stored = (sem(f"e_{x}") for x in ("down", "added", "wcol", "stored"))
    HT = B * FT
    PW = KT

    def piece(w, i, k):
        return w[i][:, k, :] if i < 2 else w[i][:, 2 * k:2 * k + 2, :]

    def loop(eng, body):
        body(0)
        with eng.Fori(1, E) as e:
            body(e)

    with nc.Block() as block:
        @block.sync
        def _(sp):
            wait = alone(sp, passed_sp)
            sp.dma_start(rw[:], ins["router"]).then_inc(rw_in, 16)

            def body(e):
                for i in range(3):
                    wait(w_lo[i], PW * e)
                    sp.dma_start(raw[i][:], ins[("gate", "up", "down")[i]][bass.ds(e, 1)]
                                 .rearrange("a p k n -> p (a k) n")).then_inc(raw_in[i], 16)

            loop(sp, body)
            for t in range(NT):
                wait(added, NT * (E - 1) + t + 1)
                sp.dma_start(out_d[t], X[:, t, :]).then_inc(stored, 16)
            wait(stored, 16 * NT)

        @block.gpsimd
        def _(pool):
            wait = alone(pool, passed_pool)
            for i in range(2):
                wait(raw_in[i], 16)
                for k in range(PW):
                    pool.tensor_scalar(piece(wh, i, k), piece(raw, i, k), WS, 1.0, ALU.mult, ALU.mult)\
                        .then_inc(w_hi[i], 1)

            def body(e):
                for i in range(HT):
                    half, f = i // FT, i % FT
                    wait(made, HT * e + i + 1)
                    if f == 0:
                        wait(down, NT * (e - 1) + BT * (half + 1))
                    pool.tensor_scalar(hh[half][:, f, :], h[i % 2][:], 1.0, 1.0, ALU.mult, ALU.mult).then_inc(h_hi, 1)
                    wait(h_hi, HT * e + i + 1)
                    pool.tensor_tensor(hl[half][:, f, :], h[i % 2][:], hh[half][:, f, :], ALU.subtract).then_inc(h_lo, 1)

            loop(pool, body)

        @block.scalar
        def _(act):
            def split_hi(e, i, k):
                act.wait_ge(raw_in[i], 16 * (e + 1))
                if k == 0:
                    after(act, upped if i < 2 else down, HT * e if i < 2 else NT * e)
                act.activation(piece(wh, i, k), piece(raw, i, k), ACT.Copy, scale=WS).then_inc(w_hi[i], 1)

            norm_scalar(act, n, X, XTh, bank)
            act.wait_ge(rw_in, 16)
            act.activation(rwh[:], rw[:], ACT.Copy, scale=WS).then_inc(rw_hi, 1)
            act.wait_ge(routed, 1)
            act.activation(logits[:], bank[:, 4, 0:NT * E].rearrange("p (t e) -> p t e", t=NT), ACT.Copy, scale=1.0 / WS)\
                .then_inc(l_read, 1)
            act.wait_ge(route, 2)
            act.activation(prob[:], logits[:], ACT.Exp).then_inc(l_exp, 1)

            def body(e):
                for i in range(HT):
                    act.wait_ge(gated, HT * e + i + 1)
                    after(act, made, HT * e + i - 1)
                    act.activation(sil[i % 2][:], bank[:, 2 * (i % 2), :], ACT.Silu, scale=1.0 / WS).then_inc(silu, 1)
                    if 1 <= i <= PW:
                        split_hi(e, 2, i - 1)

            def next_weights(e):
                for i in range(2):
                    for k in range(PW):
                        split_hi(e, i, k)

            body(0)
            with act.Fori(1, E) as e:
                next_weights(e)
                body(e)

        @block.vector
        def _(dve):
            def split_lo(e, i, k):
                dve.wait_ge(w_hi[i], PW * e + k + 1)
                dve.scalar_tensor_tensor(out=piece(wl, i, k), in0=piece(raw, i, k), scalar=WS, in1=piece(wh, i, k),
                                         op0=ALU.mult, op1=ALU.subtract).then_inc(w_lo[i], 1)

            norm_lo(dve, n, XTh, XTl, bank)
            dve.wait_ge(rw_hi, 1)
            dve.scalar_tensor_tensor(out=rwl[:], in0=rw[:], scalar=WS, in1=rwh[:], op0=ALU.mult, op1=ALU.subtract)\
                .then_inc(rw_lo, 1)
            for i in range(2):
                for k in range(PW):
                    split_lo(0, i, k)

            steps = 0

            def step(ins_):
                nonlocal steps
                ins_.then_inc(route, 1)
                steps += 1
                dve.wait_ge(route, steps)

            def wide(a):
                return a.unsqueeze(2).broadcast_to([P, NT, E])

            dve.wait_ge(l_read, 1)
            step(dve.tensor_reduce(m8[:], logits[:], AX.X, ALU.max))
            step(dve.tensor_tensor(logits[:], logits[:], wide(m8[:]), ALU.subtract))
            dve.wait_ge(l_exp, 1)
            step(dve.tensor_reduce(s8[:], prob[:], AX.X, ALU.add))
            step(dve.reciprocal(r8[:], s8[:]))
            step(dve.tensor_tensor(prob[:], prob[:], wide(r8[:]), ALU.mult))
            for e in range(E):
                mine = prob[:, :, e]
                if e:
                    dve.tensor_tensor(larger[:, e, :, 0:e], prob[:, :, 0:e],
                                      mine.unsqueeze(2).broadcast_to([P, NT, e]), ALU.is_ge).then_inc(route, 1)
                    steps += 1
                step(dve.tensor_tensor(larger[:, e, :, e:E], prob[:, :, e:E],
                                       mine.unsqueeze(2).broadcast_to([P, NT, E - e]), ALU.is_gt))
            step(dve.tensor_tensor(larger[:], larger[:], prob[:].unsqueeze(1).broadcast_to([P, E, NT, E]), ALU.mult))
            step(dve.tensor_reduce(before[:].rearrange("p t e -> p (t e)").rearrange("p (e t) -> p e t", e=E),
                                   larger[:], AX.X, ALU.add))
            kept = before[:].rearrange("p t e -> p (t e)").rearrange("p (e t) -> p e t", e=E)
            step(dve.tensor_scalar(kept, kept, TOP_P, 1.0 / WS ** 2, ALU.is_le, ALU.mult))
            step(dve.tensor_tensor(weight[:], kept, prob[:].rearrange("p t e -> p e t"), ALU.mult))

            def body(e):
                for i in range(HT):
                    dve.wait_ge(silu, HT * e + i + 1)
                    dve.wait_ge(upped, HT * e + i + 1)
                    after(dve, h_lo, HT * e + i - 1)
                    dve.tensor_tensor(h[i % 2][:], bank[:, 2 * (i % 2) + 1, :], sil[i % 2][:], ALU.mult).then_inc(made, 1)
                    if 2 <= i < 2 + PW:
                        split_lo(e, 2, i - 2)
                after(dve, added, NT * e)
                dve.tensor_copy(wcol[:], weight[:].rearrange("p e t -> p (e t)")[:, bass.ds(NT * e, NT)])\
                    .then_inc(s_wcol, 1)
                dve.wait_ge(s_wcol, e + 1)

            def add(e, t):
                dve.wait_ge(down, NT * e + t + 1)
                dve.scalar_tensor_tensor(out=X[:, t, :], in0=bank[:, 4 + t % 4, :], scalar=wcol[:, t:t + 1],
                                         in1=X[:, t, :], op0=ALU.mult, op1=ALU.add).then_inc(added, 1)

            body(0)
            with dve.Fori(1, E) as e:
                for i in range(2):
                    for k in range(PW):
                        split_lo(e, i, k)
                        add(e - 1, PW * i + k)
                body(e)
            for t in range(NT):
                add(E - 1, t)

        @block.tensor
        def _(pe):
            norm_tensor(pe, n, bank, ident)
            pe.wait_ge(rw_lo, 1)
            pe.wait_ge(n.s_lo, NT)
            for t in range(NT):
                for k in range(KT):
                    tok = slice(P * t, P * (t + 1))
                    last = three(pe, bank[:, 4, E * t:E * (t + 1)], XTh[:, k, tok], XTl[:, k, tok], rwh[:, k, :],
                                 rwl[:, k, :], k == 0, k == KT - 1)
            last.then_inc(routed, 1)

            def body(e):
                for i in range(HT):
                    half, f = i // FT, i % FT
                    after(pe, made, HT * e + i - 1)
                    for w, done in ((0, gated), (1, upped)):
                        if i == 0:
                            pe.wait_ge(w_lo[w], PW * (e + 1))
                        for k in range(KT):
                            c = slice(P * f, P * (f + 1))
                            tok = slice(S * half, S * (half + 1))
                            last = three(pe, bank[:, 2 * (i % 2) + w, :], wh[w][:, k, c], wl[w][:, k, c],
                                         XTh[:, k, tok], XTl[:, k, tok], k == 0, k == KT - 1)
                        last.then_inc(done, 1)
                pe.wait_ge(w_lo[2], PW * (e + 1))
                for t in range(NT):
                    half = t // BT
                    if t % BT == 0:
                        pe.wait_ge(h_lo, HT * e + FT * (half + 1))
                    after(pe, added, NT * e + t - 3)
                    if isinstance(e, int) and e == 0 and t == 0:
                        pe.wait_ge(l_read, 1)
                    tok = slice(P * (t % BT), P * (t % BT + 1))
                    for f in range(FT):
                        last = three(pe, bank[:, 4 + t % 4, :], hh[half][:, f, tok], hl[half][:, f, tok],
                                     wh[2][:, f, :], wl[2][:, f, :], f == 0, f == FT - 1)
                    last.then_inc(down, 1)

            loop(pe, body)


def pack(x):
    c = np.ascontiguousarray
    rows = lambda w: w.reshape(-1, P, w.shape[-1]).transpose(1, 0, 2)
    wq, wk, wv = np.split(x["L0_attn_w_qkv"].T, 3, axis=1)
    bq, bk, bv = np.split(x["L0_attn_b_qkv"], 3)
    quad = lambda w: w.reshape(D, QUADS, P)
    per_part = lambda v: v.reshape(-1, P).T
    a = {
        "x": x["x"].reshape(T, D),
        "cols": cols(x),
        "w_qkv": np.stack([rows(np.concatenate([quad(w)[:, i] for w in (wq, wk, wv)], axis=1)) for i in range(QUADS)]),
        "b_qk": np.stack([np.stack([bq[P * i:P * (i + 1)], bk[P * i:P * (i + 1)]], axis=1) for i in range(QUADS)]),
        "b_v": np.stack([np.broadcast_to(bv[P * i:P * (i + 1)], (P, P)) for i in range(QUADS)]),
        "w_out": x["L0_attn_w_out"].T.reshape(QUADS, P, D),
        "bout": np.broadcast_to(x["L0_attn_b_out"], (P, D)),
    }
    xa = lambda name: x["L0_xattn_" + name]
    heads = lambda w: w.T.reshape(D, GROUPS, -1)
    wkx, wvx = np.split(xa("w_kv_x"), 2)
    wp = xa("wproj").T.reshape(2, GROUPS, HPG * DH, D)
    one = [np.concatenate([heads(xa(n)) for n in ("wq", "wqx")], axis=2),
           np.concatenate([heads(w) for w in (xa("wk"), xa("wv"), wkx, wvx)], axis=2)]
    a["w_group"] = np.stack([np.stack([rows(one[0][:, g]), rows(one[1][:, g]),
                                       rows(wp[:, g].reshape(KINDS * DH, D))]) for g in range(GROUPS)])
    for name in ("gate", "up", "down"):
        a[name] = np.stack([rows(w.T) for w in x["L0_ffn_" + name + "_w"]])
    a["router"] = rows(x["L0_ffn_router_w"].T)
    a["ctx"] = x["ctx_2048"].transpose(2, 0, 1).reshape(KT, P, B * SX)
    return {k: c(v) for k, v in a.items()}


def cols(x):
    xa = lambda name: x["L0_xattn_" + name]
    per_part = lambda v: v.reshape(-1, P).T
    smooth = xa("proj_smooth").reshape(2, GROUPS, HPG, P).transpose(3, 1, 0, 2).reshape(P, GROUPS * KINDS)
    return np.concatenate(
        [per_part(xa("ln_w")), per_part(xa("ln_b"))]
        + [per_part(xa(n + "_in_scale")) for n in ("q", "qx", "k", "v")]
        + [per_part(xa(n)) for h in ("qln", "kln", "qxln", "kxln") for n in (h + "_w", h + "_b")]
        + [smooth]
        + [np.broadcast_to(xa(n).reshape(1, 1), (P, 1))
           for n in ("wq_scale", "wqx_scale", "wk_scale", "wv_scale", "proj_in_scale", "proj_w_scale")], axis=1)


def kernel(**inputs):
    import concourse.bacc as bacc
    from concourse.bass_utils import run_bass_kernel_spmd

    nc = bacc.Bacc("TRN2", target_bir_lowering=False, num_devices=1)
    arrays, args = {}, {}
    for name, a in pack({k: np.asarray(v) for k, v in inputs.items()}).items():
        arrays[f"in_{name}"] = a
        args[name] = nc.dram_tensor(f"in_{name}", a.shape, mybir.dt.from_np(a.dtype), kind="ExternalInput").ap()
    out = nc.dram_tensor("out", (B, S, D), F32, kind="ExternalOutput").ap()
    build(nc, args, out)
    r = run_bass_kernel_spmd(nc, [arrays], core_ids=[0])
    return r.results[0]["out"]
```
